# Optimizing a Trainium2 kernel written in Bass

```python
import numpy as np
import jax
import jax.numpy as jnp

def _softmax(x, axis=-1):
    return jax.nn.softmax(x, axis=axis)

def _gelu(x):
    return jax.nn.gelu(x, approximate=True)

def _silu(x):
    return jax.nn.silu(x)

def _sigmoid(x):
    return jax.nn.sigmoid(x)

def _layernorm(x, axis=-1, eps=1e-05):
    m = jnp.mean(x, axis=axis, keepdims=True)
    v = jnp.var(x, axis=axis, keepdims=True)
    return (x - m) / jnp.sqrt(v + eps)

def _scatter_add(tgt, idx, src, axis=0):
    return tgt.at[idx].add(src)

def _segment_sum(src, seg, n):
    return jax.ops.segment_sum(src, seg, n)
kernel_name = 'mk_gps_d1_gnn_r8_d74edc'

def setup_inputs(seed: int=0):
    np.random.seed(seed)
    _w = jnp.asarray

    def _rec_inputs():
        import jax
        import jax.numpy as jnp
        _gk = jax.random.key(seed)
        x = -0.0003713 + 1 * jax.random.normal(jax.random.fold_in(_gk, 1), (6250, 256), jnp.float32)
        src = jax.random.randint(jax.random.fold_in(_gk, 2), (100000,), 0, 6250, jnp.int32)
        dst = jax.random.randint(jax.random.fold_in(_gk, 3), (100000,), 0, 6250, jnp.int32)
        _o = jnp.argsort(dst, stable=True)
        src = src[_o]
        dst = dst[_o]
        return (x, src, dst)
    x, src, dst = _rec_inputs()

    def _L0_gnn_setup():
        import jax, jax.numpy as jnp
        import numpy as np
        N = 6250
        E = 200000
        F_IN = 256
        F_OUT = 256
        ALPHA = 0.2
        key = jax.random.key(seed)
        ks = jax.random.split(key, 7)
        x = jax.random.normal(ks[0], (N, F_IN), dtype=jnp.float32)
        row = jax.random.randint(ks[1], (E,), 0, N, dtype=jnp.int32)
        col = jax.random.randint(ks[2], (E,), 0, N, dtype=jnp.int32)
        W_w = jax.random.normal(ks[3], (F_IN, F_OUT), dtype=jnp.float32) / np.sqrt(F_IN).astype(np.float32)
        W_b = jax.random.normal(ks[4], (F_OUT,), dtype=jnp.float32) * 0.01
        a_w = jax.random.normal(ks[5], (2 * F_OUT,), dtype=jnp.float32) / np.sqrt(2 * F_OUT).astype(np.float32)
        a_b = jax.random.normal(ks[6], (1,), dtype=jnp.float32) * 0.01
        return {'x': x, 'W_w': W_w, 'W_b': W_b, 'a_w': a_w, 'a_b': a_b, 'row': row, 'col': col}
    _L0_gnn_all = _L0_gnn_setup()
    _L0_gnn_in = {k: v for k, v in _L0_gnn_all.items() if k in ('W_w', 'W_b', 'a_w', 'a_b')}
    del _L0_gnn_all

    def _L0_mix_setup():
        import jax, jax.numpy as jnp
        import numpy as np
        D_MODEL = 256
        NHEAD = 8
        D_HEAD = D_MODEL // NHEAD
        DIM_FF = 1024
        B, L = (4, 2048)
        LN_EPS = 1e-05

        def _layernorm(x, g, b):
            mu = jnp.mean(x, axis=-1, keepdims=True)
            var = jnp.mean((x - mu) ** 2, axis=-1, keepdims=True)
            return (x - mu) * jax.lax.rsqrt(var + LN_EPS) * g + b

        def _phi(x):
            return jnp.where(x > 0, x + 1.0, jnp.exp(x))
        key = jax.random.key(seed)
        ks = jax.random.split(key, 16)
        s_in = 1.0 / np.sqrt(D_MODEL)
        s_ff = 1.0 / np.sqrt(DIM_FF)
        inp = {'x': jax.random.normal(ks[0], (B, L, D_MODEL), dtype=jnp.float32), 'Wq': jax.random.normal(ks[1], (D_MODEL, D_MODEL), dtype=jnp.float32) * s_in, 'bq': jnp.zeros((D_MODEL,), jnp.float32), 'Wk': jax.random.normal(ks[2], (D_MODEL, D_MODEL), dtype=jnp.float32) * s_in, 'bk': jnp.zeros((D_MODEL,), jnp.float32), 'Wv': jax.random.normal(ks[3], (D_MODEL, D_MODEL), dtype=jnp.float32) * s_in, 'bv': jnp.zeros((D_MODEL,), jnp.float32), 'Wo': jax.random.normal(ks[4], (D_MODEL, D_MODEL), dtype=jnp.float32) * s_in, 'bo': jnp.zeros((D_MODEL,), jnp.float32), 'W1': jax.random.normal(ks[5], (D_MODEL, DIM_FF), dtype=jnp.float32) * s_in, 'b1': jnp.zeros((DIM_FF,), jnp.float32), 'W2': jax.random.normal(ks[6], (DIM_FF, D_MODEL), dtype=jnp.float32) * s_ff, 'b2': jnp.zeros((D_MODEL,), jnp.float32), 'ln1_g': jnp.ones((D_MODEL,), jnp.float32), 'ln1_b': jnp.zeros((D_MODEL,), jnp.float32), 'ln2_g': jnp.ones((D_MODEL,), jnp.float32), 'ln2_b': jnp.zeros((D_MODEL,), jnp.float32)}
        return inp
    _L0_mix_all = _L0_mix_setup()
    _L0_mix_in = {k: v for k, v in _L0_mix_all.items() if k in ('Wq', 'bq', 'Wk', 'bk', 'Wv', 'bv', 'Wo', 'bo', 'W1', 'b1', 'W2', 'b2', 'ln1_g', 'ln1_b', 'ln2_g', 'ln2_b')}
    del _L0_mix_all

    def _L0_ffn_setup():
        import jax, jax.numpy as jnp
        import numpy as np
        E, D, H, TOP_K = (6, 256, 256, 2)
        ROUTER_H = D // 2
        key = jax.random.key(seed)
        ks = jax.random.split(key, 12)
        s = 1.0 / np.sqrt(D)
        sh = 1.0 / np.sqrt(H)
        sr = 1.0 / np.sqrt(ROUTER_H)
        return {'features': jax.random.normal(ks[0], (8, 512, D), dtype=jnp.float32), 'router_w1': jax.random.uniform(ks[1], (D, ROUTER_H), jnp.float32, -s, s), 'router_b1': jnp.zeros((ROUTER_H,), jnp.float32), 'router_w2': jax.random.uniform(ks[2], (ROUTER_H, E), jnp.float32, -sr, sr), 'router_b2': jnp.zeros((E,), jnp.float32), 'expert_w1': jax.random.uniform(ks[3], (E, D, H), jnp.float32, -s, s), 'expert_b1': jnp.zeros((E, H), jnp.float32), 'expert_w2': jax.random.uniform(ks[4], (E, H, H), jnp.float32, -sh, sh), 'expert_b2': jnp.zeros((E, H), jnp.float32), 'expert_w3': jax.random.uniform(ks[5], (E, H, D), jnp.float32, -sh, sh), 'expert_b3': jnp.zeros((E, D), jnp.float32)}
    _L0_ffn_all = _L0_ffn_setup()
    _L0_ffn_in = {k: v for k, v in _L0_ffn_all.items() if k in ('router_w1', 'router_b1', 'router_w2', 'router_b2', 'expert_w1', 'expert_b1', 'expert_w2', 'expert_b2', 'expert_w3', 'expert_b3')}
    del _L0_ffn_all
    return {'x': x, 'src': src, 'dst': dst, 'L0_gnn_W_w': _L0_gnn_in['W_w'], 'L0_gnn_W_b': _L0_gnn_in['W_b'], 'L0_gnn_a_w': _L0_gnn_in['a_w'], 'L0_gnn_a_b': _L0_gnn_in['a_b'], 'L0_mix_Wq': _L0_mix_in['Wq'], 'L0_mix_bq': _L0_mix_in['bq'], 'L0_mix_Wk': _L0_mix_in['Wk'], 'L0_mix_bk': _L0_mix_in['bk'], 'L0_mix_Wv': _L0_mix_in['Wv'], 'L0_mix_bv': _L0_mix_in['bv'], 'L0_mix_Wo': _L0_mix_in['Wo'], 'L0_mix_bo': _L0_mix_in['bo'], 'L0_mix_W1': _L0_mix_in['W1'], 'L0_mix_b1': _L0_mix_in['b1'], 'L0_mix_W2': _L0_mix_in['W2'], 'L0_mix_b2': _L0_mix_in['b2'], 'L0_mix_ln1_g': _L0_mix_in['ln1_g'], 'L0_mix_ln1_b': _L0_mix_in['ln1_b'], 'L0_mix_ln2_g': _L0_mix_in['ln2_g'], 'L0_mix_ln2_b': _L0_mix_in['ln2_b'], 'L0_ffn_router_w1': _L0_ffn_in['router_w1'], 'L0_ffn_router_b1': _L0_ffn_in['router_b1'], 'L0_ffn_router_w2': _L0_ffn_in['router_w2'], 'L0_ffn_router_b2': _L0_ffn_in['router_b2'], 'L0_ffn_expert_w1': _L0_ffn_in['expert_w1'], 'L0_ffn_expert_b1': _L0_ffn_in['expert_b1'], 'L0_ffn_expert_w2': _L0_ffn_in['expert_w2'], 'L0_ffn_expert_b2': _L0_ffn_in['expert_b2'], 'L0_ffn_expert_w3': _L0_ffn_in['expert_w3'], 'L0_ffn_expert_b3': _L0_ffn_in['expert_b3']}

def reference(x, src, dst, L0_gnn_W_w, L0_gnn_W_b, L0_gnn_a_w, L0_gnn_a_b, L0_mix_Wq, L0_mix_bq, L0_mix_Wk, L0_mix_bk, L0_mix_Wv, L0_mix_bv, L0_mix_Wo, L0_mix_bo, L0_mix_W1, L0_mix_b1, L0_mix_W2, L0_mix_b2, L0_mix_ln1_g, L0_mix_ln1_b, L0_mix_ln2_g, L0_mix_ln2_b, L0_ffn_router_w1, L0_ffn_router_b1, L0_ffn_router_w2, L0_ffn_router_b2, L0_ffn_expert_w1, L0_ffn_expert_b1, L0_ffn_expert_w2, L0_ffn_expert_b2, L0_ffn_expert_w3, L0_ffn_expert_b3):
    import jax
    import jax.numpy as jnp

    def _L0_gnn_ref(x, W_w, W_b, a_w, a_b, row, col):
        import jax, jax.numpy as jnp
        import numpy as np
        N = 6250
        E = 200000
        F_IN = 256
        F_OUT = 256
        ALPHA = 0.2
        Wh = x @ W_w + W_b
        f_dst_part = Wh @ a_w[:F_OUT]
        f_row_part = Wh @ a_w[F_OUT:]
        e = f_dst_part[col] + f_row_part[row] + a_b[0]
        e = jnp.where(e > 0, e, ALPHA * e)
        m = jax.ops.segment_max(e, row, num_segments=N)
        ex = jnp.exp(e - m[row])
        denom = jax.ops.segment_sum(ex, row, num_segments=N)
        att = ex / denom[row]
        h_prime = jax.ops.segment_sum(att[:, None] * Wh[col], row, num_segments=N)
        return jax.nn.relu(h_prime)

    def _L0_mix_ref(x, Wq, bq, Wk, bk, Wv, bv, Wo, bo, W1, b1, W2, b2, ln1_g, ln1_b, ln2_g, ln2_b):
        import jax, jax.numpy as jnp
        import numpy as np
        D_MODEL = 256
        NHEAD = 8
        D_HEAD = D_MODEL // NHEAD
        DIM_FF = 1024
        B, L = (4, 2048)
        LN_EPS = 1e-05

        def _layernorm(x, g, b):
            mu = jnp.mean(x, axis=-1, keepdims=True)
            var = jnp.mean((x - mu) ** 2, axis=-1, keepdims=True)
            return (x - mu) * jax.lax.rsqrt(var + LN_EPS) * g + b

        def _phi(x):
            return jnp.where(x > 0, x + 1.0, jnp.exp(x))
        Bq, Lq, _ = x.shape
        q = (x @ Wq + bq).reshape(Bq, Lq, NHEAD, D_HEAD)
        k = (x @ Wk + bk).reshape(Bq, Lq, NHEAD, D_HEAD)
        v = (x @ Wv + bv).reshape(Bq, Lq, NHEAD, D_HEAD)
        q_phi = _phi(q)
        k_phi = _phi(k)
        kv = jnp.einsum('blhd,blhe->bhde', k_phi, v)
        k_sum = k_phi.sum(axis=1)
        z = 1.0 / (jnp.einsum('blhd,bhd->blh', q_phi, k_sum) + 1e-06)
        out = jnp.einsum('blhd,bhde,blh->blhe', q_phi, kv, z)
        out = out.reshape(Bq, Lq, D_MODEL) @ Wo + bo
        x = _layernorm(x + out, ln1_g, ln1_b)
        ff = jax.nn.relu(x @ W1 + b1) @ W2 + b2
        x = _layernorm(x + ff, ln2_g, ln2_b)
        return x

    def _L0_ffn_ref(features, router_w1, router_b1, router_w2, router_b2, expert_w1, expert_b1, expert_w2, expert_b2, expert_w3, expert_b3):
        import jax, jax.numpy as jnp
        import numpy as np
        E, D, H, TOP_K = (6, 256, 256, 2)
        ROUTER_H = D // 2
        rh = jax.nn.relu(features @ router_w1 + router_b1)
        expert_logits = jax.nn.softmax(rh @ router_w2 + router_b2, axis=-1)
        top_w, top_i = jax.lax.top_k(expert_logits, TOP_K)
        routing_weights = jax.nn.softmax(top_w, axis=-1)
        h1 = jax.nn.relu(jnp.einsum('bsd,edh->bseh', features, expert_w1) + expert_b1)
        h2 = jax.nn.relu(jnp.einsum('bseh,ehf->bsef', h1, expert_w2) + expert_b2)
        expert_out = jnp.einsum('bsef,efo->bseo', h2, expert_w3) + expert_b3
        sel = jnp.take_along_axis(expert_out, top_i[:, :, :, None], axis=2)
        combined = jnp.sum(sel * routing_weights[..., None], axis=2)
        return combined
    xn = _layernorm(x, axis=-1)
    x = x + _L0_gnn_ref(xn, L0_gnn_W_w, L0_gnn_W_b, L0_gnn_a_w, L0_gnn_a_b, src, dst) + _L0_mix_ref(xn[None], L0_mix_Wq, L0_mix_bq, L0_mix_Wk, L0_mix_bk, L0_mix_Wv, L0_mix_bv, L0_mix_Wo, L0_mix_bo, L0_mix_W1, L0_mix_b1, L0_mix_W2, L0_mix_b2, L0_mix_ln1_g, L0_mix_ln1_b, L0_mix_ln2_g, L0_mix_ln2_b)[0]
    x = x + _L0_ffn_ref(_layernorm(x, axis=-1)[None], L0_ffn_router_w1, L0_ffn_router_b1, L0_ffn_router_w2, L0_ffn_router_b2, L0_ffn_expert_w1, L0_ffn_expert_b1, L0_ffn_expert_w2, L0_ffn_expert_b2, L0_ffn_expert_w3, L0_ffn_expert_b3)[0]
    return x

_drawn_inputs = setup_inputs


def setup_inputs(seed=0):
    import zlib

    import numpy as np

    out = dict(_drawn_inputs(seed))
    spreads = {'L0_mix_bq': (0.0, 0.8),
     'L0_mix_bk': (0.0, 0.8),
     'L0_mix_bv': (0.0, 0.1),
     'L0_mix_bo': (0.0, 0.1),
     'L0_mix_b1': (0.0, 0.1),
     'L0_mix_b2': (0.0, 0.1),
     'L0_mix_ln1_g': (1.0, 0.2),
     'L0_mix_ln1_b': (0.0, 0.1),
     'L0_mix_ln2_g': (1.0, 0.2),
     'L0_mix_ln2_b': (0.0, 0.1),
     'L0_ffn_router_b1': (0.0, 0.393),
     'L0_ffn_router_b2': (0.0, 0.1),
     'L0_ffn_expert_b1': (0.0, 0.8),
     'L0_ffn_expert_b2': (0.0, 0.557),
     'L0_ffn_expert_b3': (0.0, 0.1)}
    factors = {'L0_gnn_W_b': 8.0, 'L0_mix_Wq': 8.0, 'L0_mix_Wk': 8.0, 'L0_mix_Wv': 6.726}
    for name, (base, spread) in spreads.items():
        noise = np.random.default_rng([zlib.crc32(name.encode()), seed]).standard_normal(out[name].shape)
        drawn = base * np.exp(spread * noise) if base else spread * noise
        out[name] = jnp.asarray(drawn.astype(out[name].dtype))
    for name, factor in factors.items():
        out[name] = (out[name] * factor).astype(out[name].dtype)
    return out
```

```python
import concourse.bass as bass
from concourse import mybir
from contextlib import ExitStack

F32 = mybir.dt.float32
I32 = mybir.dt.int32
U32 = mybir.dt.uint32
ALU = mybir.AluOpType
ACT = mybir.ActivationFunctionType
AX = mybir.AxisListType

N, D, E = 6250, 256, 100000
R = 125
NT = N // R
CH = 2 * R
NC = N // CH
L = 128
COLS = -(-E // L)
GT = 4
GS = GT * L
NG = 250
assert NG >= (E - NT) // GS + NT and NG % 10 == 0 and NT * R == N and NC * 2 == NT
SLOTS = NG * GS
WROW = D + 2
FF, RH, NX = 1024, 128, 6
HD = 32
FAR = 2.0e6
NOROW = 200.0
STAGE = 17
SC_IT = COLS // (2 * STAGE)
assert SC_IT * 2 * STAGE == COLS


def at(step, k=1, off=0):
    it, per, j = step
    return it * (per * k) + (j * k + off)


def wait(eng, sem, value):
    if not isinstance(value, int) or value > 0:
        eng.wait_ge(sem, value)


def mixer_order(first, both, final, eng):
    first((0, 2, 0), 0)
    both((0, 2, 0), 0, (0, 2, 1), 1)
    both((0, 2, 1), 1, (0, 2, 2), 0)
    with eng.Fori(1, NC // 2 - 1) as it:
        both((it, 2, 0), 0, (it, 2, 1), 1)
        both((it, 2, 1), 1, (it, 2, 2), 0)
    it = NC // 2 - 1
    both((it, 2, 0), 0, (it, 2, 1), 1)
    both((it, 2, 1), 1, (it, 2, 2), 0, False)
    final((NC // 2, 2, 0), 0)


def gps_kernel(nc, x, src, dst, gW, gWb, ga, gab, Wq, bq, Wk, bk, Wv, bv, Wo, bo, W1, b1, W2, b2,
               l1g, l1b, l2g, l2b, rw1, rb1, rw2, rb2, ew1, eb1, ew2, eb2, ew3, eb3, out):
    table = nc.dram_tensor("wh_table", [N, WROW], F32, kind="Internal").ap()
    slots = nc.dram_tensor("sorted_slots", [SLOTS, 2], I32, kind="Internal").ap()

    with ExitStack() as ctx:
        def sb(name, shape, dt=F32):
            return ctx.enter_context(nc.sbuf_tensor(name, shape, dt))

        def sem(name):
            return ctx.enter_context(nc.semaphore(name))

        bank = [ctx.enter_context(nc.psum_tensor(f"bank{i}", [128, 512], F32)) for i in range(8)]

        xn = sb("xn", [R, NT, D])
        iota_row = sb("iota_row", [L, R])
        ident = sb("ident", [128, 128])
        ones = sb("ones", [128, 128])
        iota8 = sb("iota8", [128, 8])
        eps = sb("eps", [128, 1])
        fd = sb("fd", [R, NT])
        fr = sb("fr", [R, NT])
        fr_c = sb("fr_c", [R, NT])
        shift = sb("shift", [128, 1])
        group_block = sb("group_block", [1, NG], I32)
        rstd_all = sb("rstd_all", [R, NT])
        acc_mem = sb("acc_mem", [128, NT * WROW])
        acc = acc_mem[0:R, :].rearrange("p (b w) -> p b w", w=WROW)
        srt_mem = acc_mem[:, 0:9 * COLS]
        srt = [srt_mem[:, i * COLS:(i + 1) * COLS] for i in range(9)]
        AREA = 22300
        area = sb("area", [128, AREA])

        def carve(start):
            place = [start]

            def take(*shape):
                n = 1
                for s in shape:
                    n *= s
                a = area[:, place[0]:place[0] + n]
                place[0] += n
                assert place[0] <= AREA, place[0]
                if len(shape) == 2:
                    a = a.rearrange("p (a b) -> p a b", a=shape[0])
                if len(shape) == 3:
                    a = a.rearrange("p (a b c) -> p a b c", a=shape[0], b=shape[1])
                return a
            return take

        take = carve(0)
        w_gk = take(2, 512)
        w_v = take(2, D)
        w_q = take(2, D)
        w_o = take(2, D)
        w_1 = take(2, FF)
        w_2 = take(8, D)
        bias_g, bias_k, bias_v, bias_o, bias_2 = (take(D) for _ in range(5))
        g1, be1, g2, be2 = (take(D) for _ in range(4))
        a_dst, a_src = take(D), take(D)
        ab = take(1)
        bias_q = take(2)
        bias_1 = take(8)
        xnT = take(2, 2, CH)
        kb = take(2, D)
        ke = take(2, D)
        kr = take(2, D)
        vaug = take(2, 2, R + 4)
        whs = take(2, WROW)
        kv_bd = take(2, 128)
        ks_bd = take(2, 128)
        diag_mask = take(128)
        tri = take(128)
        scratch, scratch2 = take(D), take(D)
        qe, qr, phiq, att = (take(2, CH) for _ in range(4))
        y1 = take(2, 2, D)
        x1 = take(2, 2, D)
        x1T = take(2, CH)
        xs = take(2, 2, D)
        hT = take(8, CH)
        stats = take(2, 2, 6)
        mv = take(2, 2, 2)
        sd = take(2, 2)
        rs = take(2, 2)
        fdiag = take(128)
        held_vector = sem("held_vector")
        held_gpsimd = sem("held_gpsimd")

        def hold(eng):
            eng.sem_inc(held_gpsimd if eng is nc.gpsimd else held_vector, 1)

        def rows(t):
            return xn[:, bass.ds(t, 1), :].rearrange("p a b -> p (a b)")

        hflat = hT.rearrange("p a b -> p (a b)")
        sts = hflat[0:R, 0:NT * 6].rearrange("p (t s) -> p t s", s=6)
        mvs = sb("mvs_mem", [R, 2 * NT])[:, :].rearrange("p (t s) -> p t s", s=2)

        iota_blk = sb("iota_blk", [128, NT])
        tot = sb("tot", [128, NT])
        this_blk = sb("this_blk", [128, 1])
        one_tot = sb("one_tot", [128, 1])
        fr_one = sb("fr_one", [128, 2])
        cnt = sb("cnt", [128, NT])
        off = sb("off", [128, NT])
        ngf = sb("ngf", [128, NT])
        tmp50 = sb("tmp50", [128, NT])
        gend = sb("gend", [128, NT])
        gcol = sb("gcol", [128, 1])
        neg1 = sb("neg1", [128, 1])
        int50 = sb("int50", [128, NT], I32)
        iota_g = sb("iota_g", [NT, NG])
        gcmp = sb("gcmp", [NT, NG])
        stage_pos = sb("stage_pos", [L, 2, STAGE], I32)
        stage_pay = sb("stage_pay", [L, 2, STAGE, 2], I32)
        srcf, blk, q0, posf, cmp, cum, onesl = srt[0:7]
        pay = srt_mem[:, 7 * COLS:9 * COLS].bitcast(I32).rearrange("p (c k) -> p c k", k=2)
        srci = q0.bitcast(I32)
        dsti = cum.bitcast(I32)
        posi = blk.bitcast(I32)

        edges_in = sem("edges_in")
        prefilled = sem("prefilled")
        consts = sem("consts")
        const_step = sem("const_step")
        w_in = sem("w_in")
        x_in = [sem(f"x_in{i}") for i in range(NC)]
        rank_step = sem("rank_step")
        rank_loop = sem("rank_loop")
        count_step = sem("count_step")
        prefix_done = sem("prefix_done")
        gcmp_ready = sem("gcmp_ready")
        gmap_done = sem("gmap_done")
        pos_ready = sem("pos_ready")
        staged = sem("staged")
        scattered = [sem(f"scattered{i}") for i in range(2)]
        ln_step = sem("ln_step")
        var_ready = sem("var_ready")
        sd_ready = sem("sd_ready")
        xn_ready = sem("xn_ready")
        p_tp = sem("p_tp")
        p_tc = sem("p_tc")
        p_wk = sem("p_wk")
        p_kb = sem("p_kb")
        p_free = sem("p_free")
        p_ke = sem("p_ke")
        p_kv = sem("p_kv")
        p_kvd = sem("p_kvd")
        p_wh = sem("p_wh")
        p_row = sem("p_row")
        p_out = [sem(f"p_out{i}") for i in range(2)]
        kvb = sem("kvb")
        sh_diag = sem("sh_diag")
        sh_pe = sem("sh_pe")
        sh_step = sem("sh_step")
        m_xt = sem("m_xt")
        m_xc = sem("m_xc")
        m_q = sem("m_q")
        m_qa = sem("m_qa")
        m_phi = sem("m_phi")
        m_nd = sem("m_nd")
        m_att = sem("m_att")
        m_atc = sem("m_atc")
        m_o = sem("m_o")
        m_ln = [sem(f"m_ln{i}") for i in range(2)]
        m_va = [sem(f"m_va{i}") for i in range(2)]
        m_sd = [sem(f"m_sd{i}") for i in range(2)]
        m_shift = sem("m_shift")
        m_x1 = sem("m_x1")
        m_t1 = sem("m_t1")
        m_tc1 = sem("m_tc1")
        m_h = sem("m_h")
        m_hc = sem("m_hc")
        m_ff = sem("m_ff")
        m_y = sem("m_y")
        m_x = sem("m_x")
        m_xs = sem("m_xs")

        halves = "(k p) n -> p k n"
        loads = [
            (w_gk[:, :, 0:D], gW.rearrange(halves, p=128)), (w_gk[:, :, D:2 * D], Wk.rearrange(halves, p=128)),
            (w_v, Wv.rearrange(halves, p=128)), (w_q, Wq.rearrange(halves, p=128)),
            (w_o, Wo.rearrange(halves, p=128)), (w_1, W1.rearrange(halves, p=128)),
            (w_2, W2.rearrange(halves, p=128)),
            (bias_g, gWb.partition_broadcast(128)), (bias_k, bk.partition_broadcast(128)),
            (bias_v, bv.partition_broadcast(128)), (bias_o, bo.partition_broadcast(128)),
            (bias_2, b2.partition_broadcast(128)), (g1, l1g.partition_broadcast(128)),
            (be1, l1b.partition_broadcast(128)), (g2, l2g.partition_broadcast(128)),
            (be2, l2b.partition_broadcast(128)), (a_dst, ga[0:D].partition_broadcast(128)),
            (a_src, ga[D:2 * D].partition_broadcast(128)), (ab, gab.partition_broadcast(128)),
            (bias_q, bq.rearrange("(m p) -> p m", p=128)), (bias_1, b1.rearrange("(m p) -> p m", p=128)),
        ]

        with nc.Block() as block:
            @block.sync
            def _(sp):
                last = E - (L - 1) * COLS
                for arr, to in ((src, srci), (dst, dsti)):
                    sp.dma_start(to[0:L - 1, :], arr[0:(L - 1) * COLS].rearrange("(p c) -> p c", c=COLS)).then_inc(edges_in, 16)
                    sp.dma_start(to[L - 1:L, 0:last], arr[(L - 1) * COLS:E].rearrange("(p c) -> p c", p=1)).then_inc(edges_in, 16)
                for i in range(NC):
                    sp.dma_start(xn[:, 2 * i:2 * i + 2, :],
                                 x[CH * i:CH * (i + 1), :].rearrange("(t p) d -> p t d", p=R)).then_inc(x_in[i], 16)
                with sp.Fori(0, NC) as it:
                    for j in range(2):
                        t = (it, 2, j)
                        sp.wait_ge(p_row, at(t, 1, 1))
                        sp.dma_start(table[bass.ds(at(t, R), R), :], whs[0:R, j, :]).then_inc(p_out[j], 16)
                for j in range(2):
                    sp.wait_ge(p_out[j], 16 * NC)

            @block.gpsimd
            def _(g):
                empty = area[:, 0:2000].rearrange("p (s k) -> p s k", k=2)
                g.memset(empty[:, :, 0:1].bitcast(I32), 0).then_inc(const_step, 1)
                g.memset(empty[:, :, 1:2], NOROW).then_inc(const_step, 1)
                g.wait_ge(const_step, 2)
                g.dma_start(slots.rearrange("(p s) k -> p (s k)", p=128), area[:, 0:2 * SLOTS // 128].bitcast(I32)).then_inc(prefilled, 16)
                g.iota(iota_row[:, :], pattern=[[1, R]], base=0, channel_multiplier=0, allow_small_or_imprecise_dtypes=True)
                g.iota(iota_blk[:, :], pattern=[[1, NT]], base=0, channel_multiplier=0, allow_small_or_imprecise_dtypes=True)
                g.iota(iota_g[:, :], pattern=[[1, NG]], base=0, channel_multiplier=0, allow_small_or_imprecise_dtypes=True)
                g.iota(iota8[:, :], pattern=[[1, 8]], base=0, channel_multiplier=0, allow_small_or_imprecise_dtypes=True)
                g.memset(ones[:, :], 1.0).then_inc(const_step, 1)
                g.memset(ident[:, :], 0.0).then_inc(const_step, 1)
                g.wait_ge(const_step, 4)
                g.affine_select(out=ident[:, :], in_=ident[:, :], compare_op=ALU.not_equal, fill=1.0, base=0,
                                pattern=[[-1, 128]], channel_multiplier=1)
                g.wait_ge(prefilled, 16)
                g.affine_select(out=tri, in_=ones[:, :], compare_op=ALU.is_gt, fill=0.0, base=0,
                                pattern=[[1, 128]], channel_multiplier=-1)
                heads = diag_mask.rearrange("p (h e) -> p h e", h=4)
                g.affine_select(out=heads, in_=ones[:, :].rearrange("p (h e) -> p h e", h=4), compare_op=ALU.is_ge,
                                fill=0.0, base=0, pattern=[[-HD, 4], [0, HD]], channel_multiplier=1).then_inc(const_step, 1)
                g.wait_ge(const_step, 5)
                g.affine_select(out=heads, in_=heads, compare_op=ALU.is_ge, fill=0.0, base=HD - 1,
                                pattern=[[HD, 4], [0, HD]], channel_multiplier=-1)
                for s in range(2):
                    g.memset(vaug[:, s, :, 128:129], 1.0)
                    g.memset(whs[:, s, WROW - 1:WROW], 1.0)
                g.memset(eps[:, :], 1e-5).then_inc(consts, 1)

                g.wait_ge(pos_ready, 1)

                def scatter(it, first):
                    for s in range(2):
                        if not first:
                            g.wait_ge(scattered[s], it * (16 * STAGE))
                            hold(g)
                        col = it * (2 * STAGE) + s * STAGE
                        g.tensor_copy(stage_pos[:, s, :], posi[:, bass.ds(col, STAGE)])
                        g.tensor_copy(stage_pay[:, s, :, :], pay[:, bass.ds(col, STAGE), :]).then_inc(staged, 1)
                        g.wait_ge(staged, it * 2 + s + 1)
                        hold(g)
                        for c in range(STAGE):
                            g.indirect_dma_start(out=slots, out_offset=bass.IndirectOffsetOnAxis(ap=stage_pos[:, s, c:c + 1], axis=0),
                                                 in_=stage_pay[:, s, c, :], in_offset=None,
                                                 bounds_check=SLOTS - 1, oob_is_err=False).then_inc(scattered[s], 16)
                scatter(0, True)
                with g.Fori(1, SC_IT) as it:
                    scatter(it, False)
                for s in range(2):
                    g.wait_ge(scattered[s], 16 * STAGE * SC_IT)

            @block.vector
            def _(dve):
                V = nc.vector
                n = [0]

                def step(ins):
                    n[0] += 1
                    ins.then_inc(rank_step, 1)
                    dve.wait_ge(rank_step, n[0])

                dve.wait_ge(edges_in, 64)
                dve.wait_ge(consts, 1)
                V.memset(srcf, float(N))
                step(V.memset(pay, 0))
                last = E - (L - 1) * COLS
                V.tensor_copy(srcf[0:96, :], srci[0:96, :])
                V.tensor_copy(pay[0:96, :, 0], dsti[0:96, :])
                V.tensor_copy(srcf[96:128, 0:last], srci[96:128, 0:last])
                V.tensor_copy(pay[96:128, 0:last, 0], dsti[96:128, 0:last])
                V.tensor_copy(srcf[96:127, last:COLS], srci[96:127, last:COLS])
                step(V.tensor_copy(pay[96:127, last:COLS, 0], dsti[96:127, last:COLS]))
                step(V.tensor_scalar(cum.bitcast(I32), srcf, 0.5, 1.0 / R, ALU.add, ALU.mult))
                step(V.tensor_copy(q0, cum.bitcast(I32)))
                step(V.scalar_tensor_tensor(cmp, q0, float(R), srcf, ALU.mult, ALU.is_gt))
                step(V.tensor_tensor(blk, q0, cmp, ALU.subtract))
                step(V.scalar_tensor_tensor(pay.bitcast(F32)[:, :, 1], blk, -float(R), srcf, ALU.mult, ALU.add))
                V.memset(onesl, 1.0)
                step(V.memset(this_blk[:, :], 0.0))
                with dve.Fori(0, NT) as a:
                    V.tensor_scalar(cmp, blk, this_blk[:, :], None, ALU.is_equal, ALU.add, accum_out=one_tot[:, :]).then_inc(count_step, 1)
                    dve.wait_ge(count_step, a * 3 + 1)
                    hold(dve)
                    V.tensor_copy(tot[:, bass.ds(a, 1)], one_tot[:, :]).then_inc(count_step, 1)
                    V.tensor_scalar(this_blk[:, :], this_blk[:, :], 1.0, None, ALU.add).then_inc(count_step, 1)
                    dve.wait_ge(count_step, a * 3 + 3)
                V.memset(posf, FAR)
                dve.wait_ge(prefix_done, 1)
                step(V.tensor_scalar(cnt[:, :], bank[7][:, 0:NT], float(GS - 1), None, ALU.add))
                step(V.tensor_scalar(int50[:, :], cnt[:, :], 0.5, 1.0 / GS, ALU.add, ALU.mult))
                step(V.tensor_copy(ngf[:, :], int50[:, :]))
                step(V.scalar_tensor_tensor(tmp50[:, :], ngf[:, :], float(GS), cnt[:, :], ALU.mult, ALU.is_gt))
                step(V.tensor_tensor(ngf[:, :], ngf[:, :], tmp50[:, :], ALU.subtract))
                step(V.tensor_tensor_scan(gend[:, :], onesl[:, 0:NT], ngf[:, :], 0.0, ALU.mult, ALU.add))
                step(V.tensor_tensor(tmp50[:, :], gend[:, :], ngf[:, :], ALU.subtract))
                step(V.scalar_tensor_tensor(off[:, :], tmp50[:, :], float(GS), bank[6][:, 0:NT], ALU.mult, ALU.add))
                step(V.tensor_tensor(tmp50[:, :], gend[:, :], ident[:, 0:NT], ALU.mult))
                step(V.tensor_reduce(gcol[:, :], tmp50[:, :], AX.X, ALU.add))
                V.tensor_scalar(gcmp[:, :], iota_g[:, :], gcol[0:NT, :], None, ALU.is_ge).then_inc(gcmp_ready, 1)
                dve.wait_ge(gmap_done, 1)
                V.tensor_scalar(group_block[:, :], bank[5][0:1, 0:NG], float(NT - 1), None, ALU.min)
                with dve.Fori(0, NT) as a:
                    V.tensor_scalar(cmp, blk, iota_blk[:, bass.ds(a, 1)], None, ALU.is_equal).then_inc(rank_loop, 1)
                    dve.wait_ge(rank_loop, a * 3 + 1)
                    V.tensor_tensor_scan(cum, onesl, cmp, off[:, bass.ds(a, 1)], ALU.mult, ALU.add).then_inc(rank_loop, 1)
                    dve.wait_ge(rank_loop, a * 3 + 2)
                    hold(dve)
                    V.copy_predicated(posf, cmp.bitcast(I32), cum).then_inc(rank_loop, 1)
                    dve.wait_ge(rank_loop, a * 3 + 3)
                V.tensor_scalar(posi, posf, -1.0, None, ALU.add).then_inc(pos_ready, 1)

                for i in range(NC):
                    dve.wait_ge(x_in[i], 16)
                with dve.Fori(0, NT) as t:
                    V.bn_stats(sts[:, bass.ds(t, 1), :].rearrange("p a b -> p (a b)"),
                               xn[:, bass.ds(t, 1), :].rearrange("p a b -> p (a b)")).then_inc(ln_step, 1)
                dve.wait_ge(ln_step, NT)
                step(V.tensor_tensor(mvs[:, :, 0], sts[:, :, 1], sts[:, :, 4], ALU.add))
                V.tensor_tensor(mvs[:, :, 1], sts[:, :, 1], sts[:, :, 4], ALU.subtract)
                step(V.tensor_scalar(mvs[:, :, 0], mvs[:, :, 0], 0.5, None, ALU.mult))
                step(V.tensor_tensor(rstd_all[:, :], mvs[:, :, 1], mvs[:, :, 1], ALU.mult))
                step(V.tensor_scalar(rstd_all[:, :], rstd_all[:, :], D / 4.0, None, ALU.mult))
                step(V.tensor_tensor(rstd_all[:, :], rstd_all[:, :], sts[:, :, 2], ALU.add))
                step(V.tensor_tensor(rstd_all[:, :], rstd_all[:, :], sts[:, :, 5], ALU.add))
                V.tensor_scalar(mvs[:, :, 1], rstd_all[:, :], 1.0 / D, None, ALU.mult).then_inc(var_ready, 1)
                dve.wait_ge(sd_ready, 1)
                step(V.reciprocal(rstd_all[:, :], rstd_all[:, :]))
                dve.wait_ge(w_in, 16 * len(loads))

                def normalise(t, j):
                    wait(dve, p_tp, at(t, 1, -1))
                    V.tensor_scalar(xs[0:R, 0, j, :], rows(at(t)), mvs[:, bass.ds(at(t), 1), 0], rstd_all[:, bass.ds(at(t), 1)],
                                    ALU.subtract, ALU.mult).then_inc(xn_ready, 1)

                def proj(t, j):
                    prod, vb = bank[2 + j], bank[4 + j]
                    dve.wait_ge(p_wk, at(t, 1, 1))
                    wait(dve, p_kvd, at(t, 1, -1))
                    V.tensor_tensor(kb[0:R, j, :], prod[0:R, D:2 * D], bias_k[0:R, :], ALU.add).then_inc(p_kb, 1)
                    wait(dve, p_out[j], at((t[0], 1, 0), 16))
                    V.tensor_tensor(whs[0:R, j, 0:D], prod[0:R, 0:D], bias_g[0:R, :], ALU.add).then_inc(p_wh, 1)
                    V.tensor_tensor(vaug[0:R, j, :, 0:128], vb[0:R, 0:D].rearrange("p (h e) -> p h e", h=2),
                                    bias_v[0:R, :].rearrange("p (h e) -> p h e", h=2), ALU.add).then_inc(p_free, 1)
                    dve.wait_ge(p_wh, at(t, 2, 1))
                    V.tensor_tensor_reduce(scratch[0:R, :], whs[0:R, j, 0:D], a_src[0:R, :], 1.0, 0.0, ALU.mult, ALU.add,
                                           accum_out=fr_one[0:R, j:j + 1])
                    V.tensor_tensor_reduce(scratch2[0:R, :], whs[0:R, j, 0:D], a_dst[0:R, :], 1.0, 0.0, ALU.mult, ALU.add,
                                           accum_out=whs[0:R, j, D:D + 1]).then_inc(p_row, 1)
                    dve.wait_ge(p_row, at(t, 1, 1))
                    hold(dve)
                    V.tensor_copy(fd[:, bass.ds(at(t), 1)], whs[0:R, j, D:D + 1])
                    V.tensor_copy(fr[:, bass.ds(at(t), 1)], fr_one[0:R, j:j + 1]).then_inc(p_wh, 1)
                    dve.wait_ge(p_ke, at(t, 1, 1))
                    V.scalar_tensor_tensor(kb[0:R, j, :], ke[0:R, j, :], 1.0, kr[0:R, j, :], ALU.min, ALU.add).then_inc(p_kv, 1)

                for j in range(2):
                    normalise((0, 2, j), j)
                normalise((0, 2, 2), 0)
                proj((0, 2, 0), 0)
                normalise((0, 2, 3), 1)
                proj((0, 2, 1), 1)
                with dve.Fori(1, NC - 1) as it:
                    for j in range(2):
                        normalise((it, 2, j + 2), j)
                        proj((it, 2, j), j)
                for j in range(2):
                    proj((NC - 1, 2, j), j)

                dve.wait_ge(p_wh, 2 * NT)
                step(V.tensor_reduce(neg1[0:R, :], fd[:, :], AX.X, ALU.min))
                V.tensor_scalar(fdiag[0:R, 0:R], ident[0:R, 0:R], neg1[0:R, :], None, ALU.mult).then_inc(sh_diag, 1)
                dve.wait_ge(p_kvd, NT)
                for h in range(2):
                    V.tensor_tensor(kv_bd[:, h, :], bank[6 + h][:, 0:128], diag_mask, ALU.mult)
                    last_i = V.tensor_scalar(ks_bd[:, h, :], diag_mask, bank[6 + h][:, 128:129], None, ALU.mult)
                last_i.then_inc(kvb, 1)
                dve.wait_ge(sh_pe, 1)
                step(V.tensor_reduce(gcol[:, :], bank[2][:, 0:R], AX.X, ALU.min))
                step(V.tensor_scalar(shift[:, :], gcol[:, :], -1.0, 1.0, ALU.mult, ALU.add))
                step(V.tensor_scalar(fr[:, :], fr[:, :], ab[0:R, :], None, ALU.add))
                V.tensor_scalar(fr_c[:, :], fr[:, :], shift[0:R, :], None, ALU.subtract).then_inc(m_shift, 1)

                def norm(c, k, dst_of, bias, gam, bet):
                    mine = m_ln[k]
                    dve.wait_ge(mine, at(c, 6, 1))
                    V.tensor_tensor(y1[0:R, k, :, :], y1[0:R, k, :, :], bias[0:R, :].unsqueeze(1).to_broadcast([R, 2, D]), ALU.add).then_inc(mine, 1)
                    dve.wait_ge(mine, at(c, 6, 2))
                    for r in range(2):
                        last_s = V.bn_stats(stats[0:R, k, r, :], y1[0:R, k, r, :])
                    last_s.then_inc(mine, 1)
                    dve.wait_ge(mine, at(c, 6, 3))
                    hold(dve)
                    for r in range(2):
                        last_s = V.bn_aggr(mv[0:R, k, r, :], stats[0:R, k, r, :])
                    last_s.then_inc(m_va[k], 1)
                    dve.wait_ge(m_sd[k], at(c, 1, 1))
                    V.reciprocal(rs[0:R, k, :], sd[0:R, k, :]).then_inc(mine, 1)
                    dve.wait_ge(mine, at(c, 6, 4))
                    for r in range(2):
                        last_s = V.tensor_scalar(y1[0:R, k, r, :], y1[0:R, k, r, :], mv[0:R, k, r, 0:1], rs[0:R, k, r:r + 1],
                                                 ALU.subtract, ALU.mult)
                    last_s.then_inc(mine, 1)
                    dve.wait_ge(mine, at(c, 6, 5))
                    V.tensor_tensor(y1[0:R, k, :, :], y1[0:R, k, :, :], gam[0:R, :].unsqueeze(1).to_broadcast([R, 2, D]), ALU.mult).then_inc(mine, 1)
                    dve.wait_ge(mine, at(c, 6, 6))
                    return V.tensor_tensor(dst_of, y1[0:R, k, :, :], bet[0:R, :].unsqueeze(1).to_broadcast([R, 2, D]), ALU.add)

                def attend(c, j):
                    dve.wait_ge(m_qa, at(c, 1, 1))
                    V.scalar_tensor_tensor(phiq, qe, 1.0, qr, ALU.min, ALU.add).then_inc(m_phi, 1)
                    dve.wait_ge(m_nd, at(c, 1, 1))
                    V.tensor_scalar(att, bank[4][:, 0:2 * CH].rearrange("p (m n) -> p m n", m=2), 1e-6, None, ALU.add).then_inc(m_atc, 1)
                    dve.wait_ge(m_atc, at(c, 2, 1))
                    V.reciprocal(att, att).then_inc(m_atc, 1)
                    dve.wait_ge(m_atc, at(c, 2, 2))
                    V.tensor_tensor(att, att, bank[3][:, 0:2 * CH].rearrange("p (m n) -> p m n", m=2), ALU.mult).then_inc(m_att, 1)
                    dve.wait_ge(m_o, at(c, 1, 1))
                    wait(dve, m_x1, at(c))
                    V.tensor_tensor(y1[0:R, 0, :, :], bank[5][0:R, :].rearrange("p (t d) -> p t d", t=2),
                                    xs[0:R, j, :, :], ALU.add).then_inc(m_ln[0], 1)
                    norm(c, 0, x1[0:R, j, :, :], bias_o, g1, be1).then_inc(m_x1, 1)

                def feed(c, j):
                    dve.wait_ge(m_ff, at(c, 1, 1))
                    wait(dve, m_x, at(c))
                    V.tensor_tensor(y1[0:R, 1, :, :], bank[2][0:R, :].rearrange("p (t d) -> p t d", t=2), x1[0:R, j, :, :],
                                    ALU.add).then_inc(m_ln[1], 1)
                    norm(c, 1, y1[0:R, 1, :, :], bias_2, g2, be2).then_inc(m_y, 1)
                    dve.wait_ge(m_y, at(c, 1, 1))
                    both_rows = xn[:, bass.ds(at(c, 2), 2), :]
                    V.tensor_tensor(both_rows, both_rows, y1[0:R, 1, :, :], ALU.add).then_inc(m_x, 1)

                def prepare(c, j):
                    for r in range(2):
                        t = at(c, 2, r)
                        last_p = V.tensor_scalar(xs[0:R, j, r, :], rows(t), mvs[:, bass.ds(t, 1), 0], rstd_all[:, bass.ds(t, 1)],
                                                 ALU.subtract, ALU.mult)
                    last_p.then_inc(m_xs, 1)

                def first(c, j):
                    prepare(c, j)
                    prepare((0, 2, 1), 1)
                    attend(c, j)

                def both(c, j, d, jd, more=True):
                    attend(d, jd)
                    if more:
                        prepare((c[0], 2, j + 2), j)
                    feed(c, j)

                mixer_order(first, both, feed, dve)

            @block.scalar
            def _(act):
                A = nc.scalar
                for to, frm in loads:
                    if to is loads[0][0]:
                        act.wait_ge(prefilled, 16)
                    act.dma_start(to, frm, allow_slow_non_contiguous=True).then_inc(w_in, 16)
                act.wait_ge(var_ready, 1)
                act.wait_ge(consts, 1)
                A.activation(rstd_all[:, :], mvs[:, :, 1], ACT.Sqrt, bias=eps[0:R, :]).then_inc(sd_ready, 1)

                def proj(t, j):
                    act.wait_ge(p_tp, at(t, 1, 1))
                    wait(act, p_wk, at(t, 1, -1))
                    A.copy(xnT[:, j, :, 0:R], bank[j][:, 0:2 * R].rearrange("p (k n) -> p k n", k=2)).then_inc(p_tc, 1)

                def keys(t, j):
                    act.wait_ge(p_kb, at(t, 1, 1))
                    wait(act, p_kv, at(t, 1, -1))
                    A.activation(ke[0:R, j, :], kb[0:R, j, :], ACT.Exp)
                    A.activation(kr[0:R, j, :], kb[0:R, j, :], ACT.Relu).then_inc(p_ke, 1)

                proj((0, 2, 0), 0)
                proj((0, 2, 1), 1)
                keys((0, 2, 0), 0)
                with act.Fori(1, NC) as it:
                    proj((it, 2, 0), 0)
                    keys((it, 2, -1), 1)
                    proj((it, 2, 1), 1)
                    keys((it, 2, 0), 0)
                keys((NC, 2, -1), 1)

                def attend_in(c, j):
                    act.wait_ge(m_xt, at(c, 1, 1))
                    wait(act, m_q, at(c, 1, -1))
                    A.copy(xnT[:, j, :, :], bank[0][:, 0:2 * CH].rearrange("p (k n) -> p k n", k=2)).then_inc(m_xc, 1)

                def attend_q(c, j):
                    act.wait_ge(m_q, at(c, 1, 1))
                    wait(act, m_phi, at(c))
                    for m in range(2):
                        A.activation(qe[:, m, :], bank[2][:, m * CH:(m + 1) * CH], ACT.Exp, bias=bias_q[:, m:m + 1])
                    for m in range(2):
                        last = A.activation(qr[:, m, :], bank[2][:, m * CH:(m + 1) * CH], ACT.Relu, bias=bias_q[:, m:m + 1])
                    last.then_inc(m_qa, 1)

                def root(c, k):
                    act.wait_ge(m_va[k], at(c, 1, 1))
                    A.activation(sd[0:R, k, :], mv[0:R, k, :, 1], ACT.Sqrt, bias=eps[0:R, :]).then_inc(m_sd[k], 1)

                def feed_in(c, j):
                    act.wait_ge(m_t1, at(c, 1, 1))
                    wait(act, m_h, at(c, 4))
                    A.copy(x1T, bank[1][:, 0:2 * CH].rearrange("p (k n) -> p k n", k=2)).then_inc(m_tc1, 1)

                def hidden(c, p):
                    act.wait_ge(m_h, at(c, 4, p + 1))
                    wait(act, m_ff, at(c))
                    for i in range(2):
                        f = 2 * p + i
                        last = A.activation(hT[:, f, :], bank[6 + p % 2][:, i * CH:(i + 1) * CH], ACT.Relu, bias=bias_1[:, f:f + 1])
                    last.then_inc(m_hc, 1)

                def first(c, j):
                    attend_in(c, j)
                    attend_q(c, j)
                    root(c, 0)

                def both(c, j, d, jd, more=True):
                    feed_in(c, j)
                    attend_in(d, jd)
                    hidden(c, 0)
                    attend_q(d, jd)
                    for p in range(1, 4):
                        hidden(c, p)
                    root(d, 0)
                    root(c, 1)

                def final(c, j):
                    feed_in(c, j)
                    for p in range(4):
                        hidden(c, p)
                    root(c, 1)

                mixer_order(first, both, final, act)

            @block.tensor
            def _(pe):
                T = nc.tensor
                pe.wait_ge(consts, 1)
                pe.wait_ge(count_step, 3 * NT)
                T.matmul(bank[6][:, 0:NT], tri, tot[:, :], start=True, stop=True)
                T.matmul(bank[7][:, 0:NT], ones[:, :], tot[:, :], start=True, stop=True).then_inc(prefix_done, 1)
                pe.wait_ge(gcmp_ready, 1)
                T.matmul(bank[5][:, 0:NG], ones[0:NT, :], gcmp[:, :], start=True, stop=True).then_inc(gmap_done, 1)
                pe.wait_ge(pos_ready, 1)
                pe.wait_ge(w_in, 16 * len(loads))

                def transposes(t, j):
                    pe.wait_ge(xn_ready, at(t, 1, 1))
                    wait(pe, p_tc, at(t, 1, -1))
                    for k in range(2):
                        last = T.transpose(bank[j][:, k * R:(k + 1) * R],
                                           xs[0:R, 0, j, k * 128:(k + 1) * 128], ident[0:R, 0:R])
                    last.then_inc(p_tp, 1)

                def products(t, j):
                    pe.wait_ge(p_tc, at(t, 1, 1))
                    wait(pe, p_free, at(t, 1, -1))
                    for k in range(2):
                        T.matmul(bank[2 + j][0:R, :], xnT[:, j, k, 0:R], w_gk[:, k, :], start=(k == 0), stop=(k == 1))
                        last = T.matmul(bank[4 + j][0:R, 0:D], xnT[:, j, k, 0:R], w_v[:, k, :], start=(k == 0), stop=(k == 1))
                    last.then_inc(p_wk, 1)

                def kv(t, j, start, stop):
                    pe.wait_ge(p_kv, at(t, 1, 1))
                    for h in range(2):
                        last = T.matmul(bank[6 + h][:, 0:129], kb[0:R, j, h * 128:(h + 1) * 128], vaug[0:R, j, h, 0:129],
                                        start=start, stop=stop)
                    last.then_inc(p_kvd, 1)

                transposes((0, 2, 0), 0)
                transposes((0, 2, 1), 1)
                products((0, 2, 0), 0)
                products((0, 2, 1), 1)
                kv((0, 2, 0), 0, True, False)
                with pe.Fori(1, NC) as it:
                    transposes((it, 2, 0), 0)
                    kv((it, 2, -1), 1, False, False)
                    products((it, 2, 0), 0)
                    transposes((it, 2, 1), 1)
                    kv((it, 2, 0), 0, False, False)
                    products((it, 2, 1), 1)
                kv((NC, 2, -1), 1, False, True)
                pe.wait_ge(sh_diag, 1)
                pe.wait_ge(p_free, NT)
                T.matmul(bank[2][:, 0:R], ones[0:R, :], fdiag[0:R, 0:R], start=True, stop=True).then_inc(sh_pe, 1)
                pe.wait_ge(kvb, 1)

                def xt(c, j):
                    pe.wait_ge(m_xs, at(c, 1, 1))
                    wait(pe, m_xc, at(c))
                    for k in range(2):
                        for r in range(2):
                            last = T.transpose(bank[0][:, k * CH + r * R:k * CH + (r + 1) * R],
                                               xs[0:R, j, r, k * 128:(k + 1) * 128],
                                               ident[0:R, 0:R])
                    last.then_inc(m_xt, 1)

                def q(c, j):
                    pe.wait_ge(m_xc, at(c, 1, 1))
                    wait(pe, m_y, at(c, 1, -1))
                    if isinstance(c[0], int) and at(c) == 0:
                        pe.wait_ge(m_shift, 1)
                    for m in range(2):
                        for k in range(2):
                            last = T.matmul(bank[2][:, m * CH:(m + 1) * CH], w_q[:, k, m * 128:(m + 1) * 128], xnT[:, j, k, :],
                                            start=(k == 0), stop=(k == 1))
                    last.then_inc(m_q, 1)

                def numden(c):
                    pe.wait_ge(m_phi, at(c, 1, 1))
                    wait(pe, m_att, at(c))
                    for m in range(2):
                        T.matmul(bank[3][:, m * CH:(m + 1) * CH], kv_bd[:, m, :], phiq[:, m, :], start=True, stop=True)
                        last = T.matmul(bank[4][:, m * CH:(m + 1) * CH], ks_bd[:, m, :], phiq[:, m, :], start=True, stop=True)
                    last.then_inc(m_nd, 1)

                def o(c):
                    pe.wait_ge(m_att, at(c, 1, 1))
                    wait(pe, m_x1, at(c))
                    for r in range(2):
                        for m in range(2):
                            last = T.matmul(bank[5][0:R, r * D:(r + 1) * D], att[:, m, r * R:(r + 1) * R], w_o[:, m, :],
                                            start=(m == 0), stop=(m == 1))
                    last.then_inc(m_o, 1)

                def t1(c, j):
                    pe.wait_ge(m_x1, at(c, 1, 1))
                    wait(pe, m_tc1, at(c))
                    for k in range(2):
                        for r in range(2):
                            last = T.transpose(bank[1][:, k * CH + r * R:k * CH + (r + 1) * R],
                                               x1[0:R, j, r, k * 128:(k + 1) * 128], ident[0:R, 0:R])
                    last.then_inc(m_t1, 1)

                def hidden(c, p):
                    if p == 0:
                        pe.wait_ge(m_tc1, at(c, 1, 1))
                    wait(pe, m_hc, at(c, 4, p - 1))
                    for i in range(2):
                        for k in range(2):
                            f = 2 * p + i
                            last = T.matmul(bank[6 + p % 2][:, i * CH:(i + 1) * CH], w_1[:, k, f * 128:(f + 1) * 128], x1T[:, k, :],
                                            start=(k == 0), stop=(k == 1))
                    last.then_inc(m_h, 1)

                def ff(c, r):
                    if r == 0:
                        pe.wait_ge(m_hc, at(c, 4, 4))
                    for f in range(8):
                        last = T.matmul(bank[2][0:R, r * D:(r + 1) * D], hT[:, f, r * R:(r + 1) * R], w_2[:, f, :],
                                        start=(f == 0), stop=(f == 7))
                    if r == 1:
                        last.then_inc(m_ff, 1)

                def first(c, j):
                    xt(c, j)
                    q(c, j)
                    numden(c)
                    o(c)

                def both(c, j, d, jd, more=True):
                    t1(c, j)
                    xt(d, jd)
                    hidden(c, 0)
                    q(d, jd)
                    hidden(c, 1)
                    hidden(c, 2)
                    numden(d)
                    hidden(c, 3)
                    ff(c, 0)
                    o(d)
                    ff(c, 1)

                def final(c, j):
                    t1(c, j)
                    for p in range(4):
                        hidden(c, p)
                    ff(c, 0)
                    ff(c, 1)

                mixer_order(first, both, final, pe)

        take = carve(0)
        gath = take(5, GT, WROW)
        payr = take(5, GT, 2)
        xm = take(2, GT, R)
        hot = take(2, GS)
        sm = take(2, GT, R)
        fdc = take(2, GT)
        gmax, gt, gl = take(2), take(2), take(2)
        gd = take(2)
        alpha = take(5)
        frm = take(2, 2)
        mrun = take(NT)
        e1, e2, e3, e4, ex = (take(2, GT) for _ in range(5))
        payi = payr.bitcast(I32)
        XT, QE, US = (0, 1), (2, 3), (4, 5)

        acc_zero = sem("acc_zero")
        pay_in = [sem(f"pay_in{i}") for i in range(5)]
        gathered = [sem(f"gathered{i}") for i in range(5)]
        d_fdc = sem("d_fdc")
        d_x = sem("d_x")
        p_xt = sem("p_xt")
        a_hot = sem("a_hot")
        d_m = sem("d_m")
        d_frm = sem("d_frm")
        a_alpha = sem("a_alpha")
        p_q = sem("p_q")
        d_es = sem("d_es")
        d_e = sem("d_e")
        a_ex = sem("a_ex")
        d_s = sem("d_s")
        p_main = sem("p_main")
        d_acc = sem("d_acc")
        PER = 10

        def pipeline(eng, stages):
            def run(it, j, first):
                for lag, stage in enumerate(stages):
                    if stage is not None and not (first and j < lag):
                        stage((it, PER, j - lag), j - lag)
            for j in range(PER):
                run(0, j, True)
            with eng.Fori(1, NG // PER) as it:
                for j in range(PER):
                    run(it, j, False)
            for j in range(len(stages) - 1):
                for lag, stage in enumerate(stages):
                    if stage is not None and lag > j:
                        stage((NG // PER, PER, j - lag), j - lag)

        with nc.Block() as block:
            @block.sync
            def _(sp):
                def load(s, j):
                    wait(sp, d_s, at(s, 1, -4))
                    sp.dma_start(payi[:, j % 5, :, :].rearrange("p t k -> p (t k)"),
                                 slots[bass.ds(at(s, GS), GS), :].rearrange("(p t) k -> p (t k)", t=GT)).then_inc(pay_in[j % 5], 16)
                pipeline(sp, [load])

            @block.gpsimd
            def _(g):
                g.memset(acc_mem[:, :], 0.0).then_inc(acc_zero, 1)

                def gather(s, j):
                    g.wait_ge(pay_in[j % 5], at((s[0], 2, j // 5), 16, 16))
                    wait(g, p_main, at(s, 1, -4))
                    hold(g)
                    for t in range(GT):
                        g.indirect_dma_start(out=gath[:, j % 5, t, :], out_offset=None, in_=table,
                                             in_offset=bass.IndirectOffsetOnAxis(ap=payi[:, j % 5, t, 0:1], axis=0),
                                             bounds_check=N - 1, oob_is_err=False).then_inc(gathered[j % 5], 16)
                pipeline(g, [gather])

            @block.vector
            def _(dve):
                V = nc.vector
                V.memset(mrun[0:R, :], -1.0e30).then_inc(acc_zero, 1)
                dve.wait_ge(acc_zero, 2)

                def block_of(s):
                    return dve.value_load(group_block[0:1, bass.ds(at(s), 1)], min_val=0, max_val=NT - 1)

                def mark(s, j):
                    b = j % 2
                    dve.wait_ge(gathered[j % 5], at((s[0], 2, j // 5), 16 * GT, 16 * GT))
                    wait(dve, p_xt, at(s, 1, -1))
                    V.tensor_scalar(fdc[:, b, :], gath[:, j % 5, :, D], shift[:, :], None, ALU.add).then_inc(d_fdc, 1)
                    dve.wait_ge(d_fdc, at(s, 1, 1))
                    for t in range(GT):
                        last = V.tensor_scalar(xm[:, b, t, :], iota_row[:, :], payr[:, j % 5, t, 1:2], fdc[:, b, t:t + 1],
                                               ALU.is_equal, ALU.mult)
                    last.then_inc(d_x, 1)

                def peak(s, j):
                    b = j % 2
                    dve.wait_ge(p_xt, at(s, 1, 1))
                    V.tensor_reduce(gmax[0:R, b:b + 1], bank[XT[b]][0:R, :], AX.X, ALU.max).then_inc(d_m, 1)
                    r = block_of(s)
                    wait(dve, p_q, at(s, 1, -1))
                    hold(dve)
                    V.tensor_copy(frm[0:R, b, 0:1], fr[:, bass.ds(r, 1)])
                    dve.wait_ge(d_m, at(s, 5, 1))
                    V.tensor_tensor(gt[0:R, b:b + 1], gmax[0:R, b:b + 1], fr_c[:, bass.ds(r, 1)], ALU.add).then_inc(d_m, 1)
                    dve.wait_ge(d_m, at(s, 5, 2))
                    V.scalar_tensor_tensor(gl[0:R, b:b + 1], gt[0:R, b:b + 1], 0.2, gt[0:R, b:b + 1], ALU.mult, ALU.max).then_inc(d_m, 1)
                    dve.wait_ge(d_m, at(s, 5, 3))
                    wait(dve, d_frm, at(s))
                    V.tensor_tensor(frm[0:R, b, 1:2], gl[0:R, b:b + 1], mrun[0:R, bass.ds(r, 1)], ALU.max).then_inc(d_m, 1)
                    dve.wait_ge(d_m, at(s, 5, 4))
                    wait(dve, a_alpha, at(s, 1, -1))
                    V.tensor_tensor(gd[0:R, b:b + 1], mrun[0:R, bass.ds(r, 1)], frm[0:R, b, 1:2], ALU.subtract).then_inc(d_m, 1)
                    dve.wait_ge(d_m, at(s, 5, 5))
                    hold(dve)
                    V.tensor_copy(mrun[0:R, bass.ds(r, 1)], frm[0:R, b, 1:2]).then_inc(d_frm, 1)

                def score(s, j):
                    b = j % 2
                    dve.wait_ge(p_q, at(s, 1, 1))
                    pair = bank[QE[b]][:, 0:2 * GT].rearrange("p (t k) -> p t k", k=2)
                    V.tensor_tensor(e1[:, b, :], gath[:, j % 5, :, D], pair[:, :, 0], ALU.add).then_inc(d_es, 1)
                    dve.wait_ge(d_es, at(s, 3, 1))
                    V.scalar_tensor_tensor(e2[:, b, :], e1[:, b, :], 0.2, e1[:, b, :], ALU.mult, ALU.max).then_inc(d_es, 1)
                    dve.wait_ge(d_es, at(s, 3, 2))
                    V.tensor_tensor(e3[:, b, :], e2[:, b, :], pair[:, :, 1], ALU.subtract).then_inc(d_es, 1)
                    dve.wait_ge(d_es, at(s, 3, 3))
                    V.tensor_scalar(e4[:, b, :], e3[:, b, :], 60.0, None, ALU.min).then_inc(d_e, 1)

                def weigh(s, j):
                    b = j % 2
                    dve.wait_ge(a_ex, at(s, 1, 1))
                    wait(dve, p_main, at(s, 1, -1))
                    for t in range(GT):
                        last = V.tensor_scalar(sm[:, b, t, :], iota_row[:, :], payr[:, j % 5, t, 1:2], ex[:, b, t:t + 1],
                                               ALU.is_equal, ALU.mult)
                    last.then_inc(d_s, 1)

                def gather_up(s, j):
                    b = j % 2
                    r = block_of(s)
                    dve.wait_ge(a_alpha, at(s, 1, 1))
                    dve.wait_ge(p_main, at(s, 1, 1))
                    wait(dve, d_acc, at(s))
                    row = acc[:, bass.ds(r, 1), :].rearrange("p a b -> p (a b)")
                    V.scalar_tensor_tensor(row, row, alpha[0:R, j % 5:j % 5 + 1], bank[US[b]][0:R, 0:WROW], ALU.mult, ALU.add).then_inc(d_acc, 1)

                pipeline(dve, [mark, peak, score, weigh, gather_up])

            @block.scalar
            def _(act):
                A = nc.scalar

                def spread(s, j):
                    b = j % 2
                    act.wait_ge(d_m, at(s, 5, 1))
                    wait(act, p_q, at(s, 1, -1))
                    A.activation(hot[0:R, b, :], bank[XT[b]][0:R, :], ACT.Sign).then_inc(a_hot, 1)
                    act.wait_ge(d_m, at(s, 5, 5))
                    wait(act, d_acc, at(s, 1, -4))
                    A.activation(alpha[0:R, j % 5:j % 5 + 1], gd[0:R, b:b + 1], ACT.Exp).then_inc(a_alpha, 1)

                def expo(s, j):
                    b = j % 2
                    act.wait_ge(d_e, at(s, 1, 1))
                    wait(act, d_s, at(s, 1, -1))
                    A.activation(ex[:, b, :], e4[:, b, :], ACT.Exp).then_inc(a_ex, 1)

                pipeline(act, [None, spread, expo])

            @block.tensor
            def _(pe):
                T = nc.tensor

                def turn(s, j):
                    b = j % 2
                    pe.wait_ge(d_x, at(s, 1, 1))
                    wait(pe, a_hot, at(s, 1, -1))
                    wait(pe, d_m, at(s, 5, -9))
                    for t in range(GT):
                        last = T.transpose(bank[XT[b]][0:R, t * L:(t + 1) * L], xm[:, b, t, :], ident[:, :])
                    last.then_inc(p_xt, 1)

                def fetch(s, j):
                    b = j % 2
                    pe.wait_ge(a_hot, at(s, 1, 1))
                    pe.wait_ge(d_frm, at(s, 1, 1))
                    wait(pe, d_e, at(s, 1, -1))
                    for t in range(GT):
                        last = T.matmul(bank[QE[b]][:, 2 * t:2 * t + 2], hot[0:R, b, t * L:(t + 1) * L], frm[0:R, b, :],
                                        start=True, stop=True)
                    last.then_inc(p_q, 1)

                def total(s, j):
                    b = j % 2
                    pe.wait_ge(d_s, at(s, 1, 1))
                    wait(pe, d_acc, at(s, 1, -1))
                    for t in range(GT):
                        last = T.matmul(bank[US[b]][0:R, 0:WROW], sm[:, b, t, :], gath[:, j % 5, t, :], start=(t == 0), stop=(t == GT - 1))
                    last.then_inc(p_main, 1)

                pipeline(pe, [turn, fetch, None, total])

        take = carve(0)
        w_x1, w_x2, w_x3 = (take(2 * NX, D) for _ in range(3))
        w_r1 = take(2, RH)
        w_r2 = take(NX)
        b_x1, b_x2 = take(2 * NX), take(2 * NX)
        b_r1 = take(1)
        b_r2 = take(NX)
        b_x3 = take(D)
        rec = take(NT)
        den = take(NT)
        x2 = take(2, 2, D)
        feat = take(2, D)
        featT = take(2, 2, CH)
        rh = take(CH)
        lg, lm, pe_ = take(2, NX), take(2, NX), take(2, NX)
        prob = take(2, 8)
        top = take(2, 8)
        topi = take(2, 8).bitcast(U32)
        topf = take(2, 2)
        mx, sm2, dd, ee, dn, w_a, w_b = (take(2) for _ in range(7))
        ca, cb = take(2, NX), take(2, NX)
        cw = take(2, 2, NX)
        cT = take(CH)
        h1 = take(2, 2, CH)
        h2 = take(2, 2, CH)
        res = take(2, 2, D)
        st3, mv3 = take(2, 6), take(2, 2)
        sd3, rs3 = take(2), take(2)

        w3_in = sem("w3_in")
        z3 = sem("z3")
        f_st = sem("f_st")
        f_va = sem("f_va")
        f_sd = sem("f_sd")
        f_rdy = sem("f_rdy")
        t_ft = sem("t_ft")
        c_ft = sem("c_ft")
        t_r = sem("t_r")
        c_rh = sem("c_rh")
        t_lg = sem("t_lg")
        k_st = sem("k_st")
        k_lm = sem("k_lm")
        c_pe = sem("c_pe")
        k_dd = sem("k_dd")
        c_ee = sem("c_ee")
        k_cs = sem("k_cs")
        k_cw = sem("k_cw")
        t_ct = sem("t_ct")
        c_ct = sem("c_ct")
        t_b3 = sem("t_b3")
        k_base = sem("k_base")
        t_h1 = sem("t_h1")
        c_h1 = sem("c_h1")
        t_h2 = sem("t_h2")
        c_h2 = sem("c_h2")
        t_o = sem("t_o")
        k_o = sem("k_o")
        out_sem = [sem(f"out_sem{i}") for i in range(2)]
        loads3 = [
            (w_x1, ew1.rearrange("e (k p) n -> p (e k) n", p=128)), (w_x2, ew2.rearrange("e (k p) n -> p (e k) n", p=128)),
            (w_x3, ew3.rearrange("e (k p) n -> p (e k) n", p=128)), (w_r1, rw1.rearrange("(k p) n -> p k n", p=128)),
            (w_r2, rw2), (b_x1, eb1.rearrange("e (m p) -> p (e m)", p=128)), (b_x2, eb2.rearrange("e (m p) -> p (e m)", p=128)),
            (b_r1, rb1.rearrange("(p a) -> p a", a=1)), (b_r2, rb2.partition_broadcast(128)), (b_x3[0:NX, :], eb3),
        ]

        def chunks(eng, before, body, drain):
            before()
            body((0, 2, 0), 0)
            body((0, 2, 1), 1)
            with eng.Fori(1, NC // 2) as it:
                body((it, 2, 0), 0)
                body((it, 2, 1), 1)
            drain((NC // 2, 2, 0), 0)

        with nc.Block() as block:
            @block.sync
            def _(sp):
                def store(c, j):
                    sp.wait_ge(k_o, at(c, NX, NX))
                    sp.dma_start(out[bass.ds(at(c, CH), CH), :].rearrange("(t p) d -> p t d", p=R), res[0:R, j, :, :]).then_inc(out_sem[j], 16)

                chunks(sp, lambda: None, store, store)
                sp.wait_ge(out_sem[0], 16 * (NC // 2 + 1))
                sp.wait_ge(out_sem[1], 16 * (NC // 2))

            @block.vector
            def _(dve):
                V = nc.vector
                V.tensor_scalar(den[0:R, :], acc[:, :, WROW - 1], 0.0, None, ALU.is_equal).then_inc(z3, 1)
                V.memset(prob, -1.0)
                dve.wait_ge(z3, 1)
                V.tensor_tensor(rec[0:R, :], den[0:R, :], acc[:, :, WROW - 1], ALU.add).then_inc(z3, 1)
                dve.wait_ge(z3, 2)
                V.reciprocal(rec[0:R, :], rec[0:R, :]).then_inc(z3, 1)
                dve.wait_ge(z3, 3)
                dve.wait_ge(w3_in, 16 * len(loads3))

                def features(c, j):
                    wait(dve, k_base, at(c, 1, -1))
                    for r in range(2):
                        last = V.tensor_scalar(x2[0:R, j, r, :], acc[:, bass.ds(at(c, 2, r), 1), 0:D].rearrange("p a b -> p (a b)"),
                                               rec[0:R, bass.ds(at(c, 2, r), 1)], 0.0, ALU.mult, ALU.max)
                    last.then_inc(f_st, 1)
                    dve.wait_ge(f_st, at(c, 4, 1))
                    V.tensor_tensor(x2[0:R, j, :, :], x2[0:R, j, :, :], xn[:, bass.ds(at(c, 2), 2), :], ALU.add).then_inc(f_st, 1)
                    dve.wait_ge(f_st, at(c, 4, 2))
                    for r in range(2):
                        last = V.bn_stats(st3[0:R, r, :], x2[0:R, j, r, :])
                    last.then_inc(f_st, 1)
                    dve.wait_ge(f_st, at(c, 4, 3))
                    hold(dve)
                    for r in range(2):
                        last = V.bn_aggr(mv3[0:R, r, :], st3[0:R, r, :])
                    last.then_inc(f_va, 1)
                    dve.wait_ge(f_sd, at(c, 1, 1))
                    V.reciprocal(rs3[0:R, :], sd3[0:R, :]).then_inc(f_st, 1)
                    dve.wait_ge(f_st, at(c, 4, 4))
                    wait(dve, t_ft, at(c))
                    for r in range(2):
                        last = V.tensor_scalar(feat[0:R, r, :], x2[0:R, j, r, :], mv3[0:R, r, 0:1], rs3[0:R, r:r + 1],
                                               ALU.subtract, ALU.mult)
                    last.then_inc(f_rdy, 1)

                def route(c, j):
                    k = [0]

                    def step(ins):
                        k[0] += 1
                        ins.then_inc(k_st, 1)
                        dve.wait_ge(k_st, at(c, 11, k[0]))
                        hold(dve)

                    dve.wait_ge(t_lg, at(c, 1, 1))
                    step(V.tensor_tensor(lg[0:R, :, :], bank[7][0:R, 256:256 + 2 * NX].rearrange("p (t e) -> p t e", t=2),
                                         b_r2[0:R, :].unsqueeze(1).to_broadcast([R, 2, NX]), ALU.add))
                    step(V.tensor_reduce(mx[0:R, :], lg[0:R, :, :], AX.X, ALU.max))
                    V.tensor_tensor(lm[0:R, :, :], lg[0:R, :, :], mx[0:R, :].unsqueeze(2).to_broadcast([R, 2, NX]), ALU.subtract).then_inc(k_lm, 1)
                    dve.wait_ge(c_pe, at(c, 1, 1))
                    step(V.tensor_reduce(sm2[0:R, :], pe_[0:R, :, :], AX.X, ALU.add))
                    step(V.reciprocal(sm2[0:R, :], sm2[0:R, :]))
                    step(V.tensor_tensor(prob[0:R, :, 0:NX], pe_[0:R, :, :], sm2[0:R, :].unsqueeze(2).to_broadcast([R, 2, NX]), ALU.mult))
                    for r in range(2):
                        last = V.max(top[0:R, r, :], prob[0:R, r, :])
                    step(last)
                    for r in range(2):
                        last = V.max_index(topi[0:R, r, :], top[0:R, r, :], prob[0:R, r, :])
                    step(last)
                    V.tensor_tensor(dd[0:R, :], top[0:R, :, 1], top[0:R, :, 0], ALU.subtract).then_inc(k_dd, 1)
                    step(V.tensor_copy(topf[0:R, :, :], topi[0:R, :, 0:2]))
                    dve.wait_ge(c_ee, at(c, 1, 1))
                    step(V.tensor_scalar(dn[0:R, :], ee[0:R, :], 1.0, None, ALU.add))
                    step(V.reciprocal(w_a[0:R, :], dn[0:R, :]))
                    step(V.tensor_tensor(w_b[0:R, :], w_a[0:R, :], ee[0:R, :], ALU.mult))
                    assert k[0] == 11
                    for r in range(2):
                        V.tensor_scalar(ca[0:R, r, :], iota8[0:R, 0:NX], topf[0:R, r, 0:1], w_a[0:R, r:r + 1], ALU.is_equal, ALU.mult)
                        last = V.tensor_scalar(cb[0:R, r, :], iota8[0:R, 0:NX], topf[0:R, r, 1:2], w_b[0:R, r:r + 1], ALU.is_equal, ALU.mult)
                    last.then_inc(k_cs, 1)
                    dve.wait_ge(k_cs, at(c, 1, 1))
                    V.tensor_tensor(cw[0:R, j, :, :], ca[0:R, :, :], cb[0:R, :, :], ALU.add).then_inc(k_cw, 1)

                def base(c, j):
                    dve.wait_ge(t_b3, at(c, 1, 1))
                    wait(dve, out_sem[j], at((c[0], 1, 0), 16))
                    V.tensor_tensor(res[0:R, j, :, :], x2[0:R, j, :, :], bank[6][0:R, :].rearrange("p (t d) -> p t d", t=2), ALU.add).then_inc(k_base, 1)
                    dve.wait_ge(k_base, at(c, 1, 1))
                    dve.wait_ge(k_cw, at(c, 1, 1))

                def add(c, j, e):
                    dve.wait_ge(t_o, at(c, NX, e + 1))
                    wait(dve, k_o, at(c, NX, e))
                    for r in range(2):
                        last = V.scalar_tensor_tensor(res[0:R, j, r, :], bank[4 + e % 2][0:R, r * D:(r + 1) * D], cw[0:R, j, r, e:e + 1],
                                                      res[0:R, j, r, :], ALU.mult, ALU.add)
                    last.then_inc(k_o, 1)

                def before():
                    features((0, 2, 0), 0)
                    route((0, 2, 0), 0)

                def body(c, j, more=True):
                    base(c, j)
                    for e in range(3):
                        add(c, j, e)
                    if more:
                        features((c[0], 2, j + 1), 1 - j)
                    for e in range(3, NX):
                        add(c, j, e)
                    if more:
                        route((c[0], 2, j + 1), 1 - j)
                chunks(dve, before, body, lambda c, j: body(c, j, False))

            @block.scalar
            def _(act):
                A = nc.scalar
                for to, frm_ in loads3:
                    act.dma_start(to, frm_, allow_slow_non_contiguous=True).then_inc(w3_in, 16)
                act.wait_ge(w3_in, 16 * len(loads3))

                def relu2(src_bank, to, bias, e, done):
                    for m in range(2):
                        last = A.activation(to[:, m, :], src_bank[:, m * CH:(m + 1) * CH], ACT.Relu, bias=bias[:, 2 * e + m:2 * e + m + 1])
                    last.then_inc(done, 1)

                def up(c, e):
                    act.wait_ge(t_h1, at(c, NX, e + 1))
                    wait(act, t_h2, at(c, NX, e - 1))
                    relu2(bank[e % 2], h1[:, e % 2, :, :], b_x1, e, c_h1)

                def mid(c, e):
                    act.wait_ge(t_h2, at(c, NX, e + 1))
                    wait(act, t_o, at(c, NX, e - 1))
                    relu2(bank[2 + e % 2], h2[:, e % 2, :, :], b_x2, e, c_h2)

                def root(c):
                    act.wait_ge(f_va, at(c, 1, 1))
                    A.activation(sd3[0:R, :], mv3[0:R, :, 1], ACT.Sqrt, bias=eps[0:R, :]).then_inc(f_sd, 1)

                def ft(c, j):
                    act.wait_ge(t_ft, at(c, 1, 1))
                    wait(act, t_h1, at(c, NX, -NX))
                    A.copy(featT[:, j, :, :], bank[6][:, 0:2 * CH].rearrange("p (k n) -> p k n", k=2)).then_inc(c_ft, 1)

                def rhid(c):
                    act.wait_ge(t_r, at(c, 1, 1))
                    wait(act, t_lg, at(c))
                    A.activation(rh, bank[7][:, 0:CH], ACT.Relu, bias=b_r1).then_inc(c_rh, 1)

                def exps(c):
                    act.wait_ge(k_lm, at(c, 1, 1))
                    A.activation(pe_[0:R, :, :], lm[0:R, :, :], ACT.Exp).then_inc(c_pe, 1)
                    act.wait_ge(k_dd, at(c, 1, 1))
                    A.activation(ee[0:R, :], dd[0:R, :], ACT.Exp).then_inc(c_ee, 1)

                def ct(c):
                    act.wait_ge(t_ct, at(c, 1, 1))
                    wait(act, t_b3, at(c))
                    A.copy(cT[0:NX, :], bank[7][0:NX, 0:CH]).then_inc(c_ct, 1)

                def before():
                    root((0, 2, 0))
                    ft((0, 2, 0), 0)
                    rhid((0, 2, 0))
                    exps((0, 2, 0))

                def body(c, j, more=True):
                    d = (c[0], 2, j + 1)
                    up(c, 0)
                    up(c, 1)
                    mid(c, 0)
                    up(c, 2)
                    mid(c, 1)
                    ct(c)
                    up(c, 3)
                    mid(c, 2)
                    up(c, 4)
                    mid(c, 3)
                    if more:
                        root(d)
                    up(c, 5)
                    mid(c, 4)
                    if more:
                        ft(d, 1 - j)
                    mid(c, 5)
                    if more:
                        rhid(d)
                        exps(d)
                chunks(act, before, body, lambda c, j: body(c, j, False))

            @block.tensor
            def _(pe):
                T = nc.tensor
                pe.wait_ge(w3_in, 16 * len(loads3))

                def tf(c):
                    pe.wait_ge(f_rdy, at(c, 1, 1))
                    wait(pe, k_base, at(c))
                    for k in range(2):
                        for r in range(2):
                            last = T.transpose(bank[6][:, k * CH + r * R:k * CH + (r + 1) * R], feat[0:R, r, k * 128:(k + 1) * 128], ident[0:R, 0:R])
                    last.then_inc(t_ft, 1)

                def router(c, j):
                    pe.wait_ge(c_ft, at(c, 1, 1))
                    wait(pe, c_ct, at(c))
                    for k in range(2):
                        last = T.matmul(bank[7][:, 0:CH], w_r1[:, k, :], featT[:, j, k, :], start=(k == 0), stop=(k == 1))
                    last.then_inc(t_r, 1)

                def logits(c):
                    pe.wait_ge(c_rh, at(c, 1, 1))
                    for r in range(2):
                        last = T.matmul(bank[7][0:R, 256 + r * NX:256 + (r + 1) * NX], rh[:, r * R:(r + 1) * R], w_r2, start=True, stop=True)
                    last.then_inc(t_lg, 1)

                def bias3(c, j):
                    pe.wait_ge(k_cw, at(c, 1, 1))
                    for r in range(2):
                        last = T.transpose(bank[7][0:NX, r * R:(r + 1) * R], cw[0:R, j, r, :], ident[0:R, 0:R])
                    last.then_inc(t_ct, 1)

                def bias3b(c):
                    pe.wait_ge(c_ct, at(c, 1, 1))
                    for r in range(2):
                        last = T.matmul(bank[6][0:R, r * D:(r + 1) * D], cT[0:NX, r * R:(r + 1) * R], b_x3[0:NX, :], start=True, stop=True)
                    last.then_inc(t_b3, 1)

                def up(c, j, e):
                    wait(pe, c_h1, at(c, NX, e - 1))
                    for m in range(2):
                        for k in range(2):
                            last = T.matmul(bank[e % 2][:, m * CH:(m + 1) * CH], w_x1[:, 2 * e + k, m * 128:(m + 1) * 128], featT[:, j, k, :],
                                            start=(k == 0), stop=(k == 1))
                    last.then_inc(t_h1, 1)

                def mid(c, e):
                    pe.wait_ge(c_h1, at(c, NX, e + 1))
                    wait(pe, c_h2, at(c, NX, e - 1))
                    for m in range(2):
                        for k in range(2):
                            last = T.matmul(bank[2 + e % 2][:, m * CH:(m + 1) * CH], w_x2[:, 2 * e + k, m * 128:(m + 1) * 128], h1[:, e % 2, k, :],
                                            start=(k == 0), stop=(k == 1))
                    last.then_inc(t_h2, 1)

                def down(c, e):
                    pe.wait_ge(c_h2, at(c, NX, e + 1))
                    wait(pe, k_o, at(c, NX, e - 1))
                    for r in range(2):
                        for k in range(2):
                            last = T.matmul(bank[4 + e % 2][0:R, r * D:(r + 1) * D], h2[:, e % 2, k, r * R:(r + 1) * R], w_x3[:, 2 * e + k, :],
                                            start=(k == 0), stop=(k == 1))
                    last.then_inc(t_o, 1)

                def before():
                    tf((0, 2, 0))
                    router((0, 2, 0), 0)
                    logits((0, 2, 0))

                def body(c, j, more=True):
                    d = (c[0], 2, j + 1)
                    up(c, j, 0)
                    up(c, j, 1)
                    mid(c, 0)
                    up(c, j, 2)
                    mid(c, 1)
                    bias3(c, j)
                    down(c, 0)
                    bias3b(c)
                    up(c, j, 3)
                    mid(c, 2)
                    down(c, 1)
                    up(c, j, 4)
                    mid(c, 3)
                    down(c, 2)
                    up(c, j, 5)
                    mid(c, 4)
                    if more:
                        tf(d)
                    down(c, 3)
                    mid(c, 5)
                    if more:
                        router(d, 1 - j)
                    down(c, 4)
                    if more:
                        logits(d)
                    down(c, 5)
                chunks(pe, before, body, lambda c, j: body(c, j, False))


_INS = ['x', 'src', 'dst', 'L0_gnn_W_w', 'L0_gnn_W_b', 'L0_gnn_a_w', 'L0_gnn_a_b', 'L0_mix_Wq', 'L0_mix_bq', 'L0_mix_Wk',
        'L0_mix_bk', 'L0_mix_Wv', 'L0_mix_bv', 'L0_mix_Wo', 'L0_mix_bo', 'L0_mix_W1', 'L0_mix_b1', 'L0_mix_W2', 'L0_mix_b2',
        'L0_mix_ln1_g', 'L0_mix_ln1_b', 'L0_mix_ln2_g', 'L0_mix_ln2_b', 'L0_ffn_router_w1', 'L0_ffn_router_b1',
        'L0_ffn_router_w2', 'L0_ffn_router_b2', 'L0_ffn_expert_w1', 'L0_ffn_expert_b1', 'L0_ffn_expert_w2',
        'L0_ffn_expert_b2', 'L0_ffn_expert_w3', 'L0_ffn_expert_b3']
_OUTS = [((N, D), 'float32')]


def kernel(**inputs):
    import numpy as _np
    import concourse.bacc as _bacc
    from concourse import mybir as _mybir
    from concourse.bass_utils import run_bass_kernel_spmd as _run

    nc = _bacc.Bacc("TRN2", target_bir_lowering=False, num_devices=1)
    arrays, args = {}, []
    for name in _INS:
        a = _np.ascontiguousarray(inputs[name])
        arrays[f"in_{name}_dram"] = a
        args.append(nc.dram_tensor(f"in_{name}_dram", a.shape, _mybir.dt.from_np(a.dtype), kind="ExternalInput").ap())
    for i, (shape, dtype) in enumerate(_OUTS):
        dt = _mybir.dt.from_np(_np.dtype(dtype))
        args.append(nc.dram_tensor(f"out_{i}_dram", shape, dt, kind="ExternalOutput").ap())
    gps_kernel(nc, *args)
    r = _run(nc, [arrays], core_ids=[0])
    return r.results[0]["out_0_dram"]
```

```python
import concourse.bass as bass
from concourse import mybir
from contextlib import ExitStack

F32 = mybir.dt.float32
I32 = mybir.dt.int32
U32 = mybir.dt.uint32
ALU = mybir.AluOpType
ACT = mybir.ActivationFunctionType
AX = mybir.AxisListType

N, D, E = 6250, 256, 100000
R = 125
RW = R + 1
NT = N // R
CH = 2 * R
NC = N // CH
L = 128
COLS = -(-E // L)
GT = 4
GS = GT * L
NG = 250
assert NG >= (E - NT) // GS + NT and NG % 10 == 0 and NT * R == N and NC * 2 == NT
SLOTS = NG * GS
WROW = D + 2
FF, RH, NX = 1024, 128, 6
HD = 32
FAR = 2.0e6
NOROW = 200.0
FEW, SOME = 5, 10
STAGE = 17
PER = 10
SC_IT = COLS // (2 * STAGE)
assert NT % SOME == 0 and NT % FEW == 0
assert SC_IT * 2 * STAGE == COLS


def at(step, k=1, off=0):
    it, per, j = step
    return it * (per * k) + (j * k + off)


def wait(eng, sem, value):
    if not isinstance(value, int) or value > 0:
        eng.wait_ge(sem, value)


def together(eng, *parts):
    def period(it, h, more=True):
        for slot in range(PER):
            for part in parts:
                if callable(part):
                    part(slot, (it, 2, h - 1), (h - 1) % 2, more)
                    continue
                for lag, stage in part:
                    k = PER * h + slot - lag
                    if not isinstance(it, int) or 0 <= 2 * PER * it + k < NG:
                        stage((it, 2 * PER, k), k)

    for h in range(2):
        period(0, h)
    with eng.Fori(1, NC // 2) as it:
        for h in range(2):
            period(it, h)
    period(NC // 2, 0, False)
    period(NC // 2, 1, None)


def gps_kernel(nc, x, src, dst, gW, gWb, ga, gab, Wq, bq, Wk, bk, Wv, bv, Wo, bo, W1, b1, W2, b2,
               l1g, l1b, l2g, l2b, rw1, rb1, rw2, rb2, ew1, eb1, ew2, eb2, ew3, eb3, out):
    table = nc.dram_tensor("wh_table", [N, WROW], F32, kind="Internal").ap()
    slots = nc.dram_tensor("sorted_slots", [SLOTS, 2], I32, kind="Internal").ap()

    with ExitStack() as ctx:
        def sb(name, shape, dt=F32):
            return ctx.enter_context(nc.sbuf_tensor(name, shape, dt))

        def sem(name):
            return ctx.enter_context(nc.semaphore(name))

        bank = [ctx.enter_context(nc.psum_tensor(f"bank{i}", [128, 512], F32)) for i in range(8)]

        xn = sb("xn", [R, NT, D])
        iota_row = sb("iota_row", [L, RW])
        ident = sb("ident", [128, 128])
        ones = sb("ones", [128, 128])
        iota8 = sb("iota8", [128, 8])
        eps = sb("eps", [128, 1])
        small = sb("small", [128, 1])
        fd = sb("fd", [R, NT])
        fr = sb("fr", [R, NT])
        fr_c = sb("fr_c", [R, NT])
        shift = sb("shift", [128, 1])
        group_block = sb("group_block", [1, NG], I32)
        rstd_all = sb("rstd_all", [R, NT])
        acc_mem = sb("acc_mem", [128, NT * WROW])
        acc = acc_mem[0:R, :].rearrange("p (b w) -> p b w", w=WROW)
        srt_mem = acc_mem[:, 0:9 * COLS]
        srt = [srt_mem[:, i * COLS:(i + 1) * COLS] for i in range(9)]
        AREA = 26000
        area = sb("area", [128, AREA])

        def carve(start):
            place = [start]

            def take(*shape):
                n = 1
                for s in shape:
                    n *= s
                a = area[:, place[0]:place[0] + n]
                place[0] += n
                assert place[0] <= AREA, place[0]
                if len(shape) == 2:
                    a = a.rearrange("p (a b) -> p a b", a=shape[0])
                if len(shape) == 3:
                    a = a.rearrange("p (a b c) -> p a b c", a=shape[0], b=shape[1])
                return a
            return take

        take = carve(0)
        w_q = take(2, D)
        w_o = take(2, D)
        w_1 = take(2, FF)
        w_2 = take(8, D)
        bias_o, bias_2, g1, be1, g2, be2 = (take(D) for _ in range(6))
        bias_q = take(2)
        bias_1 = take(8)
        kv_bd = take(2, 128)
        ks_bd = take(2, 128)
        xnT = take(2, 2, CH)
        qe, qr, phiq, att = (take(2, CH) for _ in range(4))
        den_s = qe
        y1 = take(2, 2, D)
        x1 = take(2, 2, D)
        x1T = take(2, CH)
        xs = take(2, 2, D)
        hT = take(8, CH)
        stats = take(2, 2, 6)
        mv = take(2, 2, 2)
        lv = take(2, 2)
        rs = take(2, 2)
        GRAPH = 15900
        take = carve(GRAPH)
        w_gk = take(2, 512)
        w_v = take(2, D)
        bias_g, bias_k, bias_v = (take(D) for _ in range(3))
        a_dst, a_src = take(D), take(D)
        ab = take(1)
        kb = take(2, D)
        ke = take(2, D)
        kr = take(2, D)
        vaug = take(2, 2, R + 4)
        whs = take(2, WROW)
        diag_mask = take(128)
        tri = take(128)
        scratch, scratch2 = take(D), take(D)
        fdiag = take(128)
        held_vector = sem("held_vector")
        held_gpsimd = sem("held_gpsimd")

        def hold(eng):
            eng.sem_inc(held_gpsimd if eng is nc.gpsimd else held_vector, 1)

        def rows(t):
            return xn[:, bass.ds(t, 1), :].rearrange("p a b -> p (a b)")

        hflat = hT.rearrange("p a b -> p (a b)")
        sts = hflat[0:R, 0:NT * 6].rearrange("p (t s) -> p t s", s=6)
        mvs = sb("mvs_mem", [R, 2 * NT])[:, :].rearrange("p (t s) -> p t s", s=2)

        iota_blk, tot, cnt, off, ngf, tmp50, gend = (take(NT) for _ in range(7))
        gcol, neg1 = take(1), take(1)
        few_blks, few_tots = take(FEW), take(FEW)
        fr_one = take(2)
        int50 = take(NT).bitcast(I32)
        iota_g, gcmp = take(NG)[0:NT, :], take(NG)[0:NT, :]
        stage_pos = take(2, STAGE).bitcast(I32)
        stage_pay = take(2, STAGE, 2).bitcast(I32)
        srcf, blk, q0, posf, cmp, cum, onesl = srt[0:7]
        ring = [acc_mem[:, i * COLS:(i + 1) * COLS] for i in range(9, 15)]
        dists, cums = ring[0:2], ring[2:4]
        masks = ring[4:6] + [cmp, cum, q0]
        pay = srt_mem[:, 7 * COLS:9 * COLS].bitcast(I32).rearrange("p (c k) -> p c k", k=2)
        srci = q0.bitcast(I32)
        dsti = cum.bitcast(I32)
        posi = blk.bitcast(I32)

        edges_in = sem("edges_in")
        prefilled = sem("prefilled")
        consts = sem("consts")
        const_step = sem("const_step")
        w_in = sem("w_in")
        x_in = [sem(f"x_in{i}") for i in range(NC)]
        rank_step = sem("rank_step")
        mask_dist = sem("mask_dist")
        mask_ready = sem("mask_ready")
        scanned = sem("scanned")
        placed = sem("placed")
        count_step = sem("count_step")
        prefix_done = sem("prefix_done")
        gcmp_ready = sem("gcmp_ready")
        gmap_done = sem("gmap_done")
        pos_ready = sem("pos_ready")
        staged = sem("staged")
        scattered = [sem(f"scattered{i}") for i in range(2)]
        ln_step = sem("ln_step")
        var_ready = sem("var_ready")
        sd_ready = sem("sd_ready")
        xn_ready = sem("xn_ready")
        p_tp = sem("p_tp")
        p_tc = sem("p_tc")
        p_wk = sem("p_wk")
        p_kb = sem("p_kb")
        p_free = sem("p_free")
        p_ke = sem("p_ke")
        p_kv = sem("p_kv")
        p_kvd = sem("p_kvd")
        p_wh = sem("p_wh")
        p_row = sem("p_row")
        p_out = [sem(f"p_out{i}") for i in range(2)]
        kvb = sem("kvb")
        sh_diag = sem("sh_diag")
        sh_pe = sem("sh_pe")
        sh_step = sem("sh_step")
        m_xt = sem("m_xt")
        m_xc = sem("m_xc")
        m_q = sem("m_q")
        m_qa = sem("m_qa")
        m_phi = sem("m_phi")
        m_nd = sem("m_nd")
        m_att = sem("m_att")
        m_den = sem("m_den")
        m_rec = sem("m_rec")
        m_o = sem("m_o")
        m_ln = [sem(f"m_ln{i}") for i in range(2)]
        m_va = [sem(f"m_va{i}") for i in range(2)]
        m_lv = [sem(f"m_lv{i}") for i in range(2)]
        m_rs = [sem(f"m_rs{i}") for i in range(2)]
        m_shift = sem("m_shift")
        m_x1 = sem("m_x1")
        m_t1 = sem("m_t1")
        m_tc1 = sem("m_tc1")
        m_h = sem("m_h")
        m_hc = sem("m_hc")
        m_ff = sem("m_ff")
        m_y = sem("m_y")
        m_x = sem("m_x")
        m_xs = sem("m_xs")

        halves = "(k p) n -> p k n"
        loads = [
            (w_gk[:, :, 0:D], gW.rearrange(halves, p=128)), (w_gk[:, :, D:2 * D], Wk.rearrange(halves, p=128)),
            (w_v, Wv.rearrange(halves, p=128)), (w_q, Wq.rearrange(halves, p=128)),
            (w_o, Wo.rearrange(halves, p=128)), (w_1, W1.rearrange(halves, p=128)),
            (w_2, W2.rearrange(halves, p=128)),
            (bias_g, gWb.partition_broadcast(128)), (bias_k, bk.partition_broadcast(128)),
            (bias_v, bv.partition_broadcast(128)), (bias_o, bo.partition_broadcast(128)),
            (bias_2, b2.partition_broadcast(128)), (g1, l1g.partition_broadcast(128)),
            (be1, l1b.partition_broadcast(128)), (g2, l2g.partition_broadcast(128)),
            (be2, l2b.partition_broadcast(128)), (a_dst, ga[0:D].partition_broadcast(128)),
            (a_src, ga[D:2 * D].partition_broadcast(128)), (ab, gab.partition_broadcast(128)),
            (bias_q, bq.rearrange("(m p) -> p m", p=128)), (bias_1, b1.rearrange("(m p) -> p m", p=128)),
        ]

        with nc.Block() as block:
            @block.sync
            def _(sp):
                last = E - (L - 1) * COLS
                for arr, to in ((src, srci), (dst, dsti)):
                    sp.dma_start(to[0:L - 1, :], arr[0:(L - 1) * COLS].rearrange("(p c) -> p c", c=COLS)).then_inc(edges_in, 16)
                    sp.dma_start(to[L - 1:L, 0:last], arr[(L - 1) * COLS:E].rearrange("(p c) -> p c", p=1)).then_inc(edges_in, 16)
                for i in range(NC):
                    sp.dma_start(xn[:, 2 * i:2 * i + 2, :],
                                 x[CH * i:CH * (i + 1), :].rearrange("(t p) d -> p t d", p=R)).then_inc(x_in[i], 16)
                with sp.Fori(0, NC) as it:
                    for j in range(2):
                        t = (it, 2, j)
                        sp.wait_ge(p_row, at(t, 1, 1))
                        sp.dma_start(table[bass.ds(at(t, R), R), :], whs[0:R, j, :]).then_inc(p_out[j], 16)
                for j in range(2):
                    sp.wait_ge(p_out[j], 16 * NC)

            @block.gpsimd
            def _(g):
                empty = area[:, 0:2000].rearrange("p (s k) -> p s k", k=2)
                g.memset(empty[:, :, 0:1].bitcast(I32), 0).then_inc(const_step, 1)
                g.memset(empty[:, :, 1:2], NOROW).then_inc(const_step, 1)
                g.wait_ge(const_step, 2)
                g.dma_start(slots.rearrange("(p s) k -> p (s k)", p=128), area[:, 0:2 * SLOTS // 128].bitcast(I32)).then_inc(prefilled, 16)
                g.iota(iota_row[:, :], pattern=[[1, RW]], base=0, channel_multiplier=0, allow_small_or_imprecise_dtypes=True)
                g.iota(iota_blk[:, :], pattern=[[1, NT]], base=0, channel_multiplier=0, allow_small_or_imprecise_dtypes=True)
                g.iota(iota_g[:, :], pattern=[[1, NG]], base=0, channel_multiplier=0, allow_small_or_imprecise_dtypes=True)
                g.iota(iota8[:, :], pattern=[[1, 8]], base=0, channel_multiplier=0, allow_small_or_imprecise_dtypes=True)
                g.memset(ones[:, :], 1.0).then_inc(const_step, 1)
                g.memset(ident[:, :], 0.0).then_inc(const_step, 1)
                g.wait_ge(const_step, 4)
                g.affine_select(out=ident[:, :], in_=ident[:, :], compare_op=ALU.not_equal, fill=1.0, base=0,
                                pattern=[[-1, 128]], channel_multiplier=1)
                g.wait_ge(prefilled, 16)
                g.affine_select(out=tri, in_=ones[:, :], compare_op=ALU.is_gt, fill=0.0, base=0,
                                pattern=[[1, 128]], channel_multiplier=-1)
                heads = diag_mask.rearrange("p (h e) -> p h e", h=4)
                g.affine_select(out=heads, in_=ones[:, :].rearrange("p (h e) -> p h e", h=4), compare_op=ALU.is_ge,
                                fill=0.0, base=0, pattern=[[-HD, 4], [0, HD]], channel_multiplier=1).then_inc(const_step, 1)
                g.wait_ge(const_step, 5)
                g.affine_select(out=heads, in_=heads, compare_op=ALU.is_ge, fill=0.0, base=HD - 1,
                                pattern=[[HD, 4], [0, HD]], channel_multiplier=-1)
                for s in range(2):
                    g.memset(vaug[:, s, :, 128:129], 1.0)
                    g.memset(whs[:, s, WROW - 1:WROW], 1.0)
                g.memset(small[:, :], 1e-6)
                g.memset(eps[:, :], 1e-5).then_inc(consts, 1)

                g.wait_ge(pos_ready, 1)

                def scatter(it, first):
                    for s in range(2):
                        if not first:
                            g.wait_ge(scattered[s], it * (16 * STAGE))
                            hold(g)
                        col = it * (2 * STAGE) + s * STAGE
                        g.tensor_copy(stage_pos[:, s, :], posi[:, bass.ds(col, STAGE)])
                        g.tensor_copy(stage_pay[:, s, :, :], pay[:, bass.ds(col, STAGE), :]).then_inc(staged, 1)
                        g.wait_ge(staged, it * 2 + s + 1)
                        hold(g)
                        for c in range(STAGE):
                            g.indirect_dma_start(out=slots, out_offset=bass.IndirectOffsetOnAxis(ap=stage_pos[:, s, c:c + 1], axis=0),
                                                 in_=stage_pay[:, s, c, :], in_offset=None,
                                                 bounds_check=SLOTS - 1, oob_is_err=False).then_inc(scattered[s], 16)
                scatter(0, True)
                with g.Fori(1, SC_IT) as it:
                    scatter(it, False)
                for s in range(2):
                    g.wait_ge(scattered[s], 16 * STAGE * SC_IT)

            @block.vector
            def _(dve):
                V = nc.vector
                n = [0]

                def step(ins):
                    n[0] += 1
                    ins.then_inc(rank_step, 1)
                    dve.wait_ge(rank_step, n[0])

                dve.wait_ge(edges_in, 64)
                dve.wait_ge(consts, 1)
                V.memset(srcf, float(N))
                step(V.memset(pay, 0))
                last = E - (L - 1) * COLS
                V.tensor_copy(srcf[0:96, :], srci[0:96, :])
                V.tensor_copy(pay[0:96, :, 0], dsti[0:96, :])
                V.tensor_copy(srcf[96:128, 0:last], srci[96:128, 0:last])
                V.tensor_copy(pay[96:128, 0:last, 0], dsti[96:128, 0:last])
                V.tensor_copy(srcf[96:127, last:COLS], srci[96:127, last:COLS])
                step(V.tensor_copy(pay[96:127, last:COLS, 0], dsti[96:127, last:COLS]))
                step(V.tensor_scalar(cum.bitcast(I32), srcf, 0.5, 1.0 / R, ALU.add, ALU.mult))
                step(V.tensor_copy(q0, cum.bitcast(I32)))
                step(V.scalar_tensor_tensor(cmp, q0, float(R), srcf, ALU.mult, ALU.is_gt))
                step(V.tensor_tensor(blk, q0, cmp, ALU.subtract))
                step(V.scalar_tensor_tensor(pay.bitcast(F32)[:, :, 1], blk, -float(R), srcf, ALU.mult, ALU.add))
                V.memset(onesl, 1.0)
                step(V.tensor_copy(few_blks, iota_blk[:, 0:FEW]))
                with dve.Fori(0, NT // FEW) as a:
                    for j, unread in enumerate((cmp, cum, posf, q0, srcf)):
                        last = V.tensor_scalar(unread, blk, few_blks[:, j:j + 1], None, ALU.is_equal, ALU.add, accum_out=few_tots[:, j:j + 1])
                    last.then_inc(count_step, 1)
                    dve.wait_ge(count_step, a * 3 + 1)
                    hold(dve)
                    V.tensor_copy(tot[:, bass.ds(a * FEW, FEW)], few_tots).then_inc(count_step, 1)
                    V.tensor_scalar(few_blks, few_blks, float(FEW), None, ALU.add).then_inc(count_step, 1)
                    dve.wait_ge(count_step, a * 3 + 3)
                V.memset(posf, FAR)
                dve.wait_ge(prefix_done, 1)
                step(V.tensor_scalar(cnt[:, :], bank[7][:, 0:NT], float(GS - 1), None, ALU.add))
                step(V.tensor_scalar(int50[:, :], cnt[:, :], 0.5, 1.0 / GS, ALU.add, ALU.mult))
                step(V.tensor_copy(ngf[:, :], int50[:, :]))
                step(V.scalar_tensor_tensor(tmp50[:, :], ngf[:, :], float(GS), cnt[:, :], ALU.mult, ALU.is_gt))
                step(V.tensor_tensor(ngf[:, :], ngf[:, :], tmp50[:, :], ALU.subtract))
                step(V.tensor_tensor_scan(gend[:, :], onesl[:, 0:NT], ngf[:, :], 0.0, ALU.mult, ALU.add))
                step(V.tensor_tensor(tmp50[:, :], gend[:, :], ngf[:, :], ALU.subtract))
                step(V.scalar_tensor_tensor(off[:, :], tmp50[:, :], float(GS), bank[6][:, 0:NT], ALU.mult, ALU.add))
                step(V.tensor_tensor(tmp50[:, :], gend[:, :], ident[:, 0:NT], ALU.mult))
                step(V.tensor_reduce(gcol[:, :], tmp50[:, :], AX.X, ALU.add))
                V.tensor_scalar(gcmp[:, :], iota_g[:, :], gcol[0:NT, :], None, ALU.is_ge).then_inc(gcmp_ready, 1)
                dve.wait_ge(gmap_done, 1)
                V.tensor_scalar(group_block[:, :], bank[5][0:1, 0:NG], float(NT - 1), None, ALU.min)
                def scan(b, j):
                    dve.wait_ge(mask_ready, at(b, 1, 1))
                    wait(dve, placed, at(b, 1, -1))
                    V.tensor_tensor_scan(cums[j % 2], onesl, masks[j % 5], off[:, bass.ds(at(b), 1)], ALU.mult, ALU.add).then_inc(scanned, 1)

                def place(b, j):
                    dve.wait_ge(scanned, at(b, 1, 1))
                    wait(dve, placed, at(b))
                    hold(dve)
                    V.copy_predicated(posf, masks[j % 5].bitcast(I32), cums[j % 2]).then_inc(placed, 1)

                def scan_place(it, count, ahead):
                    for j in range(count):
                        if j + 1 < count or ahead:
                            scan((it, SOME, j + 1), j + 1)
                        place((it, SOME, j), j)

                scan((0, SOME, 0), 0)
                scan_place(0, SOME, True)
                with dve.Fori(1, NT // SOME - 1) as it:
                    scan_place(it, SOME, True)
                scan_place(NT // SOME - 1, SOME, False)
                dve.wait_ge(placed, NT)
                V.tensor_scalar(posi, posf, -1.0, None, ALU.add).then_inc(pos_ready, 1)

                for i in range(NC):
                    dve.wait_ge(x_in[i], 16)
                with dve.Fori(0, NT) as t:
                    V.bn_stats(sts[:, bass.ds(t, 1), :].rearrange("p a b -> p (a b)"),
                               xn[:, bass.ds(t, 1), :].rearrange("p a b -> p (a b)")).then_inc(ln_step, 1)
                dve.wait_ge(ln_step, NT)
                step(V.tensor_tensor(mvs[:, :, 0], sts[:, :, 1], sts[:, :, 4], ALU.add))
                V.tensor_tensor(mvs[:, :, 1], sts[:, :, 1], sts[:, :, 4], ALU.subtract)
                step(V.tensor_scalar(mvs[:, :, 0], mvs[:, :, 0], 0.5, None, ALU.mult))
                step(V.tensor_tensor(rstd_all[:, :], mvs[:, :, 1], mvs[:, :, 1], ALU.mult))
                step(V.tensor_scalar(rstd_all[:, :], rstd_all[:, :], D / 4.0, None, ALU.mult))
                step(V.tensor_tensor(rstd_all[:, :], rstd_all[:, :], sts[:, :, 2], ALU.add))
                step(V.tensor_tensor(rstd_all[:, :], rstd_all[:, :], sts[:, :, 5], ALU.add))
                V.tensor_scalar(mvs[:, :, 1], rstd_all[:, :], 1.0 / D, None, ALU.mult).then_inc(var_ready, 1)
                dve.wait_ge(sd_ready, 1)
                step(V.reciprocal(rstd_all[:, :], rstd_all[:, :]))
                dve.wait_ge(w_in, 16 * len(loads))

                def normalise(t, j):
                    wait(dve, p_tp, at(t, 1, -1))
                    V.tensor_scalar(xs[0:R, 0, j, :], rows(at(t)), mvs[:, bass.ds(at(t), 1), 0], rstd_all[:, bass.ds(at(t), 1)],
                                    ALU.subtract, ALU.mult).then_inc(xn_ready, 1)

                def proj(t, j):
                    prod, vb = bank[2 + j], bank[4 + j]
                    dve.wait_ge(p_wk, at(t, 1, 1))
                    wait(dve, p_kvd, at(t, 1, -1))
                    V.tensor_tensor(kb[0:R, j, :], prod[0:R, D:2 * D], bias_k[0:R, :], ALU.add).then_inc(p_kb, 1)
                    wait(dve, p_out[j], at((t[0], 1, 0), 16))
                    V.tensor_tensor(whs[0:R, j, 0:D], prod[0:R, 0:D], bias_g[0:R, :], ALU.add).then_inc(p_wh, 1)
                    V.tensor_tensor(vaug[0:R, j, :, 0:128], vb[0:R, 0:D].rearrange("p (h e) -> p h e", h=2),
                                    bias_v[0:R, :].rearrange("p (h e) -> p h e", h=2), ALU.add).then_inc(p_free, 1)
                    dve.wait_ge(p_wh, at(t, 2, 1))
                    V.tensor_tensor_reduce(scratch[0:R, :], whs[0:R, j, 0:D], a_src[0:R, :], 1.0, 0.0, ALU.mult, ALU.add,
                                           accum_out=fr_one[0:R, j:j + 1])
                    V.tensor_tensor_reduce(scratch2[0:R, :], whs[0:R, j, 0:D], a_dst[0:R, :], 1.0, 0.0, ALU.mult, ALU.add,
                                           accum_out=whs[0:R, j, D:D + 1]).then_inc(p_row, 1)
                    dve.wait_ge(p_row, at(t, 1, 1))
                    hold(dve)
                    V.tensor_copy(fd[:, bass.ds(at(t), 1)], whs[0:R, j, D:D + 1])
                    V.tensor_copy(fr[:, bass.ds(at(t), 1)], fr_one[0:R, j:j + 1]).then_inc(p_wh, 1)
                    dve.wait_ge(p_ke, at(t, 1, 1))
                    V.scalar_tensor_tensor(kb[0:R, j, :], ke[0:R, j, :], 1.0, kr[0:R, j, :], ALU.min, ALU.add).then_inc(p_kv, 1)

                for j in range(2):
                    normalise((0, 2, j), j)
                normalise((0, 2, 2), 0)
                proj((0, 2, 0), 0)
                normalise((0, 2, 3), 1)
                proj((0, 2, 1), 1)
                with dve.Fori(1, NC - 1) as it:
                    for j in range(2):
                        normalise((it, 2, j + 2), j)
                        proj((it, 2, j), j)
                for j in range(2):
                    proj((NC - 1, 2, j), j)

                dve.wait_ge(p_wh, 2 * NT)
                step(V.tensor_reduce(neg1[0:R, :], fd[:, :], AX.X, ALU.min))
                V.tensor_scalar(fdiag[0:R, 0:R], ident[0:R, 0:R], neg1[0:R, :], None, ALU.mult).then_inc(sh_diag, 1)
                dve.wait_ge(p_kvd, NT)
                for h in range(2):
                    V.tensor_tensor(kv_bd[:, h, :], bank[6 + h][:, 0:128], diag_mask, ALU.mult)
                    last_i = V.tensor_scalar(ks_bd[:, h, :], diag_mask, bank[6 + h][:, 128:129], None, ALU.mult)
                last_i.then_inc(kvb, 1)
                dve.wait_ge(sh_pe, 1)
                step(V.tensor_reduce(gcol[:, :], bank[2][:, 0:R], AX.X, ALU.min))
                step(V.tensor_scalar(shift[:, :], gcol[:, :], -1.0, 1.0, ALU.mult, ALU.add))
                step(V.tensor_scalar(fr[:, :], fr[:, :], ab[0:R, :], None, ALU.add))
                V.tensor_scalar(fr_c[:, :], fr[:, :], shift[0:R, :], None, ALU.subtract).then_inc(m_shift, 1)

            @block.scalar
            def _(act):
                A = nc.scalar
                act.wait_ge(prefilled, 16)
                for to, frm in loads:
                    act.dma_start(to, frm, allow_slow_non_contiguous=True).then_inc(w_in, 16)
                act.wait_ge(consts, 1)
                act.wait_ge(count_step, 3 * NT // FEW)

                def mask(it, h):
                    for j in range(2):
                        b = (it, SOME, h + j)
                        wait(act, mask_ready, at(b, 1, -1))
                        A.activation(dists[j % 2], blk, ACT.Abs, bias=iota_blk[:, bass.ds(at(b), 1)], scale=-1.0).then_inc(mask_dist, 1)
                    for j in range(2):
                        b = (it, SOME, h + j)
                        act.wait_ge(mask_dist, at(b, 1, 1))
                        wait(act, placed, at(b, 1, -4))
                        A.activation(masks[(h + j) % 5], dists[j % 2], ACT.Relu, bias=ones[:, 0:1], scale=-1.0).then_inc(mask_ready, 1)

                for h in range(0, SOME, 2):
                    mask(0, h)
                with act.Fori(1, NT // SOME) as it:
                    for h in range(0, SOME, 2):
                        mask(it, h)
                act.wait_ge(var_ready, 1)
                A.activation(rstd_all[:, :], mvs[:, :, 1], ACT.Sqrt, bias=eps[0:R, :]).then_inc(sd_ready, 1)

                def proj(t, j):
                    act.wait_ge(p_tp, at(t, 1, 1))
                    wait(act, p_wk, at(t, 1, -1))
                    A.copy(xnT[:, j, :, 0:R], bank[j][:, 0:2 * R].rearrange("p (k n) -> p k n", k=2)).then_inc(p_tc, 1)

                def keys(t, j):
                    act.wait_ge(p_kb, at(t, 1, 1))
                    wait(act, p_kv, at(t, 1, -1))
                    A.activation(ke[0:R, j, :], kb[0:R, j, :], ACT.Exp)
                    A.activation(kr[0:R, j, :], kb[0:R, j, :], ACT.Relu).then_inc(p_ke, 1)

                proj((0, 2, 0), 0)
                proj((0, 2, 1), 1)
                keys((0, 2, 0), 0)
                with act.Fori(1, NC) as it:
                    proj((it, 2, 0), 0)
                    keys((it, 2, -1), 1)
                    proj((it, 2, 1), 1)
                    keys((it, 2, 0), 0)
                keys((NC, 2, -1), 1)

            @block.tensor
            def _(pe):
                T = nc.tensor
                pe.wait_ge(consts, 1)
                pe.wait_ge(count_step, 3 * NT // FEW)
                T.matmul(bank[6][:, 0:NT], tri, tot[:, :], start=True, stop=True)
                T.matmul(bank[7][:, 0:NT], ones[:, :], tot[:, :], start=True, stop=True).then_inc(prefix_done, 1)
                pe.wait_ge(gcmp_ready, 1)
                T.matmul(bank[5][:, 0:NG], ones[0:NT, :], gcmp[:, :], start=True, stop=True).then_inc(gmap_done, 1)
                pe.wait_ge(pos_ready, 1)
                pe.wait_ge(w_in, 16 * len(loads))

                def transposes(t, j):
                    pe.wait_ge(xn_ready, at(t, 1, 1))
                    wait(pe, p_tc, at(t, 1, -1))
                    for k in range(2):
                        last = T.transpose(bank[j][:, k * R:(k + 1) * R],
                                           xs[0:R, 0, j, k * 128:(k + 1) * 128], ident[0:R, 0:R])
                    last.then_inc(p_tp, 1)

                def products(t, j):
                    pe.wait_ge(p_tc, at(t, 1, 1))
                    wait(pe, p_free, at(t, 1, -1))
                    for k in range(2):
                        T.matmul(bank[2 + j][0:R, :], xnT[:, j, k, 0:R], w_gk[:, k, :], start=(k == 0), stop=(k == 1))
                        last = T.matmul(bank[4 + j][0:R, 0:D], xnT[:, j, k, 0:R], w_v[:, k, :], start=(k == 0), stop=(k == 1))
                    last.then_inc(p_wk, 1)

                def kv(t, j, start, stop):
                    pe.wait_ge(p_kv, at(t, 1, 1))
                    for h in range(2):
                        last = T.matmul(bank[6 + h][:, 0:129], kb[0:R, j, h * 128:(h + 1) * 128], vaug[0:R, j, h, 0:129],
                                        start=start, stop=stop)
                    last.then_inc(p_kvd, 1)

                transposes((0, 2, 0), 0)
                transposes((0, 2, 1), 1)
                products((0, 2, 0), 0)
                products((0, 2, 1), 1)
                kv((0, 2, 0), 0, True, False)
                with pe.Fori(1, NC) as it:
                    transposes((it, 2, 0), 0)
                    kv((it, 2, -1), 1, False, False)
                    products((it, 2, 0), 0)
                    transposes((it, 2, 1), 1)
                    kv((it, 2, 0), 0, False, False)
                    products((it, 2, 1), 1)
                kv((NC, 2, -1), 1, False, True)
                pe.wait_ge(sh_diag, 1)
                pe.wait_ge(p_free, NT)
                T.matmul(bank[2][:, 0:R], ones[0:R, :], fdiag[0:R, 0:R], start=True, stop=True).then_inc(sh_pe, 1)
                pe.wait_ge(kvb, 1)


        take = carve(GRAPH)
        gath = take(5, GT, WROW)
        payr = take(5, GT, 2)
        xm = take(2, GT, RW)
        hot = take(2, GS)
        dist = take(2, GT, RW)
        sm = take(2, GT, RW)
        fdc = take(2, GT)
        gmax, gt, gl = take(2), take(2), take(2)
        gd = take(2)
        alpha = take(5)
        frm = take(2, 2)
        mrun = take(NT)
        e1, e2, e3, e4 = (take(2, GT) for _ in range(4))
        payi = payr.bitcast(I32)
        XT, QE, US = (0, 3), 1, 2
        OB, AB, HB = 4, 5, (6, 7)

        acc_zero = sem("acc_zero")
        pay_in = [sem(f"pay_in{i}") for i in range(5)]
        gathered = [sem(f"gathered{i}") for i in range(5)]
        d_fdc = sem("d_fdc")
        d_x = sem("d_x")
        p_xt = sem("p_xt")
        a_hot = sem("a_hot")
        d_m = sem("d_m")
        d_frm = sem("d_frm")
        a_alpha = sem("a_alpha")
        p_q = sem("p_q")
        d_es = sem("d_es")
        d_e = sem("d_e")
        a_dist = sem("a_dist")
        a_s = sem("a_s")
        p_main = sem("p_main")
        d_acc = sem("d_acc")

        with nc.Block() as block:
            @block.sync
            def _(sp):
                def load(s, j):
                    wait(sp, a_s, at(s, 1, -4))
                    sp.dma_start(payi[:, j % 5, :, :].rearrange("p t k -> p (t k)"),
                                 slots[bass.ds(at(s, GS), GS), :].rearrange("(p t) k -> p (t k)", t=GT)).then_inc(pay_in[j % 5], 16)
                together(sp, [(0, load)])

            @block.gpsimd
            def _(g):
                g.memset(acc_mem[:, :], 0.0).then_inc(acc_zero, 1)

                def gather(s, j):
                    g.wait_ge(pay_in[j % 5], at((s[0], 4, j // 5), 16, 16))
                    wait(g, p_main, at(s, 1, -4))
                    hold(g)
                    for t in range(GT):
                        g.indirect_dma_start(out=gath[:, j % 5, t, :], out_offset=None, in_=table,
                                             in_offset=bass.IndirectOffsetOnAxis(ap=payi[:, j % 5, t, 0:1], axis=0),
                                             bounds_check=N - 1, oob_is_err=False).then_inc(gathered[j % 5], 16)
                together(g, [(0, gather)])

            @block.vector
            def _(dve):
                V = nc.vector
                V.memset(mrun[0:R, :], -1.0e30).then_inc(acc_zero, 1)
                dve.wait_ge(acc_zero, 2)

                blocks = [dve.alloc_register(f"block{i}") for i in range(4)]

                def block_of(j):
                    return dve.snap(blocks[j % 4], min_val=0, max_val=NT - 1)

                def shifted(s, j):
                    b = j % 2
                    dve.wait_ge(gathered[j % 5], at((s[0], 4, j // 5), 16 * GT, 16 * GT))
                    wait(dve, p_xt, at(s, 1, -1))
                    V.tensor_scalar(fdc[:, b, :], gath[:, j % 5, :, D], shift[:, :], None, ALU.add).then_inc(d_fdc, 1)

                def mark(t):
                    def stage(s, j):
                        b = j % 2
                        dve.wait_ge(d_fdc, at(s, 1, 1))
                        ins = V.tensor_scalar(xm[:, b, t, :], iota_row[:, :], payr[:, j % 5, t, 1:2], fdc[:, b, t:t + 1],
                                              ALU.is_equal, ALU.mult)
                        if t == GT - 1:
                            ins.then_inc(d_x, 1)
                    return stage

                def group_peak(s, j):
                    b = j % 2
                    dve.wait_ge(p_xt, at(s, 1, 1))
                    V.tensor_reduce(gmax[0:R, b:b + 1], bank[XT[j % 2]][0:R, :], AX.X, ALU.max).then_inc(d_m, 1)
                    dve.reg_load(blocks[j % 4], group_block[0:1, bass.ds(at(s), 1)])
                    r = block_of(j)
                    wait(dve, p_q, at(s, 1, -1))
                    hold(dve)
                    V.tensor_copy(frm[0:R, b, 0:1], fr[:, bass.ds(r, 1)])

                def row_score(s, j):
                    b = j % 2
                    r = block_of(j)
                    dve.wait_ge(d_m, at(s, 5, 1))
                    V.tensor_tensor(gt[0:R, b:b + 1], gmax[0:R, b:b + 1], fr_c[:, bass.ds(r, 1)], ALU.add).then_inc(d_m, 1)

                def row_leaky(s, j):
                    b = j % 2
                    dve.wait_ge(d_m, at(s, 5, 2))
                    V.scalar_tensor_tensor(gl[0:R, b:b + 1], gt[0:R, b:b + 1], 0.2, gt[0:R, b:b + 1], ALU.mult, ALU.max).then_inc(d_m, 1)

                def new_max(s, j):
                    b = j % 2
                    r = block_of(j)
                    dve.wait_ge(d_m, at(s, 5, 3))
                    wait(dve, d_frm, at(s))
                    V.tensor_tensor(frm[0:R, b, 1:2], gl[0:R, b:b + 1], mrun[0:R, bass.ds(r, 1)], ALU.max).then_inc(d_m, 1)

                def old_less_new(s, j):
                    b = j % 2
                    r = block_of(j)
                    dve.wait_ge(d_m, at(s, 5, 4))
                    wait(dve, a_alpha, at(s, 1, -1))
                    V.tensor_tensor(gd[0:R, b:b + 1], mrun[0:R, bass.ds(r, 1)], frm[0:R, b, 1:2], ALU.subtract).then_inc(d_m, 1)

                def keep_max(s, j):
                    b = j % 2
                    r = block_of(j)
                    dve.wait_ge(d_m, at(s, 5, 5))
                    hold(dve)
                    V.tensor_copy(mrun[0:R, bass.ds(r, 1)], frm[0:R, b, 1:2]).then_inc(d_frm, 1)

                def score_sum(s, j):
                    b = j % 2
                    dve.wait_ge(p_q, at(s, 1, 1))
                    pair = bank[QE][:, 0:2 * GT].rearrange("p (t k) -> p t k", k=2)
                    V.tensor_tensor(e1[:, b, :], gath[:, j % 5, :, D], pair[:, :, 0], ALU.add).then_inc(d_es, 1)

                def score_leaky(s, j):
                    b = j % 2
                    dve.wait_ge(d_es, at(s, 3, 1))
                    V.scalar_tensor_tensor(e2[:, b, :], e1[:, b, :], 0.2, e1[:, b, :], ALU.mult, ALU.max).then_inc(d_es, 1)

                def score_less_max(s, j):
                    b = j % 2
                    pair = bank[QE][:, 0:2 * GT].rearrange("p (t k) -> p t k", k=2)
                    dve.wait_ge(d_es, at(s, 3, 2))
                    V.tensor_tensor(e3[:, b, :], e2[:, b, :], pair[:, :, 1], ALU.subtract).then_inc(d_es, 1)

                def score_bound(s, j):
                    b = j % 2
                    dve.wait_ge(d_es, at(s, 3, 3))
                    wait(dve, a_s, at(s, 1, -1))
                    V.tensor_scalar(e4[:, b, :], e3[:, b, :], 60.0, None, ALU.min).then_inc(d_e, 1)

                def gather_up(s, j):
                    b = j % 2
                    r = block_of(j)
                    dve.wait_ge(a_alpha, at(s, 1, 1))
                    dve.wait_ge(p_main, at(s, 1, 1))
                    wait(dve, d_acc, at(s))
                    row = acc[:, bass.ds(r, 1), :].rearrange("p a b -> p (a b)")
                    V.scalar_tensor_tensor(row, row, alpha[0:R, j % 5:j % 5 + 1], bank[US][0:R, 0:WROW], ALU.mult, ALU.add).then_inc(d_acc, 1)

                def norm_in(c, k, bias):
                    mine = m_ln[k]
                    dve.wait_ge(mine, at(c, 4, 1))
                    V.tensor_tensor(y1[0:R, k, :, :], y1[0:R, k, :, :], bias[0:R, :].unsqueeze(1).to_broadcast([R, 2, D]), ALU.add).then_inc(mine, 1)
                    dve.wait_ge(mine, at(c, 4, 2))
                    for r in range(2):
                        last_s = V.bn_stats(stats[0:R, k, r, :], y1[0:R, k, r, :])
                    last_s.then_inc(mine, 1)
                    dve.wait_ge(mine, at(c, 4, 3))
                    hold(dve)
                    for r in range(2):
                        last_s = V.bn_aggr(mv[0:R, k, r, :], stats[0:R, k, r, :])
                    last_s.then_inc(m_va[k], 1)

                def norm_out(c, k, dst_of, gam, bet):
                    mine = m_ln[k]
                    dve.wait_ge(m_va[k], at(c, 1, 1))
                    for r in range(2):
                        last_s = V.scalar_tensor_tensor(y1[0:R, k, r, :], y1[0:R, k, r, :], mv[0:R, k, r, 0:1], gam[0:R, :],
                                                        ALU.subtract, ALU.mult)
                    last_s.then_inc(mine, 1)
                    dve.wait_ge(mine, at(c, 4, 4))
                    dve.wait_ge(m_rs[k], at(c, 1, 1))
                    for r in range(2):
                        last_s = V.scalar_tensor_tensor(dst_of[:, r, :], y1[0:R, k, r, :], rs[0:R, k, r:r + 1], bet[0:R, :],
                                                        ALU.mult, ALU.add)
                    return last_s

                def phi(c):
                    dve.wait_ge(m_qa, at(c, 1, 1))
                    V.scalar_tensor_tensor(phiq, qe, 1.0, qr, ALU.min, ALU.add).then_inc(m_phi, 1)

                def divide(c):
                    dve.wait_ge(m_nd, at(c, 1, 1))
                    dve.wait_ge(m_den, at(c, 1, 1))
                    V.reciprocal(att, den_s).then_inc(m_rec, 1)
                    dve.wait_ge(m_rec, at(c, 1, 1))
                    V.tensor_tensor(att, att, bank[AB][:, 0:2 * CH].rearrange("p (m n) -> p m n", m=2), ALU.mult).then_inc(m_att, 1)

                def attend_sum(c, j):
                    dve.wait_ge(m_o, at(c, 1, 1))
                    wait(dve, m_x1, at(c))
                    V.tensor_tensor(y1[0:R, 0, :, :], bank[OB][0:R, :].rearrange("p (t d) -> p t d", t=2),
                                    xs[0:R, j, :, :], ALU.add).then_inc(m_ln[0], 1)
                    norm_in(c, 0, bias_o)

                def attend_norm(c, j):
                    norm_out(c, 0, x1[0:R, j, :, :], g1, be1).then_inc(m_x1, 1)

                def feed_sum(c, j):
                    dve.wait_ge(m_ff, at(c, 1, 1))
                    wait(dve, m_x, at(c))
                    V.tensor_tensor(y1[0:R, 1, :, :], bank[AB][0:R, :].rearrange("p (t d) -> p t d", t=2), x1[0:R, j, :, :],
                                    ALU.add).then_inc(m_ln[1], 1)
                    norm_in(c, 1, bias_2)

                def feed_norm(c, j):
                    norm_out(c, 1, y1[0:R, 1, :, :], g2, be2).then_inc(m_y, 1)
                    dve.wait_ge(m_y, at(c, 1, 1))
                    both_rows = xn[:, bass.ds(at(c, 2), 2), :]
                    V.tensor_tensor(both_rows, both_rows, y1[0:R, 1, :, :], ALU.add).then_inc(m_x, 1)

                def prepare(c, j):
                    for r in range(2):
                        t = at(c, 2, r)
                        last_p = V.tensor_scalar(xs[0:R, j, r, :], rows(t), mvs[:, bass.ds(t, 1), 0], rstd_all[:, bass.ds(t, 1)],
                                                 ALU.subtract, ALU.mult)
                    last_p.then_inc(m_xs, 1)

                def mixer(slot, c, j, more):
                    b, d, e = ((c[0], 2, c[2] + i) for i in (-1, 1, 2))
                    before = not isinstance(c[0], int) or at(c) > 0
                    attends = more is not None
                    if slot == 0 and before:
                        feed_sum(b, 1 - j)
                    if slot == 2 and before:
                        feed_norm(b, 1 - j)
                    if slot == 4 and attends:
                        phi(d)
                    if slot == 6 and attends:
                        divide(d)
                    if slot == 7 and more:
                        prepare(e, j)
                    if slot == 8 and attends:
                        attend_sum(d, 1 - j)
                    if slot == 9 and attends:
                        attend_norm(d, 1 - j)
                    if slot == 9 and not attends:
                        feed_sum(c, j)
                        feed_norm(c, j)

                prepare((0, 2, 0), 0)
                together(dve, [(1, group_peak), (0, shifted), (2, score_sum), (1, row_score), (0, mark(0)), (2, score_leaky),
                               (1, row_leaky), (0, mark(1)), (2, score_less_max), (1, new_max), (0, mark(2)), (2, score_bound),
                               (1, old_less_new), (0, mark(3)), (1, keep_max), (3, gather_up)], mixer)

            @block.scalar
            def _(act):
                A = nc.scalar
                A.preload_act_table_set("natural_log_exp_and_others")

                def spread(s, j):
                    b = j % 2
                    act.wait_ge(d_m, at(s, 5, 1))
                    wait(act, p_q, at(s, 1, -1))
                    A.activation(hot[0:R, b, :], bank[XT[j % 2]][0:R, :], ACT.Sign).then_inc(a_hot, 1)

                def rescale(s, j):
                    b = j % 2
                    act.wait_ge(d_m, at(s, 5, 5))
                    wait(act, d_acc, at(s, 1, -4))
                    A.activation(alpha[0:R, j % 5:j % 5 + 1], gd[0:R, b:b + 1], ACT.Exp).then_inc(a_alpha, 1)

                def apart(s, j):
                    b = j % 2
                    act.wait_ge(d_x, at(s, 1, 1))
                    wait(act, a_s, at(s, 1, -1))
                    for t in range(GT):
                        last = A.activation(dist[:, b, t, :], iota_row[:, :], ACT.Abs, bias=payr[:, j % 5, t, 1:2], scale=-1.0)
                    last.then_inc(a_dist, 1)

                def weigh(s, j):
                    b = j % 2
                    act.wait_ge(a_dist, at(s, 1, 1))
                    act.wait_ge(d_e, at(s, 1, 1))
                    wait(act, p_main, at(s, 1, -1))
                    for t in range(GT):
                        last = A.activation(sm[:, b, t, :], dist[:, b, t, :], ACT.Exp, bias=e4[:, b, t:t + 1], scale=-10000.0)
                    last.then_inc(a_s, 1)

                def attend_in(c, j):
                    act.wait_ge(m_xt, at(c, 1, 1))
                    wait(act, m_q, at(c, 1, -1))
                    A.copy(xnT[:, j, :, :], bank[OB][:, 0:2 * CH].rearrange("p (k n) -> p k n", k=2)).then_inc(m_xc, 1)

                def attend_q(c, j):
                    act.wait_ge(m_q, at(c, 1, 1))
                    wait(act, m_phi, at(c))
                    wait(act, m_att, at(c))
                    for m in range(2):
                        A.activation(qe[:, m, :], bank[AB][:, m * CH:(m + 1) * CH], ACT.Exp, bias=bias_q[:, m:m + 1])
                    for m in range(2):
                        last = A.activation(qr[:, m, :], bank[AB][:, m * CH:(m + 1) * CH], ACT.Relu, bias=bias_q[:, m:m + 1])
                    last.then_inc(m_qa, 1)

                def root(c, k):
                    act.wait_ge(m_va[k], at(c, 1, 1))
                    wait(act, m_x1 if k == 0 else m_y, at(c))
                    A.activation(lv[0:R, k, :], mv[0:R, k, :, 1], ACT.Ln, bias=eps[0:R, :]).then_inc(m_lv[k], 1)
                    act.wait_ge(m_lv[k], at(c, 1, 1))
                    A.activation(rs[0:R, k, :], lv[0:R, k, :], ACT.Exp, scale=-0.5).then_inc(m_rs[k], 1)

                def denominators(c):
                    act.wait_ge(m_nd, at(c, 1, 1))
                    wait(act, m_att, at(c))
                    A.activation(den_s, bank[HB[1]][:, 0:2 * CH].rearrange("p (m n) -> p m n", m=2), ACT.Identity,
                                 bias=small[:, :]).then_inc(m_den, 1)

                def feed_in(c, j):
                    act.wait_ge(m_t1, at(c, 1, 1))
                    wait(act, m_h, at(c, 4))
                    A.copy(x1T, bank[HB[0]][:, 0:2 * CH].rearrange("p (k n) -> p k n", k=2)).then_inc(m_tc1, 1)

                def hidden(c, p):
                    act.wait_ge(m_h, at(c, 4, p + 1))
                    wait(act, m_ff, at(c))
                    for i in range(2):
                        f = 2 * p + i
                        last = A.activation(hT[:, f, :], bank[HB[p % 2]][:, i * CH:(i + 1) * CH], ACT.Relu, bias=bias_1[:, f:f + 1])
                    last.then_inc(m_hc, 1)

                def mixer(slot, c, j, more):
                    d = (c[0], 2, c[2] + 1)
                    now = not isinstance(c[0], int) or at(c) >= 0
                    attends = more is not None
                    if slot == 1:
                        if now:
                            feed_in(c, j)
                        if attends:
                            attend_in(d, 1 - j)
                    if slot == 3 and attends:
                        attend_q(d, 1 - j)
                    if slot in (3, 4, 5, 8) and now:
                        hidden(c, (3, 4, 5, 8).index(slot))
                    if slot == 5 and attends:
                        denominators(d)

                def roots(slot, c, j, more):
                    b, d = ((c[0], 2, c[2] + i) for i in (-1, 1))
                    if slot == 1 and (not isinstance(c[0], int) or at(c) > 0):
                        root(b, 1)
                    if slot == 9 and more is not None:
                        root(d, 0)

                together(act, roots, [(1, spread), (1, apart), (2, rescale), (2, weigh)], mixer)
                root((NC // 2, 2, 0), 1)

            @block.tensor
            def _(pe):
                T = nc.tensor

                def turn(s, j):
                    b = j % 2
                    pe.wait_ge(d_x, at(s, 1, 1))
                    wait(pe, a_hot, at(s, 1, -1))
                    for t in range(GT):
                        last = T.transpose(bank[XT[j % 2]][0:RW, t * L:(t + 1) * L], xm[:, b, t, :], ident[:, :])
                    last.then_inc(p_xt, 1)

                def fetch(s, j):
                    b = j % 2
                    pe.wait_ge(a_hot, at(s, 1, 1))
                    pe.wait_ge(d_frm, at(s, 1, 1))
                    wait(pe, d_e, at(s))
                    for t in range(GT):
                        last = T.matmul(bank[QE][:, 2 * t:2 * t + 2], hot[0:R, b, t * L:(t + 1) * L], frm[0:R, b, :],
                                        start=True, stop=True)
                    last.then_inc(p_q, 1)

                def total(s, j):
                    b = j % 2
                    pe.wait_ge(a_s, at(s, 1, 1))
                    wait(pe, d_acc, at(s))
                    for t in range(GT):
                        last = T.matmul(bank[US][0:RW, 0:WROW], sm[:, b, t, :], gath[:, j % 5, t, :], start=(t == 0), stop=(t == GT - 1))
                    last.then_inc(p_main, 1)

                def xt(c, j):
                    pe.wait_ge(m_xs, at(c, 1, 1))
                    wait(pe, m_x1, at(c))
                    for k in range(2):
                        for r in range(2):
                            last = T.transpose(bank[OB][:, k * CH + r * R:k * CH + (r + 1) * R],
                                               xs[0:R, j, r, k * 128:(k + 1) * 128],
                                               ident[0:R, 0:R])
                    last.then_inc(m_xt, 1)

                def q(c, j):
                    pe.wait_ge(m_xc, at(c, 1, 1))
                    wait(pe, m_ln[1], at(c, 4, -7))
                    for m in range(2):
                        for k in range(2):
                            last = T.matmul(bank[AB][:, m * CH:(m + 1) * CH], w_q[:, k, m * 128:(m + 1) * 128], xnT[:, j, k, :],
                                            start=(k == 0), stop=(k == 1))
                    last.then_inc(m_q, 1)

                def numden(c):
                    pe.wait_ge(m_phi, at(c, 1, 1))
                    wait(pe, m_hc, at(c, 4, -2))
                    for m in range(2):
                        T.matmul(bank[AB][:, m * CH:(m + 1) * CH], kv_bd[:, m, :], phiq[:, m, :], start=True, stop=True)
                        last = T.matmul(bank[HB[1]][:, m * CH:(m + 1) * CH], ks_bd[:, m, :], phiq[:, m, :], start=True, stop=True)
                    last.then_inc(m_nd, 1)

                def o(c):
                    pe.wait_ge(m_att, at(c, 1, 1))
                    pe.wait_ge(m_xc, at(c, 1, 1))
                    for r in range(2):
                        for m in range(2):
                            last = T.matmul(bank[OB][0:R, r * D:(r + 1) * D], att[:, m, r * R:(r + 1) * R], w_o[:, m, :],
                                            start=(m == 0), stop=(m == 1))
                    last.then_inc(m_o, 1)

                def t1(c, j):
                    pe.wait_ge(m_x1, at(c, 1, 1))
                    wait(pe, m_hc, at(c, 4, -1))
                    for k in range(2):
                        for r in range(2):
                            last = T.transpose(bank[HB[0]][:, k * CH + r * R:k * CH + (r + 1) * R],
                                               x1[0:R, j, r, k * 128:(k + 1) * 128], ident[0:R, 0:R])
                    last.then_inc(m_t1, 1)

                def hidden(c, p, last_chunk):
                    if p == 0:
                        pe.wait_ge(m_tc1, at(c, 1, 1))
                    wait(pe, m_hc, at(c, 4, p - 1))
                    if p == 3:
                        pe.wait_ge(m_den, at(c, 1, 1 if last_chunk else 2))
                    for i in range(2):
                        for k in range(2):
                            f = 2 * p + i
                            last = T.matmul(bank[HB[p % 2]][:, i * CH:(i + 1) * CH], w_1[:, k, f * 128:(f + 1) * 128], x1T[:, k, :],
                                            start=(k == 0), stop=(k == 1))
                    last.then_inc(m_h, 1)

                def ff(c, r):
                    pe.wait_ge(m_hc, at(c, 4, 3))
                    for f in range(8):
                        if f == 6:
                            pe.wait_ge(m_hc, at(c, 4, 4))
                        last = T.matmul(bank[AB][0:R, r * D:(r + 1) * D], hT[:, f, r * R:(r + 1) * R], w_2[:, f, :],
                                        start=(f == 0), stop=(f == 7))
                    if r == 1:
                        last.then_inc(m_ff, 1)

                def mixer(slot, c, j, more):
                    d = (c[0], 2, c[2] + 1)
                    now = not isinstance(c[0], int) or at(c) >= 0
                    attends = more is not None
                    if slot == 0 and now:
                        t1(c, j)
                    if slot == 0 and attends:
                        xt(d, 1 - j)
                    if slot == 2 and attends:
                        q(d, 1 - j)
                    if slot in (2, 3, 4, 7) and now:
                        hidden(c, (2, 3, 4, 7).index(slot), not attends)
                    if slot == 5 and attends:
                        numden(d)
                    if slot == 7 and attends:
                        o(d)
                    if slot in (8, 9) and now:
                        ff(c, slot - 8)

                together(pe, [(3, total)], mixer, [(0, turn), (1, fetch)])

        take = carve(0)
        w_x1, w_x2, w_x3 = (take(2 * NX, D) for _ in range(3))
        w_r1 = take(2, RH)
        w_r2 = take(NX)
        b_x1, b_x2 = take(2 * NX), take(2 * NX)
        b_r1 = take(1)
        b_r2 = take(NX)
        b_x3 = take(D)
        rec = take(NT)
        den = take(NT)
        x2 = take(2, 2, D)
        feat = take(2, D)
        featT = take(2, 2, CH)
        rh = take(CH)
        lg, lm, pe_ = take(2, NX), take(2, NX), take(2, NX)
        prob = take(2, 8)
        top = take(2, 8)
        topi = take(2, 8).bitcast(U32)
        topf = take(2, 2)
        mx, sm2, dd, ee, dn, w_a, w_b = (take(2) for _ in range(7))
        ca, cb = take(2, NX), take(2, NX)
        cw = take(2, 2, NX)
        cT = take(CH)
        h1 = take(2, 2, CH)
        h2 = take(2, 2, CH)
        res = take(2, 2, D)
        st3, mv3 = take(2, 6), take(2, 2)
        lv3, rs3 = take(2), take(2)

        w3_in = sem("w3_in")
        z3 = sem("z3")
        f_st = sem("f_st")
        f_va = sem("f_va")
        f_lv = sem("f_lv")
        f_rs = sem("f_rs")
        f_rdy = sem("f_rdy")
        t_ft = sem("t_ft")
        c_ft = sem("c_ft")
        t_r = sem("t_r")
        c_rh = sem("c_rh")
        t_lg = sem("t_lg")
        k_st = sem("k_st")
        k_lm = sem("k_lm")
        c_pe = sem("c_pe")
        k_dd = sem("k_dd")
        c_ee = sem("c_ee")
        k_cs = sem("k_cs")
        k_cw = sem("k_cw")
        t_ct = sem("t_ct")
        c_ct = sem("c_ct")
        t_b3 = sem("t_b3")
        k_base = sem("k_base")
        t_h1 = sem("t_h1")
        c_h1 = sem("c_h1")
        t_h2 = sem("t_h2")
        c_h2 = sem("c_h2")
        t_o = sem("t_o")
        k_o = sem("k_o")
        out_sem = [sem(f"out_sem{i}") for i in range(2)]
        loads3 = [
            (w_x1, ew1.rearrange("e (k p) n -> p (e k) n", p=128)), (w_x2, ew2.rearrange("e (k p) n -> p (e k) n", p=128)),
            (w_x3, ew3.rearrange("e (k p) n -> p (e k) n", p=128)), (w_r1, rw1.rearrange("(k p) n -> p k n", p=128)),
            (w_r2, rw2), (b_x1, eb1.rearrange("e (m p) -> p (e m)", p=128)), (b_x2, eb2.rearrange("e (m p) -> p (e m)", p=128)),
            (b_r1, rb1.rearrange("(p a) -> p a", a=1)), (b_r2, rb2.partition_broadcast(128)), (b_x3[0:NX, :], eb3),
        ]

        def chunks(eng, before, body, drain):
            before()
            body((0, 2, 0), 0)
            body((0, 2, 1), 1)
            with eng.Fori(1, NC // 2) as it:
                body((it, 2, 0), 0)
                body((it, 2, 1), 1)
            drain((NC // 2, 2, 0), 0)

        with nc.Block() as block:
            @block.sync
            def _(sp):
                def store(c, j):
                    sp.wait_ge(k_o, at(c, NX, NX))
                    sp.dma_start(out[bass.ds(at(c, CH), CH), :].rearrange("(t p) d -> p t d", p=R), res[0:R, j, :, :]).then_inc(out_sem[j], 16)

                chunks(sp, lambda: None, store, store)
                sp.wait_ge(out_sem[0], 16 * (NC // 2 + 1))
                sp.wait_ge(out_sem[1], 16 * (NC // 2))

            @block.vector
            def _(dve):
                V = nc.vector
                V.tensor_scalar(den[0:R, :], acc[:, :, WROW - 1], 0.0, None, ALU.is_equal).then_inc(z3, 1)
                V.memset(prob, -1.0)
                dve.wait_ge(z3, 1)
                V.tensor_tensor(rec[0:R, :], den[0:R, :], acc[:, :, WROW - 1], ALU.add).then_inc(z3, 1)
                dve.wait_ge(z3, 2)
                V.reciprocal(rec[0:R, :], rec[0:R, :]).then_inc(z3, 1)
                dve.wait_ge(z3, 3)
                dve.wait_ge(w3_in, 16 * len(loads3))

                def features(c, j):
                    wait(dve, k_base, at(c, 1, -1))
                    for r in range(2):
                        last = V.tensor_scalar(x2[0:R, j, r, :], acc[:, bass.ds(at(c, 2, r), 1), 0:D].rearrange("p a b -> p (a b)"),
                                               rec[0:R, bass.ds(at(c, 2, r), 1)], 0.0, ALU.mult, ALU.max)
                    last.then_inc(f_st, 1)
                    dve.wait_ge(f_st, at(c, 3, 1))
                    V.tensor_tensor(x2[0:R, j, :, :], x2[0:R, j, :, :], xn[:, bass.ds(at(c, 2), 2), :], ALU.add).then_inc(f_st, 1)
                    dve.wait_ge(f_st, at(c, 3, 2))
                    for r in range(2):
                        last = V.bn_stats(st3[0:R, r, :], x2[0:R, j, r, :])
                    last.then_inc(f_st, 1)
                    dve.wait_ge(f_st, at(c, 3, 3))
                    hold(dve)
                    for r in range(2):
                        last = V.bn_aggr(mv3[0:R, r, :], st3[0:R, r, :])
                    last.then_inc(f_va, 1)
                    dve.wait_ge(f_rs, at(c, 1, 1))
                    wait(dve, t_ft, at(c))
                    for r in range(2):
                        last = V.tensor_scalar(feat[0:R, r, :], x2[0:R, j, r, :], mv3[0:R, r, 0:1], rs3[0:R, r:r + 1],
                                               ALU.subtract, ALU.mult)
                    last.then_inc(f_rdy, 1)

                def route(c, j):
                    k = [0]

                    def step(ins):
                        k[0] += 1
                        ins.then_inc(k_st, 1)
                        dve.wait_ge(k_st, at(c, 11, k[0]))
                        hold(dve)

                    dve.wait_ge(t_lg, at(c, 1, 1))
                    step(V.tensor_tensor(lg[0:R, :, :], bank[7][0:R, 256:256 + 2 * NX].rearrange("p (t e) -> p t e", t=2),
                                         b_r2[0:R, :].unsqueeze(1).to_broadcast([R, 2, NX]), ALU.add))
                    step(V.tensor_reduce(mx[0:R, :], lg[0:R, :, :], AX.X, ALU.max))
                    V.tensor_tensor(lm[0:R, :, :], lg[0:R, :, :], mx[0:R, :].unsqueeze(2).to_broadcast([R, 2, NX]), ALU.subtract).then_inc(k_lm, 1)
                    dve.wait_ge(c_pe, at(c, 1, 1))
                    step(V.tensor_reduce(sm2[0:R, :], pe_[0:R, :, :], AX.X, ALU.add))
                    step(V.reciprocal(sm2[0:R, :], sm2[0:R, :]))
                    step(V.tensor_tensor(prob[0:R, :, 0:NX], pe_[0:R, :, :], sm2[0:R, :].unsqueeze(2).to_broadcast([R, 2, NX]), ALU.mult))
                    for r in range(2):
                        last = V.max(top[0:R, r, :], prob[0:R, r, :])
                    step(last)
                    for r in range(2):
                        last = V.max_index(topi[0:R, r, :], top[0:R, r, :], prob[0:R, r, :])
                    step(last)
                    V.tensor_tensor(dd[0:R, :], top[0:R, :, 1], top[0:R, :, 0], ALU.subtract).then_inc(k_dd, 1)
                    step(V.tensor_copy(topf[0:R, :, :], topi[0:R, :, 0:2]))
                    dve.wait_ge(c_ee, at(c, 1, 1))
                    step(V.tensor_scalar(dn[0:R, :], ee[0:R, :], 1.0, None, ALU.add))
                    step(V.reciprocal(w_a[0:R, :], dn[0:R, :]))
                    step(V.tensor_tensor(w_b[0:R, :], w_a[0:R, :], ee[0:R, :], ALU.mult))
                    assert k[0] == 11
                    for r in range(2):
                        V.tensor_scalar(ca[0:R, r, :], iota8[0:R, 0:NX], topf[0:R, r, 0:1], w_a[0:R, r:r + 1], ALU.is_equal, ALU.mult)
                        last = V.tensor_scalar(cb[0:R, r, :], iota8[0:R, 0:NX], topf[0:R, r, 1:2], w_b[0:R, r:r + 1], ALU.is_equal, ALU.mult)
                    last.then_inc(k_cs, 1)
                    dve.wait_ge(k_cs, at(c, 1, 1))
                    V.tensor_tensor(cw[0:R, j, :, :], ca[0:R, :, :], cb[0:R, :, :], ALU.add).then_inc(k_cw, 1)

                def base(c, j):
                    dve.wait_ge(t_b3, at(c, 1, 1))
                    wait(dve, out_sem[j], at((c[0], 1, 0), 16))
                    V.tensor_tensor(res[0:R, j, :, :], x2[0:R, j, :, :], bank[6][0:R, :].rearrange("p (t d) -> p t d", t=2), ALU.add).then_inc(k_base, 1)
                    dve.wait_ge(k_base, at(c, 1, 1))
                    dve.wait_ge(k_cw, at(c, 1, 1))

                def add(c, j, e):
                    dve.wait_ge(t_o, at(c, NX, e + 1))
                    wait(dve, k_o, at(c, NX, e))
                    for r in range(2):
                        last = V.scalar_tensor_tensor(res[0:R, j, r, :], bank[4 + e % 2][0:R, r * D:(r + 1) * D], cw[0:R, j, r, e:e + 1],
                                                      res[0:R, j, r, :], ALU.mult, ALU.add)
                    last.then_inc(k_o, 1)

                def before():
                    features((0, 2, 0), 0)
                    route((0, 2, 0), 0)

                def body(c, j, more=True):
                    base(c, j)
                    for e in range(3):
                        add(c, j, e)
                    if more:
                        features((c[0], 2, j + 1), 1 - j)
                    for e in range(3, NX):
                        add(c, j, e)
                    if more:
                        route((c[0], 2, j + 1), 1 - j)
                chunks(dve, before, body, lambda c, j: body(c, j, False))

            @block.scalar
            def _(act):
                A = nc.scalar
                A.preload_act_table_set("natural_log_exp_and_others")
                for to, frm_ in loads3:
                    act.dma_start(to, frm_, allow_slow_non_contiguous=True).then_inc(w3_in, 16)
                act.wait_ge(w3_in, 16 * len(loads3))

                def relu2(src_bank, to, bias, e, done):
                    for m in range(2):
                        last = A.activation(to[:, m, :], src_bank[:, m * CH:(m + 1) * CH], ACT.Relu, bias=bias[:, 2 * e + m:2 * e + m + 1])
                    last.then_inc(done, 1)

                def up(c, e):
                    act.wait_ge(t_h1, at(c, NX, e + 1))
                    wait(act, t_h2, at(c, NX, e - 1))
                    relu2(bank[e % 2], h1[:, e % 2, :, :], b_x1, e, c_h1)

                def mid(c, e):
                    act.wait_ge(t_h2, at(c, NX, e + 1))
                    wait(act, t_o, at(c, NX, e - 1))
                    relu2(bank[2 + e % 2], h2[:, e % 2, :, :], b_x2, e, c_h2)

                def root(c):
                    act.wait_ge(f_va, at(c, 1, 1))
                    wait(act, f_rdy, at(c))
                    A.activation(lv3[0:R, :], mv3[0:R, :, 1], ACT.Ln, bias=eps[0:R, :]).then_inc(f_lv, 1)
                    act.wait_ge(f_lv, at(c, 1, 1))
                    A.activation(rs3[0:R, :], lv3[0:R, :], ACT.Exp, scale=-0.5).then_inc(f_rs, 1)

                def ft(c, j):
                    act.wait_ge(t_ft, at(c, 1, 1))
                    wait(act, t_h1, at(c, NX, -NX))
                    A.copy(featT[:, j, :, :], bank[6][:, 0:2 * CH].rearrange("p (k n) -> p k n", k=2)).then_inc(c_ft, 1)

                def rhid(c):
                    act.wait_ge(t_r, at(c, 1, 1))
                    wait(act, t_lg, at(c))
                    A.activation(rh, bank[7][:, 0:CH], ACT.Relu, bias=b_r1).then_inc(c_rh, 1)

                def exps(c):
                    act.wait_ge(k_lm, at(c, 1, 1))
                    A.activation(pe_[0:R, :, :], lm[0:R, :, :], ACT.Exp).then_inc(c_pe, 1)
                    act.wait_ge(k_dd, at(c, 1, 1))
                    A.activation(ee[0:R, :], dd[0:R, :], ACT.Exp).then_inc(c_ee, 1)

                def ct(c):
                    act.wait_ge(t_ct, at(c, 1, 1))
                    wait(act, t_b3, at(c))
                    A.copy(cT[0:NX, :], bank[7][0:NX, 0:CH]).then_inc(c_ct, 1)

                def before():
                    root((0, 2, 0))
                    ft((0, 2, 0), 0)
                    rhid((0, 2, 0))
                    exps((0, 2, 0))

                def body(c, j, more=True):
                    d = (c[0], 2, j + 1)
                    up(c, 0)
                    up(c, 1)
                    mid(c, 0)
                    up(c, 2)
                    mid(c, 1)
                    ct(c)
                    up(c, 3)
                    mid(c, 2)
                    up(c, 4)
                    mid(c, 3)
                    if more:
                        root(d)
                    up(c, 5)
                    mid(c, 4)
                    if more:
                        ft(d, 1 - j)
                    mid(c, 5)
                    if more:
                        rhid(d)
                        exps(d)
                chunks(act, before, body, lambda c, j: body(c, j, False))

            @block.tensor
            def _(pe):
                T = nc.tensor
                pe.wait_ge(w3_in, 16 * len(loads3))

                def tf(c):
                    pe.wait_ge(f_rdy, at(c, 1, 1))
                    wait(pe, k_base, at(c))
                    for k in range(2):
                        for r in range(2):
                            last = T.transpose(bank[6][:, k * CH + r * R:k * CH + (r + 1) * R], feat[0:R, r, k * 128:(k + 1) * 128], ident[0:R, 0:R])
                    last.then_inc(t_ft, 1)

                def router(c, j):
                    pe.wait_ge(c_ft, at(c, 1, 1))
                    wait(pe, c_ct, at(c))
                    for k in range(2):
                        last = T.matmul(bank[7][:, 0:CH], w_r1[:, k, :], featT[:, j, k, :], start=(k == 0), stop=(k == 1))
                    last.then_inc(t_r, 1)

                def logits(c):
                    pe.wait_ge(c_rh, at(c, 1, 1))
                    for r in range(2):
                        last = T.matmul(bank[7][0:R, 256 + r * NX:256 + (r + 1) * NX], rh[:, r * R:(r + 1) * R], w_r2, start=True, stop=True)
                    last.then_inc(t_lg, 1)

                def bias3(c, j):
                    pe.wait_ge(k_cw, at(c, 1, 1))
                    for r in range(2):
                        last = T.transpose(bank[7][0:NX, r * R:(r + 1) * R], cw[0:R, j, r, :], ident[0:R, 0:R])
                    last.then_inc(t_ct, 1)

                def bias3b(c):
                    pe.wait_ge(c_ct, at(c, 1, 1))
                    for r in range(2):
                        last = T.matmul(bank[6][0:R, r * D:(r + 1) * D], cT[0:NX, r * R:(r + 1) * R], b_x3[0:NX, :], start=True, stop=True)
                    last.then_inc(t_b3, 1)

                def up(c, j, e):
                    wait(pe, c_h1, at(c, NX, e - 1))
                    for m in range(2):
                        for k in range(2):
                            last = T.matmul(bank[e % 2][:, m * CH:(m + 1) * CH], w_x1[:, 2 * e + k, m * 128:(m + 1) * 128], featT[:, j, k, :],
                                            start=(k == 0), stop=(k == 1))
                    last.then_inc(t_h1, 1)

                def mid(c, e):
                    pe.wait_ge(c_h1, at(c, NX, e + 1))
                    wait(pe, c_h2, at(c, NX, e - 1))
                    for m in range(2):
                        for k in range(2):
                            last = T.matmul(bank[2 + e % 2][:, m * CH:(m + 1) * CH], w_x2[:, 2 * e + k, m * 128:(m + 1) * 128], h1[:, e % 2, k, :],
                                            start=(k == 0), stop=(k == 1))
                    last.then_inc(t_h2, 1)

                def down(c, e):
                    pe.wait_ge(c_h2, at(c, NX, e + 1))
                    wait(pe, k_o, at(c, NX, e - 1))
                    for r in range(2):
                        for k in range(2):
                            last = T.matmul(bank[4 + e % 2][0:R, r * D:(r + 1) * D], h2[:, e % 2, k, r * R:(r + 1) * R], w_x3[:, 2 * e + k, :],
                                            start=(k == 0), stop=(k == 1))
                    last.then_inc(t_o, 1)

                def before():
                    tf((0, 2, 0))
                    router((0, 2, 0), 0)
                    logits((0, 2, 0))

                def body(c, j, more=True):
                    d = (c[0], 2, j + 1)
                    up(c, j, 0)
                    up(c, j, 1)
                    mid(c, 0)
                    up(c, j, 2)
                    mid(c, 1)
                    bias3(c, j)
                    down(c, 0)
                    bias3b(c)
                    up(c, j, 3)
                    mid(c, 2)
                    down(c, 1)
                    up(c, j, 4)
                    mid(c, 3)
                    down(c, 2)
                    up(c, j, 5)
                    mid(c, 4)
                    if more:
                        tf(d)
                    down(c, 3)
                    mid(c, 5)
                    if more:
                        router(d, 1 - j)
                    down(c, 4)
                    if more:
                        logits(d)
                    down(c, 5)
                chunks(pe, before, body, lambda c, j: body(c, j, False))


_INS = ['x', 'src', 'dst', 'L0_gnn_W_w', 'L0_gnn_W_b', 'L0_gnn_a_w', 'L0_gnn_a_b', 'L0_mix_Wq', 'L0_mix_bq', 'L0_mix_Wk',
        'L0_mix_bk', 'L0_mix_Wv', 'L0_mix_bv', 'L0_mix_Wo', 'L0_mix_bo', 'L0_mix_W1', 'L0_mix_b1', 'L0_mix_W2', 'L0_mix_b2',
        'L0_mix_ln1_g', 'L0_mix_ln1_b', 'L0_mix_ln2_g', 'L0_mix_ln2_b', 'L0_ffn_router_w1', 'L0_ffn_router_b1',
        'L0_ffn_router_w2', 'L0_ffn_router_b2', 'L0_ffn_expert_w1', 'L0_ffn_expert_b1', 'L0_ffn_expert_w2',
        'L0_ffn_expert_b2', 'L0_ffn_expert_w3', 'L0_ffn_expert_b3']
_OUTS = [((N, D), 'float32')]


def kernel(**inputs):
    import numpy as _np
    import concourse.bacc as _bacc
    from concourse import mybir as _mybir
    from concourse.bass_utils import run_bass_kernel_spmd as _run

    nc = _bacc.Bacc("TRN2", target_bir_lowering=False, num_devices=1)
    arrays, args = {}, []
    for name in _INS:
        a = _np.ascontiguousarray(inputs[name])
        arrays[f"in_{name}_dram"] = a
        args.append(nc.dram_tensor(f"in_{name}_dram", a.shape, _mybir.dt.from_np(a.dtype), kind="ExternalInput").ap())
    for i, (shape, dtype) in enumerate(_OUTS):
        dt = _mybir.dt.from_np(_np.dtype(dtype))
        args.append(nc.dram_tensor(f"out_{i}_dram", shape, dt, kind="ExternalOutput").ap())
    gps_kernel(nc, *args)
    r = _run(nc, [arrays], core_ids=[0])
    return r.results[0]["out_0_dram"]
```

```python
import concourse.bass as bass
from concourse import mybir
from contextlib import ExitStack

F32 = mybir.dt.float32
I32 = mybir.dt.int32
U32 = mybir.dt.uint32
ALU = mybir.AluOpType
ACT = mybir.ActivationFunctionType
AX = mybir.AxisListType

N, D, E = 6250, 256, 100000
R = 125
RW = R + 1
NT = N // R
CH = 2 * R
NC = N // CH
L = 128
COLS = -(-E // L)
GT = 4
GS = GT * L
NG = 250
assert NG >= (E - NT) // GS + NT and NG % 10 == 0 and NT * R == N and NC * 2 == NT
SLOTS = NG * GS
WROW = D + 2
FF, RH, NX = 1024, 128, 6
HD = 32
FAR = 2.0e6
NOROW = 200.0
FEW, SOME = 5, 10
STAGE = 17
PER = 10
RG = 10
LAG = 5
SC_IT = COLS // (2 * STAGE)
assert NT % SOME == 0 and NT % FEW == 0
assert SC_IT * 2 * STAGE == COLS


def at(step, k=1, off=0):
    it, per, j = step
    return it * (per * k) + (j * k + off)


def wait(eng, sem, value):
    if not isinstance(value, int) or value > 0:
        eng.wait_ge(sem, value)


def attention(before, body, eng):
    def static(it, h):
        if 2 * it + h < NC:
            body((it, 2, h), h, min(2, NC - 1 - 2 * it - h))
    before()
    for it in range(2):
        for h in range(2):
            static(it, h)
    with eng.Fori(2, NC // 2 - 1) as it:
        for h in range(2):
            body((it, 2, h), h, 2)
    for it in range(NC // 2 - 1, NC // 2 + 1):
        for h in range(2):
            static(it, h)


def together(eng, *parts):
    def step(it, h, slot, now=True):
        for part in parts:
            if callable(part):
                part(slot, (it, 2, h), h % 2, now)
                continue
            for lag, stage in part:
                k = PER * h + slot - lag
                if not isinstance(it, int) or 0 <= 2 * PER * it + k < NG:
                    stage((it, 2 * PER, k), k)

    for slot in range(2 * PER):
        step(0, slot // PER, slot % PER)
    with eng.Fori(1, NC // 2) as it:
        for slot in range(2 * PER):
            step(it, slot // PER, slot % PER)
    for slot in range(PER):
        step(NC // 2, 0, slot)
    for slot in range(LAG):
        step(NC // 2, 1, slot, False)


def gps_kernel(nc, x, src, dst, gW, gWb, ga, gab, Wq, bq, Wk, bk, Wv, bv, Wo, bo, W1, b1, W2, b2,
               l1g, l1b, l2g, l2b, rw1, rb1, rw2, rb2, ew1, eb1, ew2, eb2, ew3, eb3, out):
    table = nc.dram_tensor("wh_table", [N, WROW], F32, kind="Internal").ap()
    x1_rows = nc.dram_tensor("x1_rows", [NC * R, 2 * D], F32, kind="Internal").ap()
    slots = nc.dram_tensor("sorted_slots", [SLOTS, 2], I32, kind="Internal").ap()

    with ExitStack() as ctx:
        def sb(name, shape, dt=F32):
            return ctx.enter_context(nc.sbuf_tensor(name, shape, dt))

        def sem(name):
            return ctx.enter_context(nc.semaphore(name))

        bank = [ctx.enter_context(nc.psum_tensor(f"bank{i}", [128, 512], F32)) for i in range(8)]

        xn = sb("xn", [R, NT, D])
        iota_row = sb("iota_row", [L, RW])
        ident = sb("ident", [128, 128])
        ones = sb("ones", [128, 128])
        iota8 = sb("iota8", [128, 8])
        eps = sb("eps", [128, 1])
        small = sb("small", [128, 1])
        fd = sb("fd", [R, NT])
        fr = sb("fr", [R, NT])
        fr_c = sb("fr_c", [R, NT])
        shift = sb("shift", [128, 1])
        group_block = sb("group_block", [1, NG], I32)
        rstd_all = sb("rstd_all", [R, NT])
        acc_mem = sb("acc_mem", [128, NT * WROW])
        acc = acc_mem[0:R, :].rearrange("p (b w) -> p b w", w=WROW)
        srt_mem = acc_mem[:, 0:9 * COLS]
        srt = [srt_mem[:, i * COLS:(i + 1) * COLS] for i in range(9)]
        AREA = 26000
        area = sb("area", [128, AREA])

        def carve(start):
            place = [start]

            def take(*shape):
                n = 1
                for s in shape:
                    n *= s
                a = area[:, place[0]:place[0] + n]
                place[0] += n
                assert place[0] <= AREA, place[0]
                if len(shape) == 2:
                    a = a.rearrange("p (a b) -> p a b", a=shape[0])
                if len(shape) == 3:
                    a = a.rearrange("p (a b c) -> p a b c", a=shape[0], b=shape[1])
                return a
            take.place = place
            return take

        take = carve(0)
        w_1 = take(2, FF)
        w_2 = take(8, D)
        bias_2, g2, be2 = (take(D) for _ in range(3))
        bias_1 = take(8)
        y1 = take(2, 2, D)
        x1 = take(2, 2, D)
        x1T = take(2, CH)
        hT = take(8, CH)
        stats = take(2, 2, 6)
        mv = take(2, 2, 2)
        lv = take(2, 2)
        rs = take(2, 2)
        graph = take.place[0]
        w_q = take(2, D)
        w_o = take(2, D)
        bias_o, g1, be1 = (take(D) for _ in range(3))
        bias_q = take(2)
        kv_bd = take(2, 128)
        ks_bd = take(2, 128)
        xnT = take(2, 2, CH)
        qe, qr, phiq, att = (take(2, CH) for _ in range(4))
        xs = take(2, 2, D)
        w_gk = take(2, 512)
        w_v = take(2, D)
        bias_g, bias_k, bias_v = (take(D) for _ in range(3))
        a_dst, a_src = take(D), take(D)
        ab = take(1)
        kb = take(2, D)
        ke = take(2, D)
        kr = take(2, D)
        vaug = take(2, 2, R + 4)
        whs = take(2, WROW)
        diag_mask = take(128)
        tri = take(128)
        scratch, scratch2 = take(D), take(D)
        fdiag = take(128)
        held_vector = sem("held_vector")
        held_gpsimd = sem("held_gpsimd")

        def hold(eng):
            eng.sem_inc(held_gpsimd if eng is nc.gpsimd else held_vector, 1)

        def norm_in(dve, c, k, bias):
            mine = m_ln[k]
            dve.wait_ge(mine, at(c, 4, 1))
            nc.vector.tensor_tensor(y1[0:R, k, :, :], y1[0:R, k, :, :], bias[0:R, :].unsqueeze(1).to_broadcast([R, 2, D]), ALU.add).then_inc(mine, 1)
            dve.wait_ge(mine, at(c, 4, 2))
            for r in range(2):
                last_s = nc.vector.bn_stats(stats[0:R, k, r, :], y1[0:R, k, r, :])
            last_s.then_inc(mine, 1)
            dve.wait_ge(mine, at(c, 4, 3))
            hold(dve)
            for r in range(2):
                last_s = nc.vector.bn_aggr(mv[0:R, k, r, :], stats[0:R, k, r, :])
            last_s.then_inc(m_va[k], 1)

        def norm_out(dve, c, k, dst_of, gam, bet):
            mine = m_ln[k]
            dve.wait_ge(m_va[k], at(c, 1, 1))
            for r in range(2):
                last_s = nc.vector.scalar_tensor_tensor(y1[0:R, k, r, :], y1[0:R, k, r, :], mv[0:R, k, r, 0:1], gam[0:R, :],
                                                ALU.subtract, ALU.mult)
            last_s.then_inc(mine, 1)
            dve.wait_ge(mine, at(c, 4, 4))
            dve.wait_ge(m_rs[k], at(c, 1, 1))
            for r in range(2):
                last_s = nc.vector.scalar_tensor_tensor(dst_of[:, r, :], y1[0:R, k, r, :], rs[0:R, k, r:r + 1], bet[0:R, :],
                                                ALU.mult, ALU.add)
            return last_s

        def root(act, c, k):
            act.wait_ge(m_va[k], at(c, 1, 1))
            wait(act, m_x1 if k == 0 else m_y, at(c))
            nc.scalar.activation(lv[0:R, k, :], mv[0:R, k, :, 1], ACT.Ln, bias=eps[0:R, :]).then_inc(m_lv[k], 1)
            act.wait_ge(m_lv[k], at(c, 1, 1))
            nc.scalar.activation(rs[0:R, k, :], lv[0:R, k, :], ACT.Exp, scale=-0.5).then_inc(m_rs[k], 1)

        def rows(t):
            return xn[:, bass.ds(t, 1), :].rearrange("p a b -> p (a b)")

        hflat = hT.rearrange("p a b -> p (a b)")
        sts = hflat[0:R, 0:NT * 6].rearrange("p (t s) -> p t s", s=6)
        mvs = sb("mvs_mem", [R, 2 * NT])[:, :].rearrange("p (t s) -> p t s", s=2)

        iota_blk, tot, cnt, off, ngf, tmp50, gend = (take(NT) for _ in range(7))
        gcol, neg1 = take(1), take(1)
        few_blks, few_tots = take(FEW), take(FEW)
        fr_one = take(2)
        int50 = take(NT).bitcast(I32)
        iota_g, gcmp = take(NG)[0:NT, :], take(NG)[0:NT, :]
        stage_pos = take(2, STAGE).bitcast(I32)
        stage_pay = take(2, STAGE, 2).bitcast(I32)
        srcf, blk, q0, posf, cmp, cum, onesl = srt[0:7]
        ring = [acc_mem[:, i * COLS:(i + 1) * COLS] for i in range(9, 15)]
        dists, cums = ring[0:2], ring[2:4]
        masks = ring[4:6] + [cmp, cum, q0]
        pay = srt_mem[:, 7 * COLS:9 * COLS].bitcast(I32).rearrange("p (c k) -> p c k", k=2)
        srci = q0.bitcast(I32)
        dsti = cum.bitcast(I32)
        posi = blk.bitcast(I32)

        XB, QB, NUM, DEN, OUT = 0, 1, 3, 4, 5
        edges_in = sem("edges_in")
        prefilled = sem("prefilled")
        consts = sem("consts")
        const_step = sem("const_step")
        w_in = sem("w_in")
        x_in = sem("x_in")
        rank_step = sem("rank_step")
        mask_dist = sem("mask_dist")
        mask_ready = sem("mask_ready")
        scanned = sem("scanned")
        placed = sem("placed")
        count_step = sem("count_step")
        prefix_done = sem("prefix_done")
        gcmp_ready = sem("gcmp_ready")
        gmap_done = sem("gmap_done")
        pos_ready = sem("pos_ready")
        staged = sem("staged")
        scattered = [sem(f"scattered{i}") for i in range(2)]
        ln_step = sem("ln_step")
        var_ready = sem("var_ready")
        sd_ready = sem("sd_ready")
        xn_ready = sem("xn_ready")
        p_tp = sem("p_tp")
        p_tc = sem("p_tc")
        p_wk = sem("p_wk")
        p_kb = sem("p_kb")
        p_free = sem("p_free")
        p_ke = sem("p_ke")
        p_kv = sem("p_kv")
        p_kvd = sem("p_kvd")
        p_wh = sem("p_wh")
        p_row = sem("p_row")
        p_out = [sem(f"p_out{i}") for i in range(2)]
        kvb = sem("kvb")
        sh_diag = sem("sh_diag")
        sh_pe = sem("sh_pe")
        m_xt = sem("m_xt")
        m_xc = sem("m_xc")
        m_q = sem("m_q")
        m_qa = sem("m_qa")
        m_phi = sem("m_phi")
        m_nd = sem("m_nd")
        m_att = sem("m_att")
        m_den = sem("m_den")
        m_rec = sem("m_rec")
        m_o = sem("m_o")
        m_ln = [sem(f"m_ln{i}") for i in range(2)]
        m_va = [sem(f"m_va{i}") for i in range(2)]
        m_lv = [sem(f"m_lv{i}") for i in range(2)]
        m_rs = [sem(f"m_rs{i}") for i in range(2)]
        x1_out = [sem(f"x1_out{i}") for i in range(2)]
        m_x1 = sem("m_x1")
        m_t1 = sem("m_t1")
        m_tc1 = sem("m_tc1")
        m_h = sem("m_h")
        m_hc = sem("m_hc")
        m_ff = sem("m_ff")
        m_y = sem("m_y")
        m_x = sem("m_x")
        m_xs = sem("m_xs")

        halves = "(k p) n -> p k n"
        loads = [
            (w_gk[:, :, 0:D], gW.rearrange(halves, p=128)), (w_gk[:, :, D:2 * D], Wk.rearrange(halves, p=128)),
            (w_v, Wv.rearrange(halves, p=128)), (w_q, Wq.rearrange(halves, p=128)),
            (w_o, Wo.rearrange(halves, p=128)), (w_1, W1.rearrange(halves, p=128)),
            (w_2, W2.rearrange(halves, p=128)),
            (bias_g, gWb.partition_broadcast(128)), (bias_k, bk.partition_broadcast(128)),
            (bias_v, bv.partition_broadcast(128)), (bias_o, bo.partition_broadcast(128)),
            (bias_2, b2.partition_broadcast(128)), (g1, l1g.partition_broadcast(128)),
            (be1, l1b.partition_broadcast(128)), (g2, l2g.partition_broadcast(128)),
            (be2, l2b.partition_broadcast(128)), (a_dst, ga[0:D].partition_broadcast(128)),
            (a_src, ga[D:2 * D].partition_broadcast(128)), (ab, gab.partition_broadcast(128)),
            (bias_q, bq.rearrange("(m p) -> p m", p=128)), (bias_1, b1.rearrange("(m p) -> p m", p=128)),
        ]

        with nc.Block() as block:
            @block.sync
            def _(sp):
                last = E - (L - 1) * COLS
                for arr, to in ((src, srci), (dst, dsti)):
                    sp.dma_start(to[0:L - 1, :], arr[0:(L - 1) * COLS].rearrange("(p c) -> p c", c=COLS)).then_inc(edges_in, 16)
                    sp.dma_start(to[L - 1:L, 0:last], arr[(L - 1) * COLS:E].rearrange("(p c) -> p c", p=1)).then_inc(edges_in, 16)
                for i in range(NC):
                    sp.dma_start(xn[:, 2 * i:2 * i + 2, :],
                                 x[CH * i:CH * (i + 1), :].rearrange("(t p) d -> p t d", p=R)).then_inc(x_in, 16)
                with sp.Fori(0, NC) as it:
                    for j in range(2):
                        t = (it, 2, j)
                        sp.wait_ge(p_row, at(t, 1, 1))
                        sp.dma_start(table[bass.ds(at(t, R), R), :], whs[0:R, j, :]).then_inc(p_out[j], 16)
                for j in range(2):
                    sp.wait_ge(p_out[j], 16 * NC)

                def store(c, j):
                    sp.wait_ge(m_x1, at(c, 1, 1))
                    sp.dma_start(x1_rows[bass.ds(at(c, R), R), :], x1[0:R, j, :, :].rearrange("p t d -> p (t d)")).then_inc(x1_out[j], 16)
                attention(lambda: None, lambda c, j, left: store(c, j), sp)
                for j in range(2):
                    sp.wait_ge(x1_out[j], 16 * (NC // 2 + 1 - j))

            @block.gpsimd
            def _(g):
                empty = area[:, 0:2 * SLOTS // 128].rearrange("p (s k) -> p s k", k=2)
                g.memset(empty[:, :, 0:1].bitcast(I32), 0).then_inc(const_step, 1)
                g.memset(empty[:, :, 1:2], NOROW).then_inc(const_step, 1)
                g.wait_ge(const_step, 2)
                g.dma_start(slots.rearrange("(p s) k -> p (s k)", p=128), area[:, 0:2 * SLOTS // 128].bitcast(I32)).then_inc(prefilled, 16)
                g.iota(iota_row[:, :], pattern=[[1, RW]], base=0, channel_multiplier=0, allow_small_or_imprecise_dtypes=True)
                g.iota(iota_blk[:, :], pattern=[[1, NT]], base=0, channel_multiplier=0, allow_small_or_imprecise_dtypes=True)
                g.iota(iota_g[:, :], pattern=[[1, NG]], base=0, channel_multiplier=0, allow_small_or_imprecise_dtypes=True)
                g.iota(iota8[:, :], pattern=[[1, 8]], base=0, channel_multiplier=0, allow_small_or_imprecise_dtypes=True)
                g.memset(ones[:, :], 1.0).then_inc(const_step, 1)
                g.memset(ident[:, :], 0.0).then_inc(const_step, 1)
                g.wait_ge(const_step, 4)
                g.affine_select(out=ident[:, :], in_=ident[:, :], compare_op=ALU.not_equal, fill=1.0, base=0,
                                pattern=[[-1, 128]], channel_multiplier=1)
                g.wait_ge(prefilled, 16)
                g.affine_select(out=tri, in_=ones[:, :], compare_op=ALU.is_gt, fill=0.0, base=0,
                                pattern=[[1, 128]], channel_multiplier=-1)
                heads = diag_mask.rearrange("p (h e) -> p h e", h=4)
                g.affine_select(out=heads, in_=ones[:, :].rearrange("p (h e) -> p h e", h=4), compare_op=ALU.is_ge,
                                fill=0.0, base=0, pattern=[[-HD, 4], [0, HD]], channel_multiplier=1).then_inc(const_step, 1)
                g.wait_ge(const_step, 5)
                g.affine_select(out=heads, in_=heads, compare_op=ALU.is_ge, fill=0.0, base=HD - 1,
                                pattern=[[HD, 4], [0, HD]], channel_multiplier=-1)
                for s in range(2):
                    g.memset(vaug[:, s, :, 128:129], 1.0)
                    g.memset(whs[:, s, WROW - 1:WROW], 1.0)
                g.memset(small[:, :], 1e-6)
                g.memset(eps[:, :], 1e-5).then_inc(consts, 1)

                g.wait_ge(pos_ready, 1)

                def scatter(it, first):
                    for s in range(2):
                        if not first:
                            g.wait_ge(scattered[s], it * (16 * STAGE))
                            hold(g)
                        col = it * (2 * STAGE) + s * STAGE
                        g.tensor_copy(stage_pos[:, s, :], posi[:, bass.ds(col, STAGE)])
                        g.tensor_copy(stage_pay[:, s, :, :], pay[:, bass.ds(col, STAGE), :]).then_inc(staged, 1)
                        g.wait_ge(staged, it * 2 + s + 1)
                        hold(g)
                        for c in range(STAGE):
                            g.indirect_dma_start(out=slots, out_offset=bass.IndirectOffsetOnAxis(ap=stage_pos[:, s, c:c + 1], axis=0),
                                                 in_=stage_pay[:, s, c, :], in_offset=None,
                                                 bounds_check=SLOTS - 1, oob_is_err=False).then_inc(scattered[s], 16)
                scatter(0, True)
                with g.Fori(1, SC_IT) as it:
                    scatter(it, False)
                for s in range(2):
                    g.wait_ge(scattered[s], 16 * STAGE * SC_IT)

            @block.vector
            def _(dve):
                V = nc.vector
                n = [0]

                def step(ins):
                    n[0] += 1
                    ins.then_inc(rank_step, 1)
                    dve.wait_ge(rank_step, n[0])

                dve.wait_ge(edges_in, 64)
                dve.wait_ge(consts, 1)
                V.memset(srcf, float(N))
                step(V.memset(pay, 0))
                last = E - (L - 1) * COLS
                V.tensor_copy(srcf[0:96, :], srci[0:96, :])
                V.tensor_copy(pay[0:96, :, 0], dsti[0:96, :])
                V.tensor_copy(srcf[96:128, 0:last], srci[96:128, 0:last])
                V.tensor_copy(pay[96:128, 0:last, 0], dsti[96:128, 0:last])
                V.tensor_copy(srcf[96:127, last:COLS], srci[96:127, last:COLS])
                step(V.tensor_copy(pay[96:127, last:COLS, 0], dsti[96:127, last:COLS]))
                step(V.tensor_scalar(cum.bitcast(I32), srcf, 0.5, 1.0 / R, ALU.add, ALU.mult))
                step(V.tensor_copy(q0, cum.bitcast(I32)))
                step(V.scalar_tensor_tensor(cmp, q0, float(R), srcf, ALU.mult, ALU.is_gt))
                step(V.tensor_tensor(blk, q0, cmp, ALU.subtract))
                step(V.scalar_tensor_tensor(pay.bitcast(F32)[:, :, 1], blk, -float(R), srcf, ALU.mult, ALU.add))
                V.memset(onesl, 1.0)
                step(V.tensor_copy(few_blks, iota_blk[:, 0:FEW]))
                with dve.Fori(0, NT // FEW) as a:
                    for j, unread in enumerate((cmp, cum, posf, q0, srcf)):
                        last = V.tensor_scalar(unread, blk, few_blks[:, j:j + 1], None, ALU.is_equal, ALU.add, accum_out=few_tots[:, j:j + 1])
                    last.then_inc(count_step, 1)
                    dve.wait_ge(count_step, a * 3 + 1)
                    hold(dve)
                    V.tensor_copy(tot[:, bass.ds(a * FEW, FEW)], few_tots).then_inc(count_step, 1)
                    V.tensor_scalar(few_blks, few_blks, float(FEW), None, ALU.add).then_inc(count_step, 1)
                    dve.wait_ge(count_step, a * 3 + 3)
                V.memset(posf, FAR)
                dve.wait_ge(prefix_done, 1)
                step(V.tensor_scalar(cnt[:, :], bank[7][:, 0:NT], float(GS - 1), None, ALU.add))
                step(V.tensor_scalar(int50[:, :], cnt[:, :], 0.5, 1.0 / GS, ALU.add, ALU.mult))
                step(V.tensor_copy(ngf[:, :], int50[:, :]))
                step(V.scalar_tensor_tensor(tmp50[:, :], ngf[:, :], float(GS), cnt[:, :], ALU.mult, ALU.is_gt))
                step(V.tensor_tensor(ngf[:, :], ngf[:, :], tmp50[:, :], ALU.subtract))
                step(V.tensor_tensor_scan(gend[:, :], onesl[:, 0:NT], ngf[:, :], 0.0, ALU.mult, ALU.add))
                step(V.tensor_tensor(tmp50[:, :], gend[:, :], ngf[:, :], ALU.subtract))
                step(V.scalar_tensor_tensor(off[:, :], tmp50[:, :], float(GS), bank[6][:, 0:NT], ALU.mult, ALU.add))
                step(V.tensor_tensor(tmp50[:, :], gend[:, :], ident[:, 0:NT], ALU.mult))
                step(V.tensor_reduce(gcol[:, :], tmp50[:, :], AX.X, ALU.add))
                V.tensor_scalar(gcmp[:, :], iota_g[:, :], gcol[0:NT, :], None, ALU.is_ge).then_inc(gcmp_ready, 1)
                dve.wait_ge(gmap_done, 1)
                V.tensor_scalar(group_block[:, :], bank[5][0:1, 0:NG], float(NT - 1), None, ALU.min)
                def scan(b, j):
                    dve.wait_ge(mask_ready, at(b, 1, 1))
                    wait(dve, placed, at(b, 1, -1))
                    V.tensor_tensor_scan(cums[j % 2], onesl, masks[j % 5], off[:, bass.ds(at(b), 1)], ALU.mult, ALU.add).then_inc(scanned, 1)

                def place(b, j):
                    dve.wait_ge(scanned, at(b, 1, 1))
                    wait(dve, placed, at(b))
                    hold(dve)
                    V.copy_predicated(posf, masks[j % 5].bitcast(I32), cums[j % 2]).then_inc(placed, 1)

                def scan_place(it, count, ahead):
                    for j in range(count):
                        if j + 1 < count or ahead:
                            scan((it, SOME, j + 1), j + 1)
                        place((it, SOME, j), j)

                scan((0, SOME, 0), 0)
                scan_place(0, SOME, True)
                with dve.Fori(1, NT // SOME - 1) as it:
                    scan_place(it, SOME, True)
                scan_place(NT // SOME - 1, SOME, False)
                dve.wait_ge(placed, NT)
                V.tensor_scalar(posi, posf, -1.0, None, ALU.add).then_inc(pos_ready, 1)

                dve.wait_ge(x_in, 16 * NC)
                with dve.Fori(0, NT) as t:
                    V.bn_stats(sts[:, bass.ds(t, 1), :].rearrange("p a b -> p (a b)"),
                               xn[:, bass.ds(t, 1), :].rearrange("p a b -> p (a b)")).then_inc(ln_step, 1)
                dve.wait_ge(ln_step, NT)
                step(V.tensor_tensor(mvs[:, :, 0], sts[:, :, 1], sts[:, :, 4], ALU.add))
                V.tensor_tensor(mvs[:, :, 1], sts[:, :, 1], sts[:, :, 4], ALU.subtract)
                step(V.tensor_scalar(mvs[:, :, 0], mvs[:, :, 0], 0.5, None, ALU.mult))
                step(V.tensor_tensor(rstd_all[:, :], mvs[:, :, 1], mvs[:, :, 1], ALU.mult))
                step(V.tensor_scalar(rstd_all[:, :], rstd_all[:, :], D / 4.0, None, ALU.mult))
                step(V.tensor_tensor(rstd_all[:, :], rstd_all[:, :], sts[:, :, 2], ALU.add))
                step(V.tensor_tensor(rstd_all[:, :], rstd_all[:, :], sts[:, :, 5], ALU.add))
                V.tensor_scalar(mvs[:, :, 1], rstd_all[:, :], 1.0 / D, None, ALU.mult).then_inc(var_ready, 1)
                dve.wait_ge(sd_ready, 1)
                step(V.reciprocal(rstd_all[:, :], rstd_all[:, :]))
                dve.wait_ge(w_in, 16 * len(loads))

                def normalise(t, j):
                    wait(dve, p_tp, at(t, 1, -1))
                    V.tensor_scalar(xs[0:R, 0, j, :], rows(at(t)), mvs[:, bass.ds(at(t), 1), 0], rstd_all[:, bass.ds(at(t), 1)],
                                    ALU.subtract, ALU.mult).then_inc(xn_ready, 1)

                def proj(t, j):
                    prod, vb = bank[2 + j], bank[4 + j]
                    dve.wait_ge(p_wk, at(t, 1, 1))
                    wait(dve, p_kvd, at(t, 1, -1))
                    V.tensor_tensor(kb[0:R, j, :], prod[0:R, D:2 * D], bias_k[0:R, :], ALU.add).then_inc(p_kb, 1)
                    wait(dve, p_out[j], at((t[0], 1, 0), 16))
                    V.tensor_tensor(whs[0:R, j, 0:D], prod[0:R, 0:D], bias_g[0:R, :], ALU.add).then_inc(p_wh, 1)
                    V.tensor_tensor(vaug[0:R, j, :, 0:128], vb[0:R, 0:D].rearrange("p (h e) -> p h e", h=2),
                                    bias_v[0:R, :].rearrange("p (h e) -> p h e", h=2), ALU.add).then_inc(p_free, 1)
                    dve.wait_ge(p_wh, at(t, 2, 1))
                    V.tensor_tensor_reduce(scratch[0:R, :], whs[0:R, j, 0:D], a_src[0:R, :], 1.0, 0.0, ALU.mult, ALU.add,
                                           accum_out=fr_one[0:R, j:j + 1])
                    V.tensor_tensor_reduce(scratch2[0:R, :], whs[0:R, j, 0:D], a_dst[0:R, :], 1.0, 0.0, ALU.mult, ALU.add,
                                           accum_out=whs[0:R, j, D:D + 1]).then_inc(p_row, 1)
                    dve.wait_ge(p_row, at(t, 1, 1))
                    hold(dve)
                    V.tensor_copy(fd[:, bass.ds(at(t), 1)], whs[0:R, j, D:D + 1])
                    V.tensor_copy(fr[:, bass.ds(at(t), 1)], fr_one[0:R, j:j + 1]).then_inc(p_wh, 1)
                    dve.wait_ge(p_ke, at(t, 1, 1))
                    V.scalar_tensor_tensor(kb[0:R, j, :], ke[0:R, j, :], 1.0, kr[0:R, j, :], ALU.min, ALU.add).then_inc(p_kv, 1)

                for j in range(2):
                    normalise((0, 2, j), j)
                normalise((0, 2, 2), 0)
                proj((0, 2, 0), 0)
                normalise((0, 2, 3), 1)
                proj((0, 2, 1), 1)
                with dve.Fori(1, NC - 1) as it:
                    for j in range(2):
                        normalise((it, 2, j + 2), j)
                        proj((it, 2, j), j)
                for j in range(2):
                    proj((NC - 1, 2, j), j)

                dve.wait_ge(p_wh, 2 * NT)
                step(V.tensor_reduce(neg1[0:R, :], fd[:, :], AX.X, ALU.min))
                V.tensor_scalar(fdiag[0:R, 0:R], ident[0:R, 0:R], neg1[0:R, :], None, ALU.mult).then_inc(sh_diag, 1)
                dve.wait_ge(p_kvd, NT)
                for h in range(2):
                    V.tensor_tensor(kv_bd[:, h, :], bank[6 + h][:, 0:128], diag_mask, ALU.mult)
                    last_i = V.tensor_scalar(ks_bd[:, h, :], diag_mask, bank[6 + h][:, 128:129], None, ALU.mult)
                last_i.then_inc(kvb, 1)
                dve.wait_ge(sh_pe, 1)
                step(V.tensor_reduce(gcol[:, :], bank[2][:, 0:R], AX.X, ALU.min))
                step(V.tensor_scalar(shift[:, :], gcol[:, :], -1.0, 1.0, ALU.mult, ALU.add))
                step(V.tensor_scalar(fr[:, :], fr[:, :], ab[0:R, :], None, ALU.add))
                V.tensor_scalar(fr_c[:, :], fr[:, :], shift[0:R, :], None, ALU.subtract)

                def phi(c):
                    dve.wait_ge(m_qa, at(c, 1, 1))
                    V.scalar_tensor_tensor(phiq, qe, 1.0, qr, ALU.min, ALU.add).then_inc(m_phi, 1)

                def divide(c):
                    dve.wait_ge(m_nd, at(c, 1, 1))
                    dve.wait_ge(m_den, at(c, 1, 1))
                    V.reciprocal(att, att).then_inc(m_rec, 1)
                    dve.wait_ge(m_rec, at(c, 1, 1))
                    V.tensor_tensor(att, att, bank[NUM][:, 0:2 * CH].rearrange("p (m n) -> p m n", m=2), ALU.mult).then_inc(m_att, 1)

                def attend_sum(c, j):
                    dve.wait_ge(m_o, at(c, 1, 1))
                    wait(dve, m_x1, at(c))
                    V.tensor_tensor(y1[0:R, 0, :, :], bank[OUT][0:R, :].rearrange("p (t d) -> p t d", t=2),
                                    xs[0:R, j, :, :], ALU.add).then_inc(m_ln[0], 1)
                    norm_in(dve, c, 0, bias_o)

                def attend_norm(c, j):
                    wait(dve, x1_out[j], at(c, 8, -8 * j))
                    norm_out(dve, c, 0, x1[0:R, j, :, :], g1, be1).then_inc(m_x1, 1)

                def prepare(c, j):
                    for r in range(2):
                        t = at(c, 2, r)
                        last_p = V.tensor_scalar(xs[0:R, j, r, :], rows(t), mvs[:, bass.ds(t, 1), 0], rstd_all[:, bass.ds(t, 1)],
                                                 ALU.subtract, ALU.mult)
                    last_p.then_inc(m_xs, 1)

                def before():
                    prepare((0, 2, 0), 0)
                    prepare((0, 2, 1), 1)
                    phi((0, 2, 0))

                def body(c, j, left):
                    divide(c)
                    if left > 0:
                        phi((c[0], 2, j + 1))
                    if not isinstance(c[0], int) or at(c) > 0:
                        attend_norm((c[0], 2, j - 1), 1 - j)
                    attend_sum(c, j)
                    if left > 1:
                        prepare((c[0], 2, j + 2), j)
                attention(before, body, dve)
                attend_norm((NC // 2, 2, 0), 0)

            @block.scalar
            def _(act):
                A = nc.scalar
                act.wait_ge(prefilled, 16)
                for to, frm in loads:
                    act.dma_start(to, frm, allow_slow_non_contiguous=True).then_inc(w_in, 16)
                act.wait_ge(consts, 1)
                act.wait_ge(count_step, 3 * NT // FEW)

                def mask(it, h):
                    for j in range(2):
                        b = (it, SOME, h + j)
                        wait(act, mask_ready, at(b, 1, -1))
                        A.activation(dists[j % 2], blk, ACT.Abs, bias=iota_blk[:, bass.ds(at(b), 1)], scale=-1.0).then_inc(mask_dist, 1)
                    for j in range(2):
                        b = (it, SOME, h + j)
                        act.wait_ge(mask_dist, at(b, 1, 1))
                        wait(act, placed, at(b, 1, -4))
                        A.activation(masks[(h + j) % 5], dists[j % 2], ACT.Relu, bias=ones[:, 0:1], scale=-1.0).then_inc(mask_ready, 1)

                for h in range(0, SOME, 2):
                    mask(0, h)
                with act.Fori(1, NT // SOME) as it:
                    for h in range(0, SOME, 2):
                        mask(it, h)
                act.wait_ge(var_ready, 1)
                A.activation(rstd_all[:, :], mvs[:, :, 1], ACT.Sqrt, bias=eps[0:R, :]).then_inc(sd_ready, 1)
                A.preload_act_table_set("natural_log_exp_and_others")

                def proj(t, j):
                    act.wait_ge(p_tp, at(t, 1, 1))
                    wait(act, p_wk, at(t, 1, -1))
                    A.copy(xnT[:, j, :, 0:R], bank[j][:, 0:2 * R].rearrange("p (k n) -> p k n", k=2)).then_inc(p_tc, 1)

                def keys(t, j):
                    act.wait_ge(p_kb, at(t, 1, 1))
                    wait(act, p_kv, at(t, 1, -1))
                    A.activation(ke[0:R, j, :], kb[0:R, j, :], ACT.Exp)
                    A.activation(kr[0:R, j, :], kb[0:R, j, :], ACT.Relu).then_inc(p_ke, 1)

                proj((0, 2, 0), 0)
                proj((0, 2, 1), 1)
                keys((0, 2, 0), 0)
                with act.Fori(1, NC) as it:
                    proj((it, 2, 0), 0)
                    keys((it, 2, -1), 1)
                    proj((it, 2, 1), 1)
                    keys((it, 2, 0), 0)
                keys((NC, 2, -1), 1)

                def attend_in(c, j):
                    act.wait_ge(m_xt, at(c, 1, 1))
                    wait(act, m_q, at(c, 1, -1))
                    A.copy(xnT[:, j, :, :], bank[XB][:, 0:2 * CH].rearrange("p (k n) -> p k n", k=2)).then_inc(m_xc, 1)

                def attend_q(c, j):
                    act.wait_ge(m_q, at(c, 1, 1))
                    wait(act, m_phi, at(c))
                    for m in range(2):
                        A.activation(qe[:, m, :], bank[QB][:, m * CH:(m + 1) * CH], ACT.Exp, bias=bias_q[:, m:m + 1])
                    for m in range(2):
                        last = A.activation(qr[:, m, :], bank[QB][:, m * CH:(m + 1) * CH], ACT.Relu, bias=bias_q[:, m:m + 1])
                    last.then_inc(m_qa, 1)

                def denominators(c):
                    act.wait_ge(m_nd, at(c, 1, 1))
                    wait(act, m_o, at(c))
                    A.activation(att, bank[DEN][:, 0:2 * CH].rearrange("p (m n) -> p m n", m=2), ACT.Identity,
                                 bias=small[:, :]).then_inc(m_den, 1)

                def before():
                    attend_in((0, 2, 0), 0)
                    attend_q((0, 2, 0), 0)

                def body(c, j, left):
                    denominators(c)
                    if left > 0:
                        attend_in((c[0], 2, j + 1), 1 - j)
                        attend_q((c[0], 2, j + 1), 1 - j)
                    root(act, c, 0)
                attention(before, body, act)

            @block.tensor
            def _(pe):
                T = nc.tensor
                pe.wait_ge(consts, 1)
                pe.wait_ge(count_step, 3 * NT // FEW)
                T.matmul(bank[6][:, 0:NT], tri, tot[:, :], start=True, stop=True)
                T.matmul(bank[7][:, 0:NT], ones[:, :], tot[:, :], start=True, stop=True).then_inc(prefix_done, 1)
                pe.wait_ge(gcmp_ready, 1)
                T.matmul(bank[5][:, 0:NG], ones[0:NT, :], gcmp[:, :], start=True, stop=True).then_inc(gmap_done, 1)
                pe.wait_ge(pos_ready, 1)
                pe.wait_ge(w_in, 16 * len(loads))

                def transposes(t, j):
                    pe.wait_ge(xn_ready, at(t, 1, 1))
                    wait(pe, p_tc, at(t, 1, -1))
                    for k in range(2):
                        last = T.transpose(bank[j][:, k * R:(k + 1) * R],
                                           xs[0:R, 0, j, k * 128:(k + 1) * 128], ident[0:R, 0:R])
                    last.then_inc(p_tp, 1)

                def products(t, j):
                    pe.wait_ge(p_tc, at(t, 1, 1))
                    wait(pe, p_free, at(t, 1, -1))
                    for k in range(2):
                        T.matmul(bank[2 + j][0:R, :], xnT[:, j, k, 0:R], w_gk[:, k, :], start=(k == 0), stop=(k == 1))
                        last = T.matmul(bank[4 + j][0:R, 0:D], xnT[:, j, k, 0:R], w_v[:, k, :], start=(k == 0), stop=(k == 1))
                    last.then_inc(p_wk, 1)

                def kv(t, j, start, stop):
                    pe.wait_ge(p_kv, at(t, 1, 1))
                    for h in range(2):
                        last = T.matmul(bank[6 + h][:, 0:129], kb[0:R, j, h * 128:(h + 1) * 128], vaug[0:R, j, h, 0:129],
                                        start=start, stop=stop)
                    last.then_inc(p_kvd, 1)

                transposes((0, 2, 0), 0)
                transposes((0, 2, 1), 1)
                products((0, 2, 0), 0)
                products((0, 2, 1), 1)
                kv((0, 2, 0), 0, True, False)
                with pe.Fori(1, NC) as it:
                    transposes((it, 2, 0), 0)
                    kv((it, 2, -1), 1, False, False)
                    products((it, 2, 0), 0)
                    transposes((it, 2, 1), 1)
                    kv((it, 2, 0), 0, False, False)
                    products((it, 2, 1), 1)
                kv((NC, 2, -1), 1, False, True)
                pe.wait_ge(sh_diag, 1)
                pe.wait_ge(p_free, NT)
                T.matmul(bank[2][:, 0:R], ones[0:R, :], fdiag[0:R, 0:R], start=True, stop=True).then_inc(sh_pe, 1)

                def xt(c, j):
                    pe.wait_ge(m_xs, at(c, 1, 1))
                    wait(pe, m_xc, at(c))
                    for k in range(2):
                        for r in range(2):
                            last = T.transpose(bank[XB][:, k * CH + r * R:k * CH + (r + 1) * R],
                                               xs[0:R, j, r, k * 128:(k + 1) * 128],
                                               ident[0:R, 0:R])
                    last.then_inc(m_xt, 1)

                def q(c, j):
                    pe.wait_ge(m_xc, at(c, 1, 1))
                    wait(pe, m_qa, at(c))
                    for m in range(2):
                        for k in range(2):
                            last = T.matmul(bank[QB][:, m * CH:(m + 1) * CH], w_q[:, k, m * 128:(m + 1) * 128], xnT[:, j, k, :],
                                            start=(k == 0), stop=(k == 1))
                    last.then_inc(m_q, 1)

                def numden(c):
                    pe.wait_ge(m_phi, at(c, 1, 1))
                    wait(pe, m_att, at(c))
                    for m in range(2):
                        T.matmul(bank[NUM][:, m * CH:(m + 1) * CH], kv_bd[:, m, :], phiq[:, m, :], start=True, stop=True)
                        last = T.matmul(bank[DEN][:, m * CH:(m + 1) * CH], ks_bd[:, m, :], phiq[:, m, :], start=True, stop=True)
                    last.then_inc(m_nd, 1)

                def o(c):
                    pe.wait_ge(m_att, at(c, 1, 1))
                    wait(pe, m_ln[0], at(c, 4, -3))
                    for r in range(2):
                        for m in range(2):
                            last = T.matmul(bank[OUT][0:R, r * D:(r + 1) * D], att[:, m, r * R:(r + 1) * R], w_o[:, m, :],
                                            start=(m == 0), stop=(m == 1))
                    last.then_inc(m_o, 1)

                def before():
                    xt((0, 2, 0), 0)
                    q((0, 2, 0), 0)
                    pe.wait_ge(kvb, 1)

                def body(c, j, left):
                    numden(c)
                    if left > 0:
                        xt((c[0], 2, j + 1), 1 - j)
                        q((c[0], 2, j + 1), 1 - j)
                    o(c)
                attention(before, body, pe)

        take = carve(graph)
        gath = take(RG, GT, WROW)
        payr = take(RG, GT, 2)
        xm = take(2, GT, RW)
        hot = take(2, GS)
        dist = take(2, GT, RW)
        sm = take(2, GT, RW)
        fdc = take(2, GT)
        gmax, gt, gl = take(2), take(2), take(2)
        gd = take(2)
        alpha = take(5)
        frm = take(2, 2)
        mrun = take(NT)
        e1, e2, e3, e4 = (take(2, GT) for _ in range(4))
        payi = payr.bitcast(I32)
        XT, QE, US = (0, 3), 1, 2
        TB, AB, HB = 4, 5, (6, 7)

        acc_zero = sem("acc_zero")
        x1_in = [sem(f"x1_in{i}") for i in range(2)]
        pay_in = [sem(f"pay_in{i}") for i in range(RG // 2)]
        gathered = [sem(f"gathered{i}") for i in range(RG)]
        d_fdc = sem("d_fdc")
        d_x = sem("d_x")
        p_xt = sem("p_xt")
        a_hot = sem("a_hot")
        d_m = sem("d_m")
        d_frm = sem("d_frm")
        a_alpha = sem("a_alpha")
        p_q = sem("p_q")
        d_es = sem("d_es")
        d_e = sem("d_e")
        a_dist = sem("a_dist")
        a_s = sem("a_s")
        p_main = sem("p_main")
        d_acc = sem("d_acc")

        with nc.Block() as block:
            @block.sync
            def _(sp):
                def load(s, j):
                    if j % 2 == 0:
                        wait(sp, a_s, at(s, 1, 2 - RG))
                        sp.dma_start(payi[:, j % RG:j % RG + 2, :, :].rearrange("p g t k -> p g (t k)"),
                                     slots[bass.ds(at(s, GS), 2 * GS), :].rearrange("(g p t) k -> p g (t k)", g=2, t=GT)).then_inc(pay_in[j % RG // 2], 16)

                def load_x1(c, j):
                    wait(sp, m_ln[1], at(c, 4, -7))
                    sp.dma_start(x1[0:R, j, :, :].rearrange("p t d -> p (t d)"), x1_rows[bass.ds(at(c, R), R), :]).then_inc(x1_in[j], 16)

                def feed(slot, c, j, now):
                    following = now and not (isinstance(c[0], int) and at(c) + 1 >= NC)
                    if slot == 5 and following:
                        load_x1((c[0], 2, c[2] + 1), 1 - j)

                load_x1((0, 2, 0), 0)
                together(sp, [(0, load)], feed)

            @block.gpsimd
            def _(g):
                def gather(s, j):
                    if j % 2 == 0:
                        g.wait_ge(pay_in[j % RG // 2], at((s[0], 2 * PER // RG, j // RG), 16, 16))
                        wait(g, p_main, at(s, 1, 2 - RG))
                        hold(g)
                    for t in range(GT):
                        g.indirect_dma_start(out=gath[:, j % RG, t, :], out_offset=None, in_=table,
                                             in_offset=bass.IndirectOffsetOnAxis(ap=payi[:, j % RG, t, 0:1], axis=0),
                                             bounds_check=N - 1, oob_is_err=False).then_inc(gathered[j % RG], 16)
                together(g, [(0, gather)])

            @block.vector
            def _(dve):
                V = nc.vector
                V.memset(mrun[0:R, :], -1.0e30).then_inc(acc_zero, 1)
                V.memset(acc_mem[:, :], 0.0).then_inc(acc_zero, 1)
                dve.wait_ge(acc_zero, 2)

                blocks = [dve.alloc_register(f"block{i}") for i in range(4)]

                def block_of(j):
                    return dve.snap(blocks[j % 4], min_val=0, max_val=NT - 1)

                def shifted(s, j):
                    b = j % 2
                    dve.wait_ge(gathered[j % RG], at((s[0], 2 * PER // RG, j // RG), 16 * GT, 16 * GT))
                    wait(dve, p_xt, at(s, 1, -1))
                    V.tensor_scalar(fdc[:, b, :], gath[:, j % RG, :, D], shift[:, :], None, ALU.add).then_inc(d_fdc, 1)

                def mark(t):
                    def stage(s, j):
                        b = j % 2
                        dve.wait_ge(d_fdc, at(s, 1, 1))
                        ins = V.tensor_scalar(xm[:, b, t, :], iota_row[:, :], payr[:, j % RG, t, 1:2], fdc[:, b, t:t + 1],
                                              ALU.is_equal, ALU.mult)
                        if t == GT - 1:
                            ins.then_inc(d_x, 1)
                    return stage

                def group_peak(s, j):
                    b = j % 2
                    dve.wait_ge(p_xt, at(s, 1, 1))
                    V.tensor_reduce(gmax[0:R, b:b + 1], bank[XT[j % 2]][0:R, :], AX.X, ALU.max).then_inc(d_m, 1)
                    dve.reg_load(blocks[j % 4], group_block[0:1, bass.ds(at(s), 1)])
                    r = block_of(j)
                    wait(dve, p_q, at(s, 1, -1))
                    hold(dve)
                    V.tensor_copy(frm[0:R, b, 0:1], fr[:, bass.ds(r, 1)])

                def row_score(s, j):
                    b = j % 2
                    r = block_of(j)
                    dve.wait_ge(d_m, at(s, 5, 1))
                    V.tensor_tensor(gt[0:R, b:b + 1], gmax[0:R, b:b + 1], fr_c[:, bass.ds(r, 1)], ALU.add).then_inc(d_m, 1)

                def row_leaky(s, j):
                    b = j % 2
                    dve.wait_ge(d_m, at(s, 5, 2))
                    V.scalar_tensor_tensor(gl[0:R, b:b + 1], gt[0:R, b:b + 1], 0.2, gt[0:R, b:b + 1], ALU.mult, ALU.max).then_inc(d_m, 1)

                def new_max(s, j):
                    b = j % 2
                    r = block_of(j)
                    dve.wait_ge(d_m, at(s, 5, 3))
                    wait(dve, d_frm, at(s))
                    V.tensor_tensor(frm[0:R, b, 1:2], gl[0:R, b:b + 1], mrun[0:R, bass.ds(r, 1)], ALU.max).then_inc(d_m, 1)

                def old_less_new(s, j):
                    b = j % 2
                    r = block_of(j)
                    dve.wait_ge(d_m, at(s, 5, 4))
                    wait(dve, a_alpha, at(s, 1, -1))
                    V.tensor_tensor(gd[0:R, b:b + 1], mrun[0:R, bass.ds(r, 1)], frm[0:R, b, 1:2], ALU.subtract).then_inc(d_m, 1)

                def keep_max(s, j):
                    b = j % 2
                    r = block_of(j)
                    dve.wait_ge(d_m, at(s, 5, 5))
                    hold(dve)
                    V.tensor_copy(mrun[0:R, bass.ds(r, 1)], frm[0:R, b, 1:2]).then_inc(d_frm, 1)

                def score_sum(s, j):
                    b = j % 2
                    dve.wait_ge(p_q, at(s, 1, 1))
                    pair = bank[QE][:, 0:2 * GT].rearrange("p (t k) -> p t k", k=2)
                    V.tensor_tensor(e1[:, b, :], gath[:, j % RG, :, D], pair[:, :, 0], ALU.add).then_inc(d_es, 1)

                def score_leaky(s, j):
                    b = j % 2
                    dve.wait_ge(d_es, at(s, 3, 1))
                    V.scalar_tensor_tensor(e2[:, b, :], e1[:, b, :], 0.2, e1[:, b, :], ALU.mult, ALU.max).then_inc(d_es, 1)

                def score_less_max(s, j):
                    b = j % 2
                    pair = bank[QE][:, 0:2 * GT].rearrange("p (t k) -> p t k", k=2)
                    dve.wait_ge(d_es, at(s, 3, 2))
                    V.tensor_tensor(e3[:, b, :], e2[:, b, :], pair[:, :, 1], ALU.subtract).then_inc(d_es, 1)

                def score_bound(s, j):
                    b = j % 2
                    dve.wait_ge(d_es, at(s, 3, 3))
                    wait(dve, a_s, at(s, 1, -1))
                    V.tensor_scalar(e4[:, b, :], e3[:, b, :], 60.0, None, ALU.min).then_inc(d_e, 1)

                def gather_up(s, j):
                    b = j % 2
                    r = block_of(j)
                    dve.wait_ge(a_alpha, at(s, 1, 1))
                    dve.wait_ge(p_main, at(s, 1, 1))
                    wait(dve, d_acc, at(s))
                    row = acc[:, bass.ds(r, 1), :].rearrange("p a b -> p (a b)")
                    V.scalar_tensor_tensor(row, row, alpha[0:R, j % 5:j % 5 + 1], bank[US][0:R, 0:WROW], ALU.mult, ALU.add).then_inc(d_acc, 1)

                def feed_sum(c, j):
                    dve.wait_ge(m_ff, at(c, 1, 1))
                    wait(dve, m_x, at(c))
                    V.tensor_tensor(y1[0:R, 1, :, :], bank[AB][0:R, :].rearrange("p (t d) -> p t d", t=2), x1[0:R, j, :, :],
                                    ALU.add).then_inc(m_ln[1], 1)
                    norm_in(dve, c, 1, bias_2)

                def feed_norm(c, j):
                    norm_out(dve, c, 1, y1[0:R, 1, :, :], g2, be2).then_inc(m_y, 1)
                    dve.wait_ge(m_y, at(c, 1, 1))
                    both_rows = xn[:, bass.ds(at(c, 2), 2), :]
                    V.tensor_tensor(both_rows, both_rows, y1[0:R, 1, :, :], ALU.add).then_inc(m_x, 1)

                def feed(slot, c, j, now):
                    b = (c[0], 2, c[2] - 1)
                    if not isinstance(c[0], int) or at(c) > 0:
                        if slot == 0:
                            feed_sum(b, 1 - j)
                        if slot == 2:
                            feed_norm(b, 1 - j)

                together(dve, [(2, group_peak), (0, shifted), (4, score_sum), (2, row_score), (0, mark(0)), (4, score_leaky),
                               (2, row_leaky), (0, mark(1)), (4, score_less_max), (2, new_max), (0, mark(2)), (4, score_bound),
                               (2, old_less_new), (0, mark(3)), (2, keep_max), (5, gather_up)], feed)

            @block.scalar
            def _(act):
                A = nc.scalar
                A.preload_act_table_set("natural_log_exp_and_others")

                def spread(s, j):
                    b = j % 2
                    act.wait_ge(d_m, at(s, 5, 1))
                    wait(act, p_q, at(s, 1, -1))
                    A.activation(hot[0:R, b, :], bank[XT[j % 2]][0:R, :], ACT.Sign).then_inc(a_hot, 1)

                def rescale(s, j):
                    b = j % 2
                    act.wait_ge(d_m, at(s, 5, 5))
                    wait(act, d_acc, at(s, 1, -4))
                    A.activation(alpha[0:R, j % 5:j % 5 + 1], gd[0:R, b:b + 1], ACT.Exp).then_inc(a_alpha, 1)

                def apart(s, j):
                    b = j % 2
                    act.wait_ge(d_x, at(s, 1, 1))
                    wait(act, a_s, at(s, 1, -1))
                    for t in range(GT):
                        last = A.activation(dist[:, b, t, :], iota_row[:, :], ACT.Abs, bias=payr[:, j % RG, t, 1:2], scale=-1.0)
                    last.then_inc(a_dist, 1)

                def weigh(s, j):
                    b = j % 2
                    act.wait_ge(a_dist, at(s, 1, 1))
                    act.wait_ge(d_e, at(s, 1, 1))
                    wait(act, p_main, at(s, 1, -1))
                    for t in range(GT):
                        last = A.activation(sm[:, b, t, :], dist[:, b, t, :], ACT.Exp, bias=e4[:, b, t:t + 1], scale=-10000.0)
                    last.then_inc(a_s, 1)

                def feed_in(c, j):
                    act.wait_ge(m_t1, at(c, 1, 1))
                    wait(act, m_h, at(c, 4))
                    A.copy(x1T, bank[TB][:, 0:2 * CH].rearrange("p (k n) -> p k n", k=2)).then_inc(m_tc1, 1)

                def hidden(c, p):
                    act.wait_ge(m_h, at(c, 4, p + 1))
                    wait(act, m_ff, at(c))
                    for i in range(2):
                        f = 2 * p + i
                        last = A.activation(hT[:, f, :], bank[HB[p % 2]][:, i * CH:(i + 1) * CH], ACT.Relu, bias=bias_1[:, f:f + 1])
                    last.then_inc(m_hc, 1)

                def roots(slot, c, j, now):
                    if slot == 1 and (not isinstance(c[0], int) or at(c) > 0):
                        root(act, (c[0], 2, c[2] - 1), 1)

                def feed(slot, c, j, now):
                    if slot == 1 and now:
                        feed_in(c, j)
                    if slot in (3, 4, 5, 6) and now:
                        hidden(c, slot - 3)

                together(act, roots, [(2, spread), (3, apart), (3, rescale), (4, weigh)], feed)

            @block.tensor
            def _(pe):
                T = nc.tensor

                def turn(s, j):
                    b = j % 2
                    pe.wait_ge(d_x, at(s, 1, 1))
                    wait(pe, a_hot, at(s, 1, -1))
                    for t in range(GT):
                        last = T.transpose(bank[XT[j % 2]][0:RW, t * L:(t + 1) * L], xm[:, b, t, :], ident[:, :])
                    last.then_inc(p_xt, 1)

                def fetch(s, j):
                    b = j % 2
                    pe.wait_ge(a_hot, at(s, 1, 1))
                    pe.wait_ge(d_frm, at(s, 1, 1))
                    wait(pe, d_e, at(s))
                    for t in range(GT):
                        last = T.matmul(bank[QE][:, 2 * t:2 * t + 2], hot[0:R, b, t * L:(t + 1) * L], frm[0:R, b, :],
                                        start=True, stop=True)
                    last.then_inc(p_q, 1)

                def total(s, j):
                    b = j % 2
                    pe.wait_ge(a_s, at(s, 1, 1))
                    wait(pe, d_acc, at(s))
                    for t in range(GT):
                        last = T.matmul(bank[US][0:RW, 0:WROW], sm[:, b, t, :], gath[:, j % RG, t, :], start=(t == 0), stop=(t == GT - 1))
                    last.then_inc(p_main, 1)

                def t1(c, j):
                    pe.wait_ge(x1_in[j], at((c[0], 1, 0), 16, 16))
                    wait(pe, m_tc1, at(c))
                    for k in range(2):
                        for r in range(2):
                            last = T.transpose(bank[TB][:, k * CH + r * R:k * CH + (r + 1) * R],
                                               x1[0:R, j, r, k * 128:(k + 1) * 128], ident[0:R, 0:R])
                    last.then_inc(m_t1, 1)

                def hidden(c, p):
                    if p == 0:
                        pe.wait_ge(m_tc1, at(c, 1, 1))
                    wait(pe, m_hc, at(c, 4, p - 1))
                    for i in range(2):
                        for k in range(2):
                            f = 2 * p + i
                            last = T.matmul(bank[HB[p % 2]][:, i * CH:(i + 1) * CH], w_1[:, k, f * 128:(f + 1) * 128], x1T[:, k, :],
                                            start=(k == 0), stop=(k == 1))
                    last.then_inc(m_h, 1)

                def ff(c, r, half):
                    if r == 0 and half == 0:
                        pe.wait_ge(m_hc, at(c, 4, 2))
                        wait(pe, m_ln[1], at(c, 4, -3))
                    if half == 1:
                        pe.wait_ge(m_hc, at(c, 4, 4))
                    for f in range(4 * half, 4 * half + 4):
                        last = T.matmul(bank[AB][0:R, r * D:(r + 1) * D], hT[:, f, r * R:(r + 1) * R], w_2[:, f, :],
                                        start=(f == 0), stop=(f == 7))
                    if r == 1 and half == 1:
                        last.then_inc(m_ff, 1)

                def feed(slot, c, j, now):
                    if not now:
                        return
                    if slot == 0:
                        t1(c, j)
                    if slot in (2, 3, 4, 5):
                        hidden(c, slot - 2)
                    if slot >= 6:
                        ff(c, (slot - 6) // 2, slot % 2)

                together(pe, [(5, total), (3, fetch)], feed, [(0, turn)])

        take = carve(0)
        w_x1, w_x2, w_x3 = (take(2 * NX, D) for _ in range(3))
        w_r1 = take(2, RH)
        w_r2 = take(NX)
        b_x1, b_x2 = take(2 * NX), take(2 * NX)
        b_r1 = take(1)
        b_r2 = take(NX)
        b_x3 = take(D)
        rec = take(NT)
        den = take(NT)
        x2 = take(2, 2, D)
        feat = take(2, D)
        featT = take(2, 2, CH)
        rh = take(CH)
        lg, lm, pe_ = take(2, NX), take(2, NX), take(2, NX)
        prob = take(2, 8)
        top = take(2, 8)
        topi = take(2, 8).bitcast(U32)
        topf = take(2, 2)
        mx, sm2, dd, ee, dn, w_a, w_b = (take(2) for _ in range(7))
        ca, cb = take(2, NX), take(2, NX)
        cw = take(2, 2, NX)
        cT = take(CH)
        h1 = take(2, 2, CH)
        h2 = take(2, 2, CH)
        res = take(2, 2, D)
        st3, mv3 = take(2, 6), take(2, 2)
        lv3, rs3 = take(2), take(2)

        w3_in = sem("w3_in")
        wx_in = [sem(f"wx_in{i}") for i in range(3)]
        z3 = sem("z3")
        f_st = sem("f_st")
        f_va = sem("f_va")
        f_lv = sem("f_lv")
        f_rs = sem("f_rs")
        f_rdy = sem("f_rdy")
        t_ft = sem("t_ft")
        c_ft = sem("c_ft")
        t_r = sem("t_r")
        c_rh = sem("c_rh")
        t_lg = sem("t_lg")
        k_st = sem("k_st")
        k_lm = sem("k_lm")
        c_pe = sem("c_pe")
        k_dd = sem("k_dd")
        c_ee = sem("c_ee")
        k_cs = sem("k_cs")
        k_cw = sem("k_cw")
        t_ct = sem("t_ct")
        c_ct = sem("c_ct")
        t_b3 = sem("t_b3")
        k_base = sem("k_base")
        t_h1 = sem("t_h1")
        c_h1 = sem("c_h1")
        t_h2 = sem("t_h2")
        c_h2 = sem("c_h2")
        t_o = sem("t_o")
        k_o = sem("k_o")
        out_sem = [sem(f"out_sem{i}") for i in range(2)]
        loads3 = [
            (w_r1, rw1.rearrange("(k p) n -> p k n", p=128)), (w_r2, rw2), (b_r1, rb1.rearrange("(p a) -> p a", a=1)),
            (b_r2, rb2.partition_broadcast(128)), (b_x3[0:NX, :], eb3), (b_x1, eb1.rearrange("e (m p) -> p (e m)", p=128)),
            (b_x2, eb2.rearrange("e (m p) -> p (e m)", p=128)),
        ]

        def chunks(eng, before, body, drain):
            before()
            body((0, 2, 0), 0)
            body((0, 2, 1), 1)
            with eng.Fori(1, NC // 2) as it:
                body((it, 2, 0), 0)
                body((it, 2, 1), 1)
            drain((NC // 2, 2, 0), 0)

        with nc.Block() as block:
            @block.sync
            def _(sp):
                def store(c, j):
                    sp.wait_ge(k_o, at(c, NX, NX))
                    sp.dma_start(out[bass.ds(at(c, CH), CH), :].rearrange("(t p) d -> p t d", p=R), res[0:R, j, :, :]).then_inc(out_sem[j], 16)

                for i, (to, frm_) in enumerate(((w_x1, ew1), (w_x2, ew2), (w_x3, ew3))):
                    sp.dma_start(to, frm_.rearrange("e (k p) n -> p (e k) n", p=128)).then_inc(wx_in[i], 16)
                chunks(sp, lambda: None, store, store)
                sp.wait_ge(out_sem[0], 16 * (NC // 2 + 1))
                sp.wait_ge(out_sem[1], 16 * (NC // 2))

            @block.vector
            def _(dve):
                V = nc.vector
                V.tensor_scalar(den[0:R, :], acc[:, :, WROW - 1], 0.0, None, ALU.is_equal).then_inc(z3, 1)
                V.memset(prob, -1.0)
                dve.wait_ge(z3, 1)
                V.tensor_tensor(rec[0:R, :], den[0:R, :], acc[:, :, WROW - 1], ALU.add).then_inc(z3, 1)
                dve.wait_ge(z3, 2)
                V.reciprocal(rec[0:R, :], rec[0:R, :]).then_inc(z3, 1)
                dve.wait_ge(z3, 3)

                def features(c, j):
                    wait(dve, k_base, at(c, 1, -1))
                    for r in range(2):
                        last = V.tensor_scalar(x2[0:R, j, r, :], acc[:, bass.ds(at(c, 2, r), 1), 0:D].rearrange("p a b -> p (a b)"),
                                               rec[0:R, bass.ds(at(c, 2, r), 1)], 0.0, ALU.mult, ALU.max)
                    last.then_inc(f_st, 1)
                    dve.wait_ge(f_st, at(c, 3, 1))
                    V.tensor_tensor(x2[0:R, j, :, :], x2[0:R, j, :, :], xn[:, bass.ds(at(c, 2), 2), :], ALU.add).then_inc(f_st, 1)
                    dve.wait_ge(f_st, at(c, 3, 2))
                    for r in range(2):
                        last = V.bn_stats(st3[0:R, r, :], x2[0:R, j, r, :])
                    last.then_inc(f_st, 1)
                    dve.wait_ge(f_st, at(c, 3, 3))
                    hold(dve)
                    for r in range(2):
                        last = V.bn_aggr(mv3[0:R, r, :], st3[0:R, r, :])
                    last.then_inc(f_va, 1)
                    dve.wait_ge(f_rs, at(c, 1, 1))
                    wait(dve, t_ft, at(c))
                    for r in range(2):
                        last = V.tensor_scalar(feat[0:R, r, :], x2[0:R, j, r, :], mv3[0:R, r, 0:1], rs3[0:R, r:r + 1],
                                               ALU.subtract, ALU.mult)
                    last.then_inc(f_rdy, 1)

                def route(c, j):
                    k = [0]

                    def step(ins):
                        k[0] += 1
                        ins.then_inc(k_st, 1)
                        dve.wait_ge(k_st, at(c, 11, k[0]))
                        hold(dve)

                    dve.wait_ge(w3_in, 16 * len(loads3))
                    dve.wait_ge(t_lg, at(c, 1, 1))
                    step(V.tensor_tensor(lg[0:R, :, :], bank[7][0:R, 256:256 + 2 * NX].rearrange("p (t e) -> p t e", t=2),
                                         b_r2[0:R, :].unsqueeze(1).to_broadcast([R, 2, NX]), ALU.add))
                    step(V.tensor_reduce(mx[0:R, :], lg[0:R, :, :], AX.X, ALU.max))
                    V.tensor_tensor(lm[0:R, :, :], lg[0:R, :, :], mx[0:R, :].unsqueeze(2).to_broadcast([R, 2, NX]), ALU.subtract).then_inc(k_lm, 1)
                    dve.wait_ge(c_pe, at(c, 1, 1))
                    step(V.tensor_reduce(sm2[0:R, :], pe_[0:R, :, :], AX.X, ALU.add))
                    step(V.reciprocal(sm2[0:R, :], sm2[0:R, :]))
                    step(V.tensor_tensor(prob[0:R, :, 0:NX], pe_[0:R, :, :], sm2[0:R, :].unsqueeze(2).to_broadcast([R, 2, NX]), ALU.mult))
                    for r in range(2):
                        last = V.max(top[0:R, r, :], prob[0:R, r, :])
                    step(last)
                    for r in range(2):
                        last = V.max_index(topi[0:R, r, :], top[0:R, r, :], prob[0:R, r, :])
                    step(last)
                    V.tensor_tensor(dd[0:R, :], top[0:R, :, 1], top[0:R, :, 0], ALU.subtract).then_inc(k_dd, 1)
                    step(V.tensor_copy(topf[0:R, :, :], topi[0:R, :, 0:2]))
                    dve.wait_ge(c_ee, at(c, 1, 1))
                    step(V.tensor_scalar(dn[0:R, :], ee[0:R, :], 1.0, None, ALU.add))
                    step(V.reciprocal(w_a[0:R, :], dn[0:R, :]))
                    step(V.tensor_tensor(w_b[0:R, :], w_a[0:R, :], ee[0:R, :], ALU.mult))
                    assert k[0] == 11
                    for r in range(2):
                        V.tensor_scalar(ca[0:R, r, :], iota8[0:R, 0:NX], topf[0:R, r, 0:1], w_a[0:R, r:r + 1], ALU.is_equal, ALU.mult)
                        last = V.tensor_scalar(cb[0:R, r, :], iota8[0:R, 0:NX], topf[0:R, r, 1:2], w_b[0:R, r:r + 1], ALU.is_equal, ALU.mult)
                    last.then_inc(k_cs, 1)
                    dve.wait_ge(k_cs, at(c, 1, 1))
                    V.tensor_tensor(cw[0:R, j, :, :], ca[0:R, :, :], cb[0:R, :, :], ALU.add).then_inc(k_cw, 1)

                def base(c, j):
                    dve.wait_ge(t_b3, at(c, 1, 1))
                    wait(dve, out_sem[j], at((c[0], 1, 0), 16))
                    V.tensor_tensor(res[0:R, j, :, :], x2[0:R, j, :, :], bank[6][0:R, :].rearrange("p (t d) -> p t d", t=2), ALU.add).then_inc(k_base, 1)
                    dve.wait_ge(k_base, at(c, 1, 1))
                    dve.wait_ge(k_cw, at(c, 1, 1))

                def add(c, j, e):
                    dve.wait_ge(t_o, at(c, NX, e + 1))
                    wait(dve, k_o, at(c, NX, e))
                    for r in range(2):
                        last = V.scalar_tensor_tensor(res[0:R, j, r, :], bank[4 + e % 2][0:R, r * D:(r + 1) * D], cw[0:R, j, r, e:e + 1],
                                                      res[0:R, j, r, :], ALU.mult, ALU.add)
                    last.then_inc(k_o, 1)

                def before():
                    features((0, 2, 0), 0)
                    route((0, 2, 0), 0)

                def body(c, j, more=True):
                    base(c, j)
                    for e in range(2):
                        add(c, j, e)
                    if more:
                        features((c[0], 2, j + 1), 1 - j)
                    for e in range(2, NX):
                        add(c, j, e)
                    if more:
                        route((c[0], 2, j + 1), 1 - j)
                chunks(dve, before, body, lambda c, j: body(c, j, False))

            @block.scalar
            def _(act):
                A = nc.scalar
                A.preload_act_table_set("natural_log_exp_and_others")
                for to, frm_ in loads3:
                    act.dma_start(to, frm_, allow_slow_non_contiguous=True).then_inc(w3_in, 16)

                def relu2(src_bank, to, bias, e, done):
                    for m in range(2):
                        last = A.activation(to[:, m, :], src_bank[:, m * CH:(m + 1) * CH], ACT.Relu, bias=bias[:, 2 * e + m:2 * e + m + 1])
                    last.then_inc(done, 1)

                def up(c, e):
                    act.wait_ge(w3_in, 16 * len(loads3))
                    act.wait_ge(t_h1, at(c, NX, e + 1))
                    wait(act, t_h2, at(c, NX, e - 1))
                    relu2(bank[e % 2], h1[:, e % 2, :, :], b_x1, e, c_h1)

                def mid(c, e):
                    act.wait_ge(w3_in, 16 * len(loads3))
                    act.wait_ge(t_h2, at(c, NX, e + 1))
                    wait(act, t_o, at(c, NX, e - 1))
                    relu2(bank[2 + e % 2], h2[:, e % 2, :, :], b_x2, e, c_h2)

                def root(c):
                    act.wait_ge(f_va, at(c, 1, 1))
                    wait(act, f_rdy, at(c))
                    A.activation(lv3[0:R, :], mv3[0:R, :, 1], ACT.Ln, bias=eps[0:R, :]).then_inc(f_lv, 1)
                    act.wait_ge(f_lv, at(c, 1, 1))
                    A.activation(rs3[0:R, :], lv3[0:R, :], ACT.Exp, scale=-0.5).then_inc(f_rs, 1)

                def ft(c, j):
                    act.wait_ge(t_ft, at(c, 1, 1))
                    wait(act, t_h1, at(c, NX, -NX))
                    A.copy(featT[:, j, :, :], bank[6][:, 0:2 * CH].rearrange("p (k n) -> p k n", k=2)).then_inc(c_ft, 1)

                def rhid(c):
                    act.wait_ge(w3_in, 16 * len(loads3))
                    act.wait_ge(t_r, at(c, 1, 1))
                    wait(act, t_lg, at(c))
                    A.activation(rh, bank[7][:, 0:CH], ACT.Relu, bias=b_r1).then_inc(c_rh, 1)

                def router_exp(c):
                    act.wait_ge(k_lm, at(c, 1, 1))
                    A.activation(pe_[0:R, :, :], lm[0:R, :, :], ACT.Exp).then_inc(c_pe, 1)

                def second_exp(c):
                    act.wait_ge(k_dd, at(c, 1, 1))
                    A.activation(ee[0:R, :], dd[0:R, :], ACT.Exp).then_inc(c_ee, 1)

                def ct(c):
                    act.wait_ge(t_ct, at(c, 1, 1))
                    wait(act, t_b3, at(c))
                    A.copy(cT[0:NX, :], bank[7][0:NX, 0:CH]).then_inc(c_ct, 1)

                def before():
                    root((0, 2, 0))
                    ft((0, 2, 0), 0)
                    rhid((0, 2, 0))

                def body(c, j, more=True):
                    d = (c[0], 2, j + 1)
                    up(c, 0)
                    router_exp(c)
                    up(c, 1)
                    second_exp(c)
                    mid(c, 0)
                    up(c, 2)
                    mid(c, 1)
                    ct(c)
                    up(c, 3)
                    mid(c, 2)
                    up(c, 4)
                    mid(c, 3)
                    if more:
                        root(d)
                    up(c, 5)
                    mid(c, 4)
                    if more:
                        ft(d, 1 - j)
                    mid(c, 5)
                    if more:
                        rhid(d)
                chunks(act, before, body, lambda c, j: body(c, j, False))

            @block.tensor
            def _(pe):
                T = nc.tensor

                def tf(c):
                    pe.wait_ge(f_rdy, at(c, 1, 1))
                    wait(pe, k_base, at(c))
                    for k in range(2):
                        for r in range(2):
                            last = T.transpose(bank[6][:, k * CH + r * R:k * CH + (r + 1) * R], feat[0:R, r, k * 128:(k + 1) * 128], ident[0:R, 0:R])
                    last.then_inc(t_ft, 1)

                def router(c, j):
                    pe.wait_ge(w3_in, 16 * len(loads3))
                    pe.wait_ge(c_ft, at(c, 1, 1))
                    wait(pe, c_ct, at(c))
                    for k in range(2):
                        last = T.matmul(bank[7][:, 0:CH], w_r1[:, k, :], featT[:, j, k, :], start=(k == 0), stop=(k == 1))
                    last.then_inc(t_r, 1)

                def logits(c):
                    pe.wait_ge(c_rh, at(c, 1, 1))
                    for r in range(2):
                        last = T.matmul(bank[7][0:R, 256 + r * NX:256 + (r + 1) * NX], rh[:, r * R:(r + 1) * R], w_r2, start=True, stop=True)
                    last.then_inc(t_lg, 1)

                def bias3(c, j):
                    pe.wait_ge(k_cw, at(c, 1, 1))
                    for r in range(2):
                        last = T.transpose(bank[7][0:NX, r * R:(r + 1) * R], cw[0:R, j, r, :], ident[0:R, 0:R])
                    last.then_inc(t_ct, 1)

                def bias3b(c):
                    pe.wait_ge(c_ct, at(c, 1, 1))
                    for r in range(2):
                        last = T.matmul(bank[6][0:R, r * D:(r + 1) * D], cT[0:NX, r * R:(r + 1) * R], b_x3[0:NX, :], start=True, stop=True)
                    last.then_inc(t_b3, 1)

                def up(c, j, e):
                    pe.wait_ge(wx_in[0], 16)
                    wait(pe, c_h1, at(c, NX, e - 1))
                    for m in range(2):
                        for k in range(2):
                            last = T.matmul(bank[e % 2][:, m * CH:(m + 1) * CH], w_x1[:, 2 * e + k, m * 128:(m + 1) * 128], featT[:, j, k, :],
                                            start=(k == 0), stop=(k == 1))
                    last.then_inc(t_h1, 1)

                def mid(c, e):
                    pe.wait_ge(wx_in[1], 16)
                    pe.wait_ge(c_h1, at(c, NX, e + 1))
                    wait(pe, c_h2, at(c, NX, e - 1))
                    for m in range(2):
                        for k in range(2):
                            last = T.matmul(bank[2 + e % 2][:, m * CH:(m + 1) * CH], w_x2[:, 2 * e + k, m * 128:(m + 1) * 128], h1[:, e % 2, k, :],
                                            start=(k == 0), stop=(k == 1))
                    last.then_inc(t_h2, 1)

                def down(c, e):
                    pe.wait_ge(wx_in[2], 16)
                    pe.wait_ge(c_h2, at(c, NX, e + 1))
                    wait(pe, k_o, at(c, NX, e - 1))
                    for r in range(2):
                        for k in range(2):
                            last = T.matmul(bank[4 + e % 2][0:R, r * D:(r + 1) * D], h2[:, e % 2, k, r * R:(r + 1) * R], w_x3[:, 2 * e + k, :],
                                            start=(k == 0), stop=(k == 1))
                    last.then_inc(t_o, 1)

                def before():
                    tf((0, 2, 0))
                    router((0, 2, 0), 0)
                    logits((0, 2, 0))

                def body(c, j, more=True):
                    d = (c[0], 2, j + 1)
                    up(c, j, 0)
                    up(c, j, 1)
                    mid(c, 0)
                    up(c, j, 2)
                    mid(c, 1)
                    bias3(c, j)
                    down(c, 0)
                    bias3b(c)
                    up(c, j, 3)
                    mid(c, 2)
                    down(c, 1)
                    up(c, j, 4)
                    mid(c, 3)
                    down(c, 2)
                    up(c, j, 5)
                    mid(c, 4)
                    if more:
                        tf(d)
                    down(c, 3)
                    mid(c, 5)
                    if more:
                        router(d, 1 - j)
                    down(c, 4)
                    if more:
                        logits(d)
                    down(c, 5)
                chunks(pe, before, body, lambda c, j: body(c, j, False))


_INS = ['x', 'src', 'dst', 'L0_gnn_W_w', 'L0_gnn_W_b', 'L0_gnn_a_w', 'L0_gnn_a_b', 'L0_mix_Wq', 'L0_mix_bq', 'L0_mix_Wk',
        'L0_mix_bk', 'L0_mix_Wv', 'L0_mix_bv', 'L0_mix_Wo', 'L0_mix_bo', 'L0_mix_W1', 'L0_mix_b1', 'L0_mix_W2', 'L0_mix_b2',
        'L0_mix_ln1_g', 'L0_mix_ln1_b', 'L0_mix_ln2_g', 'L0_mix_ln2_b', 'L0_ffn_router_w1', 'L0_ffn_router_b1',
        'L0_ffn_router_w2', 'L0_ffn_router_b2', 'L0_ffn_expert_w1', 'L0_ffn_expert_b1', 'L0_ffn_expert_w2',
        'L0_ffn_expert_b2', 'L0_ffn_expert_w3', 'L0_ffn_expert_b3']
_OUTS = [((N, D), 'float32')]


def kernel(**inputs):
    import numpy as _np
    import concourse.bacc as _bacc
    from concourse import mybir as _mybir
    from concourse.bass_utils import run_bass_kernel_spmd as _run

    nc = _bacc.Bacc("TRN2", target_bir_lowering=False, num_devices=1)
    arrays, args = {}, []
    for name in _INS:
        a = _np.ascontiguousarray(inputs[name])
        arrays[f"in_{name}_dram"] = a
        args.append(nc.dram_tensor(f"in_{name}_dram", a.shape, _mybir.dt.from_np(a.dtype), kind="ExternalInput").ap())
    for i, (shape, dtype) in enumerate(_OUTS):
        dt = _mybir.dt.from_np(_np.dtype(dtype))
        args.append(nc.dram_tensor(f"out_{i}_dram", shape, dt, kind="ExternalOutput").ap())
    gps_kernel(nc, *args)
    r = _run(nc, [arrays], core_ids=[0])
    return r.results[0]["out_0_dram"]
```
